# Optimizing a Trainium2 kernel written in Bass

```python
import numpy as np
import jax
import jax.numpy as jnp

def _softmax(x, axis=-1):
    return jax.nn.softmax(x, axis=axis)

def _gelu(x):
    return jax.nn.gelu(x, approximate=True)

def _silu(x):
    return jax.nn.silu(x)

def _sigmoid(x):
    return jax.nn.sigmoid(x)

def _layernorm(x, axis=-1, eps=1e-05):
    m = jnp.mean(x, axis=axis, keepdims=True)
    v = jnp.var(x, axis=axis, keepdims=True)
    return (x - m) / jnp.sqrt(v + eps)

def _scatter_add(tgt, idx, src, axis=0):
    return tgt.at[idx].add(src)

def _segment_sum(src, seg, n):
    return jax.ops.segment_sum(src, seg, n)
kernel_name = 'mk_recurrent_d2_jaxref_r4_354726'

def setup_inputs(seed: int=0):
    np.random.seed(seed)
    _w = jnp.asarray

    def _L0_attn_setup():
        import jax, jax.numpy as jnp
        import numpy as np
        NUM_HEADS = 32
        NUM_KV_HEADS = 8
        IN_FEATURES = 512
        OUT_FEATURES = 512
        HEAD_DIM = IN_FEATURES // NUM_HEADS
        BATCH, SEQ = (2, 512)
        key = jax.random.key(seed)
        ks = jax.random.split(key, 5)
        s = 0.02
        return {'x': jax.random.normal(ks[0], (BATCH, SEQ, IN_FEATURES), dtype=jnp.float16), 'Wq': (jax.random.normal(ks[1], (IN_FEATURES, NUM_HEADS * HEAD_DIM)) * s).astype(jnp.float16), 'Wk': (jax.random.normal(ks[2], (IN_FEATURES, NUM_KV_HEADS * HEAD_DIM)) * s).astype(jnp.float16), 'Wv': (jax.random.normal(ks[3], (IN_FEATURES, NUM_KV_HEADS * HEAD_DIM)) * s).astype(jnp.float16), 'Wo': (jax.random.normal(ks[4], (NUM_HEADS * HEAD_DIM, OUT_FEATURES)) * s).astype(jnp.float16)}
    _L0_attn_in = _L0_attn_setup()

    def _L0_ffn_setup():
        import jax, jax.numpy as jnp
        import numpy as np
        HIDDEN = 512
        INTER = 2048
        SCALE = 64.0

        def fwht(x):
            orig_shape = x.shape
            n = orig_shape[-1]
            x = x.reshape(-1, n)
            h = 1
            while h < n:
                x = x.reshape(-1, n // (2 * h), 2, h)
                a, b = (x[:, :, 0, :], x[:, :, 1, :])
                x = jnp.stack([a + b, a - b], axis=2).reshape(-1, n)
                h *= 2
            return (x / jnp.sqrt(jnp.asarray(n, x.dtype))).reshape(orig_shape)
        key = jax.random.key(seed)
        ks = jax.random.split(key, 8)
        inp = jax.random.normal(ks[0], (4, 512, HIDDEN), dtype=jnp.float32)
        SU_ug = jnp.where(jax.random.bernoulli(ks[1], 0.5, (HIDDEN,)), 1.0, -1.0).astype(jnp.float32)
        SU_dp = jnp.where(jax.random.bernoulli(ks[2], 0.5, (INTER,)), 1.0, -1.0).astype(jnp.float32)
        Wscale_ug = jax.random.uniform(ks[3], (2 * INTER,), jnp.float32, 0.5, 1.5)
        Wscale_dp = jax.random.uniform(ks[4], (HIDDEN,), jnp.float32, 0.5, 1.5)
        W_up = jax.random.normal(ks[5], (INTER, HIDDEN), dtype=jnp.float32) * 0.02
        W_gate = jax.random.normal(ks[6], (INTER, HIDDEN), dtype=jnp.float32) * 0.02
        W_down = jax.random.normal(ks[7], (HIDDEN, INTER), dtype=jnp.float32) * 0.02
        return {'input': inp, 'SU_ug': SU_ug, 'SU_dp': SU_dp, 'Wscale_ug': Wscale_ug, 'Wscale_dp': Wscale_dp, 'W_up': W_up, 'W_gate': W_gate, 'W_down': W_down}
    _L0_ffn_in = _L0_ffn_setup()

    def _L1_attn_setup():
        import jax, jax.numpy as jnp
        import numpy as np
        HIDDEN = 512
        NUM_HEADS = 6
        HEAD_DIM = 64
        KEY_DIM = NUM_HEADS * HEAD_DIM
        VALUE_DIM = KEY_DIM
        CONV_K = 4
        EPS = 1e-05

        def _causal_depthwise_conv(x, w):
            B, T, C = x.shape
            K = w.shape[1]
            xp = jnp.pad(x, ((0, 0), (K - 1, 0), (0, 0)))
            y = jnp.zeros_like(x)
            for i in range(K):
                y = y + xp[:, i:i + T, :] * w[:, i]
            return jax.nn.silu(y)

        def _l2norm(x, eps=1e-06):
            return x * jax.lax.rsqrt(jnp.sum(x * x, axis=-1, keepdims=True) + eps)
        key = jax.random.key(seed)
        ks = jax.random.split(key, 16)
        s = lambda fan: 1.0 / np.sqrt(fan)
        inp = {'hidden_states': jax.random.normal(ks[0], (2, 512, HIDDEN), jnp.float32), 'Wq': jax.random.normal(ks[1], (KEY_DIM, HIDDEN), jnp.float32) * s(HIDDEN), 'Wk': jax.random.normal(ks[2], (KEY_DIM, HIDDEN), jnp.float32) * s(HIDDEN), 'Wv': jax.random.normal(ks[3], (VALUE_DIM, HIDDEN), jnp.float32) * s(HIDDEN), 'Wo': jax.random.normal(ks[4], (HIDDEN, VALUE_DIM), jnp.float32) * s(VALUE_DIM), 'Wb': jax.random.normal(ks[5], (NUM_HEADS, HIDDEN), jnp.float32) * s(HIDDEN), 'Wa': jax.random.normal(ks[6], (NUM_HEADS, HIDDEN), jnp.float32) * s(HIDDEN), 'Wg': jax.random.normal(ks[7], (VALUE_DIM, HIDDEN), jnp.float32) * s(HIDDEN), 'conv_q': jax.random.normal(ks[8], (KEY_DIM, CONV_K), jnp.float32) * s(CONV_K), 'conv_k': jax.random.normal(ks[9], (KEY_DIM, CONV_K), jnp.float32) * s(CONV_K), 'conv_v': jax.random.normal(ks[10], (VALUE_DIM, CONV_K), jnp.float32) * s(CONV_K), 'o_norm_w': jnp.ones((HEAD_DIM,), jnp.float32)}
        A = jax.random.uniform(ks[11], (NUM_HEADS,), jnp.float32, 0.0001, 16.0)
        inp['A_log'] = jnp.log(A)
        dt = jnp.exp(jax.random.uniform(ks[12], (NUM_HEADS,), jnp.float32) * (np.log(0.1) - np.log(0.001)) + np.log(0.001))
        dt = jnp.clip(dt, 0.0001, None)
        inp['dt_bias'] = dt + jnp.log(-jnp.expm1(-dt))
        return inp
    _L1_attn_in = _L1_attn_setup()

    def _L1_ffn_setup():
        import jax, jax.numpy as jnp
        import numpy as np

        @jax.custom_vjp
        def ste_sign(x):
            return jnp.sign(x)

        def _ste_fwd(x):
            return (jnp.sign(x), None)

        def _ste_bwd(_, g):
            return (g,)
        ste_sign.defvjp(_ste_fwd, _ste_bwd)
        D_MODEL = 512
        D_HIDDEN = 2048
        key = jax.random.key(seed)
        k_x, k_up, k_dn = jax.random.split(key, 3)
        x = jax.random.normal(k_x, (2, 512, D_MODEL), dtype=jnp.float32)
        up_weight = jax.random.normal(k_up, (D_HIDDEN, D_MODEL), dtype=jnp.float32) * 0.02
        down_weight = jax.random.normal(k_dn, (D_MODEL, D_HIDDEN), dtype=jnp.float32) * 0.02
        up_scale = jnp.ones((D_HIDDEN,), dtype=jnp.float32)
        down_scale = jnp.ones((D_MODEL,), dtype=jnp.float32)
        output_scale = jnp.ones((1,), dtype=jnp.float32)
        return {'x': x, 'up_weight': up_weight, 'down_weight': down_weight, 'up_scale': up_scale, 'down_scale': down_scale, 'output_scale': output_scale}
    _L1_ffn_in = _L1_ffn_setup()
    _d = {'L0_attn_x': _L0_attn_in['x'], 'L0_attn_Wq': _L0_attn_in['Wq'], 'L0_attn_Wk': _L0_attn_in['Wk'], 'L0_attn_Wv': _L0_attn_in['Wv'], 'L0_attn_Wo': _L0_attn_in['Wo'], 'L0_ffn_SU_ug': _L0_ffn_in['SU_ug'], 'L0_ffn_SU_dp': _L0_ffn_in['SU_dp'], 'L0_ffn_Wscale_ug': _L0_ffn_in['Wscale_ug'], 'L0_ffn_Wscale_dp': _L0_ffn_in['Wscale_dp'], 'L0_ffn_W_up': _L0_ffn_in['W_up'], 'L0_ffn_W_gate': _L0_ffn_in['W_gate'], 'L0_ffn_W_down': _L0_ffn_in['W_down'], 'L1_attn_Wq': _L1_attn_in['Wq'], 'L1_attn_Wk': _L1_attn_in['Wk'], 'L1_attn_Wv': _L1_attn_in['Wv'], 'L1_attn_Wo': _L1_attn_in['Wo'], 'L1_attn_Wb': _L1_attn_in['Wb'], 'L1_attn_Wa': _L1_attn_in['Wa'], 'L1_attn_Wg': _L1_attn_in['Wg'], 'L1_attn_conv_q': _L1_attn_in['conv_q'], 'L1_attn_conv_k': _L1_attn_in['conv_k'], 'L1_attn_conv_v': _L1_attn_in['conv_v'], 'L1_attn_o_norm_w': _L1_attn_in['o_norm_w'], 'L1_attn_A_log': _L1_attn_in['A_log'], 'L1_attn_dt_bias': _L1_attn_in['dt_bias'], 'L1_ffn_up_weight': _L1_ffn_in['up_weight'], 'L1_ffn_down_weight': _L1_ffn_in['down_weight'], 'L1_ffn_up_scale': _L1_ffn_in['up_scale'], 'L1_ffn_down_scale': _L1_ffn_in['down_scale'], 'L1_ffn_output_scale': _L1_ffn_in['output_scale']}
    _x0 = _d['L0_attn_x']
    _d['L0_attn_x'] = jax.random.normal(jax.random.fold_in(jax.random.key(seed), 1), (4, 512, 512), dtype=_x0.dtype)
    del _x0
    return _d

def reference(L0_attn_x, L0_attn_Wq, L0_attn_Wk, L0_attn_Wv, L0_attn_Wo, L0_ffn_SU_ug, L0_ffn_SU_dp, L0_ffn_Wscale_ug, L0_ffn_Wscale_dp, L0_ffn_W_up, L0_ffn_W_gate, L0_ffn_W_down, L1_attn_Wq, L1_attn_Wk, L1_attn_Wv, L1_attn_Wo, L1_attn_Wb, L1_attn_Wa, L1_attn_Wg, L1_attn_conv_q, L1_attn_conv_k, L1_attn_conv_v, L1_attn_o_norm_w, L1_attn_A_log, L1_attn_dt_bias, L1_ffn_up_weight, L1_ffn_down_weight, L1_ffn_up_scale, L1_ffn_down_scale, L1_ffn_output_scale):

    def _L0_attn_ref(x, Wq, Wk, Wv, Wo):
        import jax, jax.numpy as jnp
        import numpy as np
        NUM_HEADS = 32
        NUM_KV_HEADS = 8
        IN_FEATURES = 512
        OUT_FEATURES = 512
        HEAD_DIM = IN_FEATURES // NUM_HEADS
        BATCH, SEQ = (2, 512)
        b, s, _ = x.shape
        groups = NUM_HEADS // NUM_KV_HEADS
        q = (x @ Wq).reshape(b, s, NUM_HEADS, HEAD_DIM).transpose(0, 2, 1, 3)
        k = (x @ Wk).reshape(b, s, NUM_KV_HEADS, HEAD_DIM).transpose(0, 2, 1, 3)
        v = (x @ Wv).reshape(b, s, NUM_KV_HEADS, HEAD_DIM).transpose(0, 2, 1, 3)
        k = jnp.repeat(k, groups, axis=1)
        v = jnp.repeat(v, groups, axis=1)
        scale = jnp.float16(1.0 / np.sqrt(HEAD_DIM))
        attn = jnp.einsum('bhqd,bhkd->bhqk', q, k) * scale
        attn = jax.nn.softmax(attn, axis=-1).astype(jnp.float16)
        out = jnp.einsum('bhqk,bhkd->bhqd', attn, v)
        out = out.transpose(0, 2, 1, 3).reshape(b, s, NUM_HEADS * HEAD_DIM)
        return out @ Wo

    def _L0_ffn_ref(input, SU_ug, SU_dp, Wscale_ug, Wscale_dp, W_up, W_gate, W_down):
        import jax, jax.numpy as jnp
        import numpy as np
        HIDDEN = 512
        INTER = 2048
        SCALE = 64.0

        def fwht(x):
            orig_shape = x.shape
            n = orig_shape[-1]
            x = x.reshape(-1, n)
            h = 1
            while h < n:
                x = x.reshape(-1, n // (2 * h), 2, h)
                a, b = (x[:, :, 0, :], x[:, :, 1, :])
                x = jnp.stack([a + b, a - b], axis=2).reshape(-1, n)
                h *= 2
            return (x / jnp.sqrt(jnp.asarray(n, x.dtype))).reshape(orig_shape)
        n = SU_ug.shape[0]
        x = input.reshape(-1, n)
        x = fwht(x * SU_ug) / SCALE
        x_up = x @ W_up.T * (Wscale_ug[:INTER] * SCALE)
        x_gate = x @ W_gate.T * (Wscale_ug[INTER:] * SCALE)
        x = jax.nn.silu(x_gate) * x_up
        x = fwht(x * SU_dp) / SCALE
        x = x @ W_down.T * (Wscale_dp * SCALE)
        return x.reshape(input.shape)

    def _L1_attn_ref(hidden_states, Wq, Wk, Wv, Wo, Wb, Wa, Wg, conv_q, conv_k, conv_v, o_norm_w, A_log, dt_bias):
        import jax, jax.numpy as jnp
        import numpy as np
        HIDDEN = 512
        NUM_HEADS = 6
        HEAD_DIM = 64
        KEY_DIM = NUM_HEADS * HEAD_DIM
        VALUE_DIM = KEY_DIM
        CONV_K = 4
        EPS = 1e-05

        def _causal_depthwise_conv(x, w):
            B, T, C = x.shape
            K = w.shape[1]
            xp = jnp.pad(x, ((0, 0), (K - 1, 0), (0, 0)))
            y = jnp.zeros_like(x)
            for i in range(K):
                y = y + xp[:, i:i + T, :] * w[:, i]
            return jax.nn.silu(y)

        def _l2norm(x, eps=1e-06):
            return x * jax.lax.rsqrt(jnp.sum(x * x, axis=-1, keepdims=True) + eps)
        x = hidden_states
        B, T, D = x.shape
        H, dk, dv = (NUM_HEADS, HEAD_DIM, HEAD_DIM)
        q = _causal_depthwise_conv(jnp.einsum('btd,kd->btk', x, Wq), conv_q)
        k = _causal_depthwise_conv(jnp.einsum('btd,kd->btk', x, Wk), conv_k)
        v = _causal_depthwise_conv(jnp.einsum('btd,kd->btk', x, Wv), conv_v)
        q = _l2norm(q.reshape(B, T, H, dk))
        k = _l2norm(k.reshape(B, T, H, dk))
        v = v.reshape(B, T, H, dv)
        beta = jax.nn.sigmoid(jnp.einsum('btd,hd->bth', x, Wb))
        g = -jnp.exp(A_log) * jax.nn.softplus(jnp.einsum('btd,hd->bth', x, Wa) + dt_bias)
        scale = dk ** (-0.5)

        def step(S, inputs):
            q_t, k_t, v_t, g_t, b_t = inputs
            S = S * jnp.exp(g_t)[..., None, None]
            kv = jnp.einsum('bhk,bhkv->bhv', k_t, S)
            u = b_t[..., None] * (v_t - kv)
            S = S + jnp.einsum('bhk,bhv->bhkv', k_t, u)
            o_t = jnp.einsum('bhk,bhkv->bhv', q_t * scale, S)
            return (S, o_t)
        tfirst = lambda a: jnp.moveaxis(a, 1, 0)
        S0 = jnp.zeros((B, H, dk, dv), x.dtype)
        _, o = jax.lax.scan(step, S0, (tfirst(q), tfirst(k), tfirst(v), tfirst(g), tfirst(beta)))
        o = jnp.moveaxis(o, 0, 1)
        gate = jnp.einsum('btd,vd->btv', x, Wg).reshape(B, T, H, dv)
        o = o * jax.lax.rsqrt(jnp.mean(o * o, axis=-1, keepdims=True) + EPS)
        o = o * o_norm_w * jax.nn.silu(gate)
        out = jnp.einsum('btv,dv->btd', o.reshape(B, T, H * dv), Wo)
        return out

    def _L1_ffn_ref(x, up_weight, down_weight, up_scale, down_scale, output_scale):
        import jax, jax.numpy as jnp
        import numpy as np

        @jax.custom_vjp
        def ste_sign(x):
            return jnp.sign(x)

        def _ste_fwd(x):
            return (jnp.sign(x), None)

        def _ste_bwd(_, g):
            return (g,)
        ste_sign.defvjp(_ste_fwd, _ste_bwd)
        D_MODEL = 512
        D_HIDDEN = 2048
        up_w = ste_sign(up_weight)
        down_w = ste_sign(down_weight)
        hidden = jnp.einsum('bsd,hd->bsh', x, up_w) * up_scale
        hidden = jax.nn.relu(hidden)
        out = jnp.einsum('bsh,dh->bsd', hidden, down_w) * down_scale
        return out * output_scale
    x = L0_attn_x
    xn = _layernorm(x, axis=-1)
    s = _L0_attn_ref(xn, L0_attn_Wq, L0_attn_Wk, L0_attn_Wv, L0_attn_Wo)
    g = _silu(_L0_ffn_ref(xn, L0_ffn_SU_ug, L0_ffn_SU_dp, L0_ffn_Wscale_ug, L0_ffn_Wscale_dp, L0_ffn_W_up, L0_ffn_W_gate, L0_ffn_W_down))
    x = x + s * g
    xn = _layernorm(x, axis=-1)
    s = _L1_attn_ref(xn, L1_attn_Wq, L1_attn_Wk, L1_attn_Wv, L1_attn_Wo, L1_attn_Wb, L1_attn_Wa, L1_attn_Wg, L1_attn_conv_q, L1_attn_conv_k, L1_attn_conv_v, L1_attn_o_norm_w, L1_attn_A_log, L1_attn_dt_bias)
    g = _silu(_L1_ffn_ref(xn, L1_ffn_up_weight, L1_ffn_down_weight, L1_ffn_up_scale, L1_ffn_down_scale, L1_ffn_output_scale))
    x = x + s * g
    return x

_drawn_inputs = setup_inputs


def setup_inputs(seed=0):
    import zlib

    import numpy as np

    out = dict(_drawn_inputs(seed))
    spreads = {'L1_attn_o_norm_w': (1.0, 0.2),
     'L1_ffn_up_scale': (1.0, 0.2),
     'L1_ffn_down_scale': (1.0, 0.2)}
    factors = {}
    for name, (base, spread) in spreads.items():
        noise = np.random.default_rng([zlib.crc32(name.encode()), seed]).standard_normal(out[name].shape)
        drawn = base * np.exp(spread * noise) if base else spread * noise
        out[name] = jnp.asarray(drawn.astype(out[name].dtype))
    for name, factor in factors.items():
        out[name] = (out[name] * factor).astype(out[name].dtype)
    return out
```

```python
import concourse.bass as bass
from concourse import mybir
from contextlib import ExitStack

F32 = mybir.dt.float32
F16 = mybir.dt.float16
I32 = mybir.dt.int32
ALU = mybir.AluOpType
ACT = mybir.ActivationFunctionType
AX = mybir.AxisListType

P = 128
B, T, D = 4, 512, 512
KT = D // P
TT = T // P
NT = B * TT
NH, NKV = 32, 8
G = NH // NKV
DH = D // NH
VW = DH + 1
SC = G * TT
INTER = 2048
FT = INTER // P
UG = 2 * FT
NCH = UG // 4
ONE = 1
RAISE = 16.0


def layer0(nc, d, x1_dram):
    ctx = ExitStack()
    with ctx:
        def sb(name, shape, dt):
            return ctx.enter_context(nc.sbuf_tensor(name, shape, dt))

        def sem(name):
            return ctx.enter_context(nc.semaphore(name))

        bank = [ctx.enter_context(nc.psum_tensor(f"bank{i}", [P, 512], F32)) for i in range(8)]
        SA, SB, OB, GB = bank[0:2], bank[2:4], bank[4], bank[5:8]

        ident = sb("ident", [P, P], F16)
        onecol = sb("onecol", [P, 1], F32)
        epscol = sb("epscol", [P, 1], F32)
        had = sb("had", [P, P], F32)
        wq = sb("wq", [P, KT, NKV, P], F16)
        wk = sb("wk", [P, KT, NKV, P], F16)
        wv = sb("wv", [P, KT, NKV * DH], F16)
        wo = sb("wo", [P, KT, D], F16)
        ug_hi = sb("ug_hi", [P, KT, 2 * INTER], F16)
        ug_lo = sb("ug_lo", [P, KT, 2 * INTER], F16)
        dn = sb("dn", [P, FT, D], F32)
        su_raw = sb("su_raw", [P, KT], F32)
        sud = sb("sud", [P, FT], F32)
        sudn = sb("sudn", [P, FT], F32)
        wsc = sb("wsc", [P, UG], F32)
        wsd = sb("wsd", [P, D], F32)
        amax = sb("amax", [P, 1 + NCH], F32)
        amaxa = sb("amaxa", [P, 1 + NCH], F32)
        powr = sb("powr", [P, 1 + NCH], F32)
        invp = sb("invp", [P, 1 + NCH], F32)
        sun = sb("sun", [P, KT], F32)
        suc = sb("suc", [P, 2, KT], F32)
        usc = sb("usc", [P, UG], F32)
        gsc = sb("gsc", [P, FT], F32)
        hsc = sb("hsc", [P, FT], F32)
        xnT = sb("xnT", [P, KT, B * T], F16)
        st = sb("st", [P, NT, 6], F32)
        mv = sb("mv", [P, NT, 2], F32)
        sd = sb("sd", [P, NT], F32)
        rs = sb("rs", [P, NT], F32)
        h = sb("h", [P, FT, T], F32)
        hflat = h[:, :, :].rearrange("p a b -> p (a b)")
        wbuf = [hflat[:, i * 2048:(i + 1) * 2048].rearrange("p (k n) -> p k n", k=KT) for i in range(2)]
        bfly = hflat[:, 4096:6144].rearrange("p (k n) -> p k n", k=KT)
        bout = hflat[:, 6144:8192].rearrange("p (k n) -> p k n", k=KT)
        q16 = sb("q16", [P, T], F16)
        kA = sb("kA", [P, T], F16)
        qB = sb("qB", [P, T], F16)
        kB = sb("kB", [P, T], F16)
        mS = sb("mS", [P, TT, P], F16)
        probs = sb("probs", [P, 4, T], F16)
        vaug = sb("vaug", [P, TT, NKV, VW], F16)
        rl = sb("rl", [P, SC], F32)
        otok = sb("otok", [P, TT, D], F16)
        oT = sb("oT", [P, KT, T], F16)
        tg = sb("tg", [P, T], F32)
        gs = sb("gs", [P, T], F32)
        fd = sb("fd", [P, 2, D], F32)
        th = sb("th", [P, 2, D], F32)
        xres = sb("xres", [P, 2, D], F16)
        x1 = sb("x1", [P, 2, D], F32)
        dflat = dn[:, :, :].rearrange("p a b -> p (a b)").bitcast(F16).rearrange("p (i t n) -> p i t n", i=2, t=NT)
        x16, xn = dflat[:, 0], dflat[:, 1]

        S = {n: sem(n) for n in (
            "turns", "x_in0", "x_in1", "x_in2", "x_in3", "const_in", "w_in0", "w_in1", "dn_in", "proj_in", "scal_in",
            "stats", "mvr", "sd_ready", "rs_ready", "xn_ready", "xnT_ps", "xnT_ready",
            "amax_ready", "amax_all", "pow_a", "pow_b", "suc_ready", "bf1", "bf2", "ug_ps", "ug_hi_ready", "ug_lo_ready",
            "sc_ready", "dbf", "dn_ps", "dn_ready", "init",
            "q_ps", "k_ps", "q_ready", "k_ready", "sa_ps", "max_done", "mT_ps", "qka_ready",
            "sb_ps", "p_ready", "pv_done", "rl_ready", "o_done", "v_ps", "v_ready",
            "gate_ps", "tanh_ready", "gs_done", "up_ps", "h_ready",
            "oT_ps", "oT_ready", "down_ps", "fd_done", "th_ready", "g2_done", "wo_ps", "y_done", "x1_ready", "x1_out0", "x1_out1", "xres_in0", "xres_in1")}

        def settle(eng):
            eng.sem_inc(S["turns"], 1)

        OWN0 = {
            "pe": ["sa_ps", "sb_ps", "mT_ps"],
            "act": ["oT_ready"],
            "dve": ["qka_ready", "h_ready", "gs_done", "fd_done", "x1_ready", "y_done", "o_done"],
            "sp": ["x1_out0", "x1_out1"],
        }

        def start(eng, who):
            for n in OWN0[who]:
                eng.sem_inc(S[n], ONE)

        block = ctx.enter_context(nc.Block())

        @block.sync
        def _(sp):
            start(sp, "sp")
            for b in range(B):
                sp.dma_start(x16[:, b * TT:(b + 1) * TT, :],
                             d["x"][b].rearrange("(t p) n -> p t n", p=P)).then_inc(S[f"x_in{b}"], 16)
            sp.dma_start(ident[:, :], d["ident16"]).then_inc(S["const_in"], 16)
            sp.dma_start(had[:, :], d["had"]).then_inc(S["const_in"], 16)
            sp.dma_start(onecol[:, :], d["onecol"]).then_inc(S["const_in"], 16)
            sp.dma_start(su_raw[:, :], d["su_ug"]).then_inc(S["scal_in"], 16)
            sp.dma_start(sud[:, :], d["su_dp"]).then_inc(S["scal_in"], 16)
            sp.dma_start(wsc[:, :], d["wscale_ug"]).then_inc(S["scal_in"], 16)
            sp.dma_start(wsd[:, :], d["wscale_dp"].partition_broadcast(P)).then_inc(S["scal_in"], 16)
            for c in range(NCH):
                if c >= 2:
                    sp.wait_ge(S["bf1"], (c - 1) * 2)
                    sp.wait_ge(S["amax_ready"], c)
                sp.dma_start(wbuf[c % 2], d["ug"][c]).then_inc(S[f"w_in{c % 2}"], 16)
            sp.dma_start(wq[:, :, :, :], d["wq"]).then_inc(S["proj_in"], 16)
            sp.dma_start(wk[:, :, :, :], d["wk"]).then_inc(S["proj_in"], 16)
            sp.dma_start(wv[:, :, :], d["wv"]).then_inc(S["proj_in"], 16)
            sp.dma_start(wo[:, :, :], d["wo"]).then_inc(S["proj_in"], 16)
            sp.wait_ge(S["ug_ps"], KT * NCH)
            sp.wait_ge(S["bf2"], 2 * NCH)
            sp.dma_start(h[:, :, :], d["down"]).then_inc(S["dn_in"], 16)
            with sp.Fori(0, B) as b:
                for tt in range(TT):
                    sp.wait_ge(S["x1_ready"], (b * TT + tt - 1 if tt >= 2 else b * TT) + ONE)
                    settle(sp)
                    sp.dma_start(xres[:, tt % 2, :], d["x"][b, tt * P:(tt + 1) * P, :]).then_inc(S[f"xres_in{tt % 2}"], 16)
                    if tt == 0:
                        continue
                    sp.wait_ge(S["x1_ready"], b * TT + tt + ONE)
                    settle(sp)
                    sp.dma_start(x1_dram[b, tt - 1], x1[:, (tt - 1) % 2, :]).then_inc(S[f"x1_out{(tt - 1) % 2}"], 16)
                sp.wait_ge(S["x1_ready"], b * TT + TT + ONE)
                settle(sp)
                sp.dma_start(x1_dram[b, TT - 1], x1[:, 1, :]).then_inc(S["x1_out1"], 16)
            sp.wait_ge(S["x1_out0"], 16 * NT // 2 + ONE)
            sp.wait_ge(S["x1_out1"], 16 * NT // 2 + ONE)

        @block.gpsimd
        def _(pool):
            pool.memset(mS[:, :, :], 0.0).then_inc(S["init"], 1)
            pool.memset(vaug[:, :, :, :], 1.0).then_inc(S["init"], 1)
            pool.memset(epscol[:, :], 1e-5).then_inc(S["init"], 1)
            for c in range(1 + NCH):
                pool.wait_ge(S["amax_ready"], c + 1)
                pool.partition_all_reduce(amaxa[:, c:c + 1], amax[:, c:c + 1], P,
                                          bass.bass_isa.ReduceOp.max).then_inc(S["amax_all"], 1)

        @block.vector
        def _(v):
            start(v, "dve")
            for tt in range(NT):
                if tt % TT == 0:
                    v.wait_ge(S[f"x_in{tt // TT}"], 16)
                v.bn_stats(st[:, tt, :], x16[:, tt, :]).then_inc(S["stats"], 1)
            for tt in range(NT):
                v.wait_ge(S["stats"], tt + 1)
                v.bn_aggr(mv[:, tt, :], st[:, tt, :]).then_inc(S["mvr"], 1)
            v.wait_ge(S["sd_ready"], 1)
            v.reciprocal(rs[:, :], sd[:, :]).then_inc(S["rs_ready"], 1)
            v.wait_ge(S["rs_ready"], 1)
            for tt in range(NT):
                v.tensor_scalar(xn[:, tt, :], x16[:, tt, :], mv[:, tt, 0:1], rs[:, tt:tt + 1],
                                ALU.subtract, ALU.mult).then_inc(S["xn_ready"], 1)
            v.wait_ge(S["scal_in"], 16 * 4)

            def power_of_two(c):
                v.wait_ge(S["amax_all"], c + 1)
                v.tensor_scalar(amaxa[:, c:c + 1], amaxa[:, c:c + 1], 1e-30, None, ALU.max).then_inc(S["pow_a"], 1)
                v.wait_ge(S["pow_a"], 3 * c + 1)
                v.tensor_scalar(powr[:, c:c + 1].bitcast(I32), amaxa[:, c:c + 1].bitcast(I32), 0x7F800000, None,
                                ALU.bitwise_and).then_inc(S["pow_a"], 1)
                v.wait_ge(S["pow_a"], 3 * c + 2)
                v.reciprocal(invp[:, c:c + 1], powr[:, c:c + 1]).then_inc(S["pow_a"], 1)
                v.wait_ge(S["pow_a"], 3 * c + 3)

            v.tensor_reduce(amax[:, 0:1], su_raw[:, :], AX.X, ALU.max,
                            apply_absolute_value=True).then_inc(S["amax_ready"], 1)
            power_of_two(0)
            v.tensor_scalar(sun[:, :], su_raw[:, :], invp[:, 0:1], RAISE, ALU.mult, ALU.mult).then_inc(S["pow_b"], 1)
            v.tensor_scalar(sudn[:, :], sud[:, :], float(INTER) ** -0.5, None, ALU.mult).then_inc(S["sc_ready"], 1)
            v.wait_ge(S["pow_b"], 1)
            for c in range(NCH):
                par = c % 2
                w = wbuf[par]
                v.wait_ge(S[f"w_in{par}"], 16 * (c // 2 + 1))
                v.tensor_reduce(amax[:, 1 + c:2 + c], w, AX.XY, ALU.max,
                                apply_absolute_value=True).then_inc(S["amax_ready"], 1)
                if c:
                    v.wait_ge(S["bf2"], 2 * c)
                wp = w.rearrange("p (a s) n -> p a s n", s=2)
                tp = bfly.rearrange("p (a s) n -> p a s n", s=2)
                v.tensor_tensor(tp[:, :, 0, :], wp[:, :, 0, :], wp[:, :, 1, :], ALU.add).then_inc(S["bf1"], 1)
                v.tensor_tensor(tp[:, :, 1, :], wp[:, :, 0, :], wp[:, :, 1, :], ALU.subtract).then_inc(S["bf1"], 1)
                v.wait_ge(S["bf1"], 2 * (c + 1))
                if c:
                    v.wait_ge(S["ug_ps"], KT * c)
                v.tensor_tensor(bout[:, 0:2, :], bfly[:, 0:2, :], bfly[:, 2:4, :], ALU.add).then_inc(S["bf2"], 1)
                v.tensor_tensor(bout[:, 2:4, :], bfly[:, 0:2, :], bfly[:, 2:4, :], ALU.subtract).then_inc(S["bf2"], 1)
                power_of_two(c + 1)
                if c > 1:
                    v.wait_ge(S["ug_hi_ready"], KT * (c - 1))
                v.tensor_scalar(suc[:, par, :], sun[:, :], invp[:, c + 1:c + 2], None, ALU.mult).then_inc(S["suc_ready"], 1)
                v.wait_ge(S["suc_ready"], c + 1)
                v.tensor_scalar(usc[:, 4 * c:4 * c + 4], wsc[:, 4 * c:4 * c + 4], powr[:, c + 1:c + 2],
                                float(D) ** -0.5 / RAISE, ALU.mult, ALU.mult).then_inc(S["sc_ready"], 1)
                v.wait_ge(S["sc_ready"], 2 * c + 2)
                v.tensor_scalar(usc[:, 4 * c:4 * c + 4], usc[:, 4 * c:4 * c + 4], powr[:, 0:1],
                                None, ALU.mult).then_inc(S["sc_ready"], 1)
                for kt in range(KT):
                    n = KT * c + kt
                    v.wait_ge(S["ug_hi_ready"], n + 1)
                    v.scalar_tensor_tensor(ug_lo[:, kt, c * 512:(c + 1) * 512], bank[n % 4][:, :],
                                           suc[:, par, kt:kt + 1], ug_hi[:, kt, c * 512:(c + 1) * 512],
                                           ALU.mult, ALU.subtract).then_inc(S["ug_lo_ready"], 1)
            v.wait_ge(S["sc_ready"], 2 * NCH + 1)
            v.tensor_scalar(gsc[:, :], usc[:, FT:UG], 0.5, None, ALU.mult).then_inc(S["sc_ready"], 1)
            v.scalar_tensor_tensor(hsc[:, :], usc[:, 0:FT], 0.5, usc[:, FT:UG], ALU.mult, ALU.mult).then_inc(S["sc_ready"], 1)
            v.wait_ge(S["dn_in"], 16)
            v.wait_ge(S["xnT_ps"], NT)
            src, dst = h, dn
            for lv in range(4):
                a = src[:, :, :].rearrange("p (a s c) n -> p a s (c n)", s=2, c=1 << lv)
                o = dst[:, :, :].rearrange("p (a s c) n -> p a s (c n)", s=2, c=1 << lv)
                if lv:
                    v.wait_ge(S["dbf"], 2 * lv)
                v.tensor_tensor(o[:, :, 0, :], a[:, :, 0, :], a[:, :, 1, :], ALU.add).then_inc(S["dbf"], 1)
                v.tensor_tensor(o[:, :, 1, :], a[:, :, 0, :], a[:, :, 1, :], ALU.subtract).then_inc(S["dbf"], 1)
                src, dst = dst, src
            v.sem_inc(S["max_done"], 2)

            def row_max(un, i):
                v.wait_ge(S["sa_ps"], un * SC + i + 1 + ONE)
                qt, j = divmod(i, G)
                v.tensor_reduce(mS[:, qt, 32 * j + DH:32 * j + DH + 1], SA[i % 2][:, :], AX.X,
                                ALU.max).then_inc(S["max_done"], 1)

            def k_copy(un):
                v.wait_ge(S["k_ready"], un + 1)
                v.wait_ge(S["sb_ps"], un * SC + ONE)
                v.tensor_copy(kB[:, :], kA[:, :]).then_inc(S["qka_ready"], 1)

            def q_aug(un):
                v.wait_ge(S["mT_ps"], un + 1 + ONE)
                v.tensor_tensor(qB[:, :], q16[:, :], GB[0][:, :].bitcast(F16)[:, 0:T],
                                ALU.subtract).then_inc(S["qka_ready"], 1)

            def gate_mul(u, t):
                v.wait_ge(S["tanh_ready"], u * 2 + t + 1)
                v.wait_ge(S["h_ready"], u * 2 + t + ONE)
                v.scalar_tensor_tensor(gs[:, :], tg[:, :], 1.0, GB[2 - t][:, :],
                                       ALU.add, ALU.mult).then_inc(S["gs_done"], 1)

            def up_mul(u, g, t):
                v.wait_ge(S["gs_done"], u * 2 + t + 1 + ONE)
                v.wait_ge(S["up_ps"], u * 2 + t + 1)
                ft = g * 2 + t
                v.scalar_tensor_tensor(h[:, ft, :], GB[2 * t][:, :], hsc[:, ft:ft + 1] if isinstance(ft, int) else hsc[:, bass.ds(ft, 1)],
                                       gs[:, :], ALU.mult, ALU.mult).then_inc(S["h_ready"], 1)

            def normalise(u, g):
                v.wait_ge(S["pv_done"], u * SC + SC + 4)
                v.wait_ge(S["o_done"], u + ONE)
                ob = OB[:, 0:SC * VW].rearrange("p (t j c) -> p t j c", t=TT, j=G)
                v.reciprocal(rl[:, :].rearrange("p (t j c) -> p t j c", t=TT, c=1),
                             ob[:, :, :, DH:VW]).then_inc(S["rl_ready"], 1)
                v.wait_ge(S["rl_ready"], u + 1)
                v.tensor_tensor(otok[:, :, bass.ds(g * (G * DH), G * DH)].rearrange("p t (j c) -> p t j c", j=G),
                                ob[:, :, :, 0:DH],
                                rl[:, :].rearrange("p (t j c) -> p t j c", t=TT, c=1).to_broadcast([P, TT, G, DH]),
                                ALU.mult).then_inc(S["o_done"], 1)

            v.wait_ge(S["init"], 3)
            v.wait_ge(S["dn_ready"], FT)
            v.wait_ge(S["sc_ready"], 2 * NCH + 3)
            with v.Fori(0, B) as b:
                for i in range(SC):
                    if i == 0:
                        v.wait_ge(S["mT_ps"], b * NKV + ONE)
                    row_max(b * NKV, i)
                k_copy(b * NKV)
                q_aug(b * NKV)
                with v.Fori(0, NKV - 1) as g:
                    u = b * NKV + g
                    for i in range(SC):
                        if i == 0:
                            v.wait_ge(S["mT_ps"], u + 1 + ONE)
                        row_max(u + 1, i)
                        if i == 5:
                            gate_mul(u, 0)
                        if i == 9:
                            up_mul(u, g, 0)
                        if i == 13:
                            gate_mul(u, 1)
                    up_mul(u, g, 1)
                    k_copy(u + 1)
                    normalise(u, g)
                    q_aug(u + 1)
                u = b * NKV + (NKV - 1)
                gate_mul(u, 0)
                up_mul(u, NKV - 1, 0)
                gate_mul(u, 1)
                up_mul(u, NKV - 1, 1)
                normalise(u, NKV - 1)
                for tt in range(TT):
                    n = b * TT + tt
                    v.wait_ge(S["down_ps"], n + 1)
                    v.wait_ge(S["x1_ready"], (n - 1 if tt >= 2 else b * TT) + ONE)
                    v.tensor_tensor(fd[:, tt % 2, :], GB[1 + tt % 2][:, :], wsd[:, :], ALU.mult).then_inc(S["fd_done"], 1)
                    v.wait_ge(S["th_ready"], n + 1)
                    v.scalar_tensor_tensor(th[:, tt % 2, :], th[:, tt % 2, :], 1.0, fd[:, tt % 2, :],
                                           ALU.add, ALU.mult).then_inc(S["g2_done"], 1)
                    v.wait_ge(S["g2_done"], n + 1)
                    v.wait_ge(S["wo_ps"], n + 1)
                    v.scalar_tensor_tensor(fd[:, tt % 2, :], SA[tt % 2][:, :], 0.5, th[:, tt % 2, :],
                                           ALU.mult, ALU.mult).then_inc(S["y_done"], 1)
                    v.wait_ge(S["y_done"], n + 1 + ONE)
                    v.wait_ge(S[f"x1_out{tt % 2}"], (b * 2 + tt // 2) * 16 + ONE)
                    v.wait_ge(S[f"xres_in{tt % 2}"], (b * 2 + tt // 2 + 1) * 16)
                    v.tensor_tensor(x1[:, tt % 2, :], fd[:, tt % 2, :], xres[:, tt % 2, :], ALU.add).then_inc(S["x1_ready"], 1)

        @block.scalar
        def _(a):
            start(a, "act")
            a.wait_ge(S["init"], 3)
            a.wait_ge(S["mvr"], NT)
            a.activation(sd[:, :], mv[:, :, 1], ACT.Sqrt, bias=epscol[:, :]).then_inc(S["sd_ready"], 1)
            for b in range(B):
                for kt in range(KT):
                    n = b * KT + kt
                    a.wait_ge(S["xnT_ps"], n + 1)
                    a.activation(xnT[:, kt, b * T:(b + 1) * T], bank[4 + n % 4][:, :].bitcast(F16)[:, 0:T],
                                 ACT.Copy).then_inc(S["xnT_ready"], 1)
            for c in range(NCH):
                a.wait_ge(S["suc_ready"], c + 1)
                for kt in range(KT):
                    n = KT * c + kt
                    a.wait_ge(S["ug_ps"], n + 1)
                    a.activation(ug_hi[:, kt, c * 512:(c + 1) * 512], bank[n % 4][:, :], ACT.Copy,
                                 scale=suc[:, c % 2, kt:kt + 1]).then_inc(S["ug_hi_ready"], 1)
            a.wait_ge(S["sc_ready"], 1)
            for ft in range(FT):
                a.wait_ge(S["dn_ps"], ft + 1)
                a.activation(dn[:, ft, :], bank[4 + ft % 4][:, :], ACT.Copy,
                             scale=sudn[:, ft:ft + 1]).then_inc(S["dn_ready"], 1)
            a.sem_inc(S["p_ready"], 2)
            a.wait_ge(S["const_in"], 48)
            a.wait_ge(S["sc_ready"], 2 * NCH + 3)

            def projections(un):
                a.wait_ge(S["q_ps"], un + 1)
                a.wait_ge(S["sa_ps"], un * SC + ONE)
                a.wait_ge(S["qka_ready"], un * 2 + ONE)
                a.activation(q16[:, :], GB[0][:, :], ACT.Copy).then_inc(S["q_ready"], 1)
                a.wait_ge(S["k_ps"], un + 1)
                a.activation(kA[:, :], GB[1][:, :], ACT.Identity, bias=onecol[:, :]).then_inc(S["k_ready"], 1)

            def exps(u, i):
                a.wait_ge(S["sb_ps"], u * SC + i + 1 + ONE)
                a.wait_ge(S["pv_done"], u * SC + i + 1)
                a.activation(probs[:, i % 4, :], SB[i % 2][:, :], ACT.Exp,
                             scale=float(DH) ** -0.5).then_inc(S["p_ready"], 1)

            def tanh_gate(u, g, t):
                a.wait_ge(S["gate_ps"], u * 2 + t + 1)
                a.wait_ge(S["gs_done"], u * 2 + t + ONE)
                ft = g * 2 + t
                a.activation(tg[:, :], GB[2 - t][:, :], ACT.Tanh,
                             scale=gsc[:, ft:ft + 1] if isinstance(ft, int) else gsc[:, bass.ds(ft, 1)]).then_inc(S["tanh_ready"], 1)

            with a.Fori(0, B) as b:
                a.wait_ge(S["v_ps"], b + 1)
                a.activation(vaug[:, :, :, 0:DH],
                             OB[:, :].rearrange("p (t g c) -> p t g c", t=TT, g=NKV), ACT.Copy).then_inc(S["v_ready"], 1)
                projections(b * NKV)
                with a.Fori(0, NKV - 1) as g:
                    u = b * NKV + g
                    projections(u + 1)
                    for i in range(SC):
                        exps(u, i)
                        if i == 5:
                            tanh_gate(u, g, 0)
                        if i == 11:
                            tanh_gate(u, g, 1)
                u = b * NKV + (NKV - 1)
                for i in range(SC):
                    exps(u, i)
                    if i == 5:
                        tanh_gate(u, NKV - 1, 0)
                    if i == 11:
                        tanh_gate(u, NKV - 1, 1)
                for kt in range(KT):
                    a.wait_ge(S["oT_ps"], b * KT + kt + 1)
                    a.activation(oT[:, kt, :], SB[kt % 2][:, :].bitcast(F16)[:, 0:T], ACT.Copy).then_inc(S["oT_ready"], 1)
                for tt in range(TT):
                    n = b * TT + tt
                    a.wait_ge(S["fd_done"], n + 1 + ONE)
                    a.wait_ge(S["y_done"], ((n - 1) if tt >= 2 else b * TT) + ONE)
                    a.activation(th[:, tt % 2, :], fd[:, tt % 2, :], ACT.Tanh, scale=0.5).then_inc(S["th_ready"], 1)

        @block.tensor
        def _(pe):
            start(pe, "pe")
            pe.wait_ge(S["const_in"], 48)
            for b in range(B):
                pe.wait_ge(S["xn_ready"], (b + 1) * TT)
                for kt in range(KT):
                    n = b * KT + kt
                    if n >= 4:
                        pe.wait_ge(S["xnT_ready"], n - 3)
                    bk = bank[4 + n % 4][:, :].bitcast(F16)
                    for tt in range(TT):
                        mm = pe.transpose(bk[:, tt * P:(tt + 1) * P], xn[:, b * TT + tt, kt * P:(kt + 1) * P], ident[:, :])
                    mm.then_inc(S["xnT_ps"], 1)
            for c in range(NCH):
                pe.wait_ge(S["bf2"], 2 * (c + 1))
                for kt in range(KT):
                    n = KT * c + kt
                    if n >= 4:
                        pe.wait_ge(S["ug_lo_ready"], n - 3)
                    pe.matmul(bank[n % 4][:, :], had[:, :], bout[:, kt, :], start=True, stop=True).then_inc(S["ug_ps"], 1)
            pe.wait_ge(S["dbf"], 8)
            pe.wait_ge(S["xnT_ready"], NT)
            for ft in range(FT):
                if ft >= 4:
                    pe.wait_ge(S["dn_ready"], ft - 3)
                pe.matmul(bank[4 + ft % 4][:, :], had[:, :], h[:, ft, :], start=True, stop=True).then_inc(S["dn_ps"], 1)
            pe.wait_ge(S["proj_in"], 64)
            pe.wait_ge(S["dn_ready"], FT)
            pe.wait_ge(S["ug_lo_ready"], KT * NCH)
            pe.sem_inc(S["pv_done"], 4)

            def xnb(b, kt):
                return xnT[:, kt, bass.ds(b * T, T)]

            def projections(un, b, g, first):
                pe.wait_ge(S["qka_ready"], un * 2 + ONE)
                if first:
                    pe.wait_ge(S["h_ready"], un * 2 + ONE)
                for kt in range(KT):
                    mm = pe.matmul(GB[0][:, :], wq[:, kt, g, :] if isinstance(g, int) else wq[:, kt, bass.ds(g, 1), :], xnb(b, kt), start=kt == 0, stop=kt == KT - 1)
                mm.then_inc(S["q_ps"], 1)
                if first:
                    pe.wait_ge(S["fd_done"], b * TT + ONE)
                else:
                    pe.wait_ge(S["gs_done"], (un - 1) * 2 + ONE)
                    pe.wait_ge(S["k_ready"], un)
                for kt in range(KT):
                    mm = pe.matmul(GB[1][:, :], wk[:, kt, g, :] if isinstance(g, int) else wk[:, kt, bass.ds(g, 1), :], xnb(b, kt), start=kt == 0, stop=kt == KT - 1)
                mm.then_inc(S["k_ps"], 1)
                pe.wait_ge(S["q_ready"], un + 1)
                pe.wait_ge(S["k_ready"], un + 1)

            def score_a(un, i):
                qt, j = divmod(i, G)
                pe.wait_ge(S["max_done"], un * SC + i + 1)
                pe.matmul(SA[i % 2][:, :], q16[32 * j:32 * j + 32, qt * P:(qt + 1) * P],
                          kA[32 * j:32 * j + 32, :], start=True, stop=True).then_inc(S["sa_ps"], 1)

            def maxima(un, first):
                pe.wait_ge(S["max_done"], un * SC + SC + 2)
                if first:
                    pe.wait_ge(S["q_ready"], un + 1)
                else:
                    pe.wait_ge(S["h_ready"], un * 2 - 1 + ONE)
                bk = GB[0][:, :].bitcast(F16)
                for qt in range(TT):
                    mm = pe.transpose(bk[:, qt * P:(qt + 1) * P], mS[:, qt, :], ident[:, :])
                mm.then_inc(S["mT_ps"], 1)

            def score_b(u, i):
                kt, j = divmod(i, G)
                pe.wait_ge(S["p_ready"], u * SC + i + 1)
                pe.matmul(SB[i % 2][:, :], kB[32 * j:32 * j + 32, kt * P:(kt + 1) * P],
                          qB[32 * j:32 * j + 32, :], start=True, stop=True).then_inc(S["sb_ps"], 1)

            def weigh(u, g, i):
                kt, j = divmod(i, G)
                pe.wait_ge(S["p_ready"], u * SC + i + 3)
                for qt in range(TT):
                    c = (qt * G + j) * VW
                    mm = pe.matmul(OB[:, c:c + VW], probs[:, i % 4, qt * P:(qt + 1) * P],
                                   vaug[:, kt, g, :] if isinstance(g, int) else vaug[:, kt, bass.ds(g, 1), :],
                                   start=i == 0 and qt == 0, stop=i == SC - 1 and qt == TT - 1, skip_group_check=True)
                mm.then_inc(S["pv_done"], 1)

            def ffn_mm(u, b, g, n, last):
                grp, r = divmod(n, 8)
                t, up = divmod(grp, 2)
                bk = GB[2 * t] if up else GB[2 - t]
                if r == 0:
                    if grp == 0:
                        pe.wait_ge(S["h_ready"], u * 2 + ONE)
                        pe.wait_ge(S["fd_done"], b * TT + ONE)
                    if grp == 1:
                        pe.wait_ge(S["qka_ready"], u * 2 + 2 + ONE)
                        if not last:
                            pe.wait_ge(S["q_ready"], u + 2)
                    if grp == 2:
                        pe.wait_ge(S["gs_done"], u * 2 + ONE)
                        if not last:
                            pe.wait_ge(S["k_ready"], u + 2)
                    if grp == 3:
                        pe.wait_ge(S["gs_done"], u * 2 + 1 + ONE)
                kt, part = divmod(r, 2)
                w = (ug_hi, ug_lo)[part]
                col = (g * 2 + t) * P + (0 if up else INTER)
                mm = pe.matmul(bk[:, :], w[:, kt, bass.ds(col, P)], xnb(b, kt), start=r == 0, stop=r == 7)
                if r == 7:
                    mm.then_inc(S["up_ps" if up else "gate_ps"], 1)

            with pe.Fori(0, B) as b:
                pe.wait_ge(S["o_done"], b * NKV + ONE)
                for tt in range(TT):
                    for kt in range(KT):
                        mm = pe.matmul(OB[:, tt * P:(tt + 1) * P], xnT[:, kt, bass.ds(b * T + tt * P, P)],
                                       wv[:, kt, :], start=kt == 0, stop=kt == KT - 1)
                mm.then_inc(S["v_ps"], 1)
                u0 = b * NKV
                projections(u0, b, 0, True)
                pe.wait_ge(S["y_done"], b * TT + ONE)
                for i in range(SC):
                    score_a(u0, i)
                maxima(u0, True)
                pe.wait_ge(S["v_ready"], b + 1)
                pe.wait_ge(S["oT_ready"], b * KT + ONE)
                settle(pe)
                with pe.Fori(0, NKV - 1) as g:
                    u = b * NKV + g
                    projections(u + 1, b, g + 1, False)
                    pe.wait_ge(S["qka_ready"], u * 2 + 2 + ONE)
                    for i in range(SC):
                        score_a(u + 1, i)
                        score_b(u, i)
                        if i == 2:
                            pe.wait_ge(S["o_done"], u + ONE)
                        if i >= 2:
                            weigh(u, g, i - 2)
                        ffn_mm(u, b, g, 2 * i, False)
                        ffn_mm(u, b, g, 2 * i + 1, False)
                    weigh(u, g, SC - 2)
                    weigh(u, g, SC - 1)
                    maxima(u + 1, False)
                u, g = b * NKV + (NKV - 1), NKV - 1
                pe.wait_ge(S["qka_ready"], u * 2 + 2 + ONE)
                for i in range(SC):
                    score_b(u, i)
                    if i == 2:
                        pe.wait_ge(S["o_done"], u + ONE)
                    if i >= 2:
                        weigh(u, g, i - 2)
                    ffn_mm(u, b, g, 2 * i, True)
                    ffn_mm(u, b, g, 2 * i + 1, True)
                weigh(u, g, SC - 2)
                weigh(u, g, SC - 1)

                def down(tt):
                    bk = GB[1 + tt % 2]
                    if tt == 0:
                        pe.wait_ge(S["gs_done"], u * 2 + 2 + ONE)
                        pe.wait_ge(S["h_ready"], u * 2 + 2 + ONE)
                    if tt >= 2:
                        pe.wait_ge(S["fd_done"], b * TT + tt - 1 + ONE)
                    for ft in range(FT):
                        mm = pe.matmul(bk[:, :], h[:, ft, tt * P:(tt + 1) * P], dn[:, ft, :],
                                       start=ft == 0, stop=ft == FT - 1)
                    mm.then_inc(S["down_ps"], 1)

                def turn(kt):
                    if kt == 0:
                        pe.wait_ge(S["o_done"], u + 1 + ONE)
                        pe.wait_ge(S["p_ready"], u * SC + SC + 2)
                    if kt >= 2:
                        pe.wait_ge(S["oT_ready"], b * KT + kt - 1 + ONE)
                    bk = SB[kt % 2][:, :].bitcast(F16)
                    for qt in range(TT):
                        mm = pe.transpose(bk[:, qt * P:(qt + 1) * P], otok[:, qt, kt * P:(kt + 1) * P], ident[:, :])
                    mm.then_inc(S["oT_ps"], 1)

                def project(tt):
                    if tt == 0:
                        pe.wait_ge(S["oT_ready"], b * KT + KT + ONE)
                        pe.wait_ge(S["max_done"], u * SC + SC + 2)
                    if tt >= 2:
                        pe.wait_ge(S["y_done"], b * TT + tt - 1 + ONE)
                    for kt in range(KT):
                        mm = pe.matmul(SA[tt % 2][:, :], oT[:, kt, tt * P:(tt + 1) * P], wo[:, kt, :],
                                       start=kt == 0, stop=kt == KT - 1)
                    mm.then_inc(S["wo_ps"], 1)

                down(0)
                turn(0)
                turn(1)
                down(1)
                turn(2)
                turn(3)
                project(0)
                down(2)
                project(1)
                down(3)
                project(2)
                project(3)


HD = 64
LH = 6
KW = LH * HD
MT = KW // P
NM = 3 * MT
HH = 3
NW1 = 4 * KW + 2 * LH
CONV = 4
LV = 7
HT = 2048 // P
XRAISE, WRAISE = 64.0, 128.0


def bank_order():
    v, a = [("bat",), ("ss",)], [("xT", k) for k in range(KT)] + [("ba",)] + [("pre", m) for m in range(NM)] + [("vec",)]
    for tt in range(TT):
        v += [("q", tt), ("k", tt), ("v", tt)]
        a += [(n, tt, hf) for hf in range(2) for n in ("D", "DT")] + [("kT", tt), ("qT", tt)]
        v += [(n, tt, hf) for hf in range(2) for n in ("KK", "KQ")] + [("gate", tt)]
        a += [("AT", tt, 0), ("AT", tt, 1)]
        for lv in range(LV):
            if lv:
                v += [("X", tt, lv, 0), ("X", tt, lv, 1), ("Y", tt, lv, 0), ("Y", tt, lv, 1)]
            a += [("TT", tt, lv, 0), ("TT", tt, lv, 1)]
        v += [("S", tt, 0), ("S", tt, 1), ("O", tt), ("SU", tt)]
        a += [("U", tt), ("yT", tt)]
    v += [("wo", tt) for tt in range(TT)]
    return {k: n for n, k in enumerate(v)}, {k: n for n, k in enumerate(a)}


def layer1(nc, d, x1_dram, out_dram):
    VI, AI = bank_order()
    NV, NA = len(VI), len(AI)
    ctx = ExitStack()
    with ctx:
        def sb(name, shape, dt=F32):
            return ctx.enter_context(nc.sbuf_tensor(name, shape, dt))

        def sem(name):
            return ctx.enter_context(nc.semaphore(name))

        vbank = [ctx.enter_context(nc.psum_tensor(f"vbank{i}", [P, 512], F32)) for i in range(3)]
        abank = [ctx.enter_context(nc.psum_tensor(f"abank{i}", [P, 512], F32)) for i in range(3)]
        fbank = [ctx.enter_context(nc.psum_tensor(f"fbank{i}", [P, 512], F32)) for i in range(2)]

        ident16 = sb("l1_ident16", [P, P], F16)
        cmat = sb("cmat", [P, 4, P])
        ident, upto, after, ones = (cmat[:, i, :] for i in range(4))
        negm = sb("negm", [P, LV, P])
        hsel = sb("hsel", [P, 2])
        onec = sb("onec", [P, 1])
        expo = sb("expo", [P, 48])
        w1 = sb("w1", [P, 2, KT, NW1], F16)
        w1h, w1l = w1[:, 0], w1[:, 1]
        up = sb("up", [P, KT, 2048], F16)
        down = sb("down", [P, HT, D], F16)
        wo1 = sb("wo1", [P, MT, D])
        cw = sb("cw", [P, NM, CONV])
        usn = sb("usn", [P, HT])
        dsc = sb("dsc", [P, D])
        onw = sb("onw", [P, KW])
        ab = sb("ab", [P, 2 * LH])
        negA = sb("negA", [P, LH])
        osc = sb("osc", [P, 1])
        am = sb("am", [P, 2])
        ama = sb("ama", [P, 2])
        pw = sb("pw", [P, 2])
        ipw = sb("ipw", [P, 2])
        un = sb("un", [P, 1])
        unh = sb("unh", [P, 1])
        hid = sb("hid", [P, 2, HT, T], F16)
        xb = sb("xb", [P, TT, D])
        xT = sb("xT", [P, KT, 2, T], F16)
        st = sb("l1_st", [P, TT, 6])
        mv = sb("l1_mv", [P, TT, 2])
        rs0 = sb("rs0", [P, TT])
        rs = sb("l1_rs", [P, TT])
        pre = sb("pre", [P, 2, CONV - 1 + T])
        ca = sb("ca", [P, T])
        ct = sb("ct", [P, T])
        sil = sb("sil", [P, NM, T])
        silf = sil[:, :, :].rearrange("p a b -> p (a b)").bitcast(F16)
        xh = silf[:, 0:TT * D].rearrange("p (t n) -> p t n", t=TT)
        xl = silf[:, TT * D:2 * TT * D].rearrange("p (t n) -> p t n", t=TT)
        ba = sb("ba", [2 * LH, T])
        z = sb("z", [P, TT, 2 * LH])
        ssq = sb("ssq", [P, TT, 2 * LH])
        rn = sb("rn", [P, TT, 2 * LH])
        sm = sb("sm", [P, 10, TT, LH])
        tb, beta, bhalf, az, ez, lz, spl, gg, nbg = (sm[:, i] for i in range(9))
        vec = sb("vec", [P, TT, 3 * LH])
        gcs = sb("gcs", [P, TT, MT])
        big = sb("big", [P, 9, LH, P])
        Gm, GT, BT, A, AT, Tm, TTm, E, gU = (big[:, i] for i in range(9))
        gL = E
        tok = sb("tok", [P, 9, KW])
        qt_, kt_, Rv, Kt, V2, U, o1, t1, gt = (tok[:, i, :] for i in range(9))
        S_ = sb("S_", [P, 2, MT, HD])
        ssS = sb("ssS", [P, MT, HD])
        os_ = sb("os_", [P, 3, LH])
        yT = sb("yT", [P, MT, T])
        r32 = sb("r32", [P, T])
        fd, th, sqf = ca, ct, yT[:, 0, :]
        xs = big[:, 0:3].rearrange("p a b c -> p (a b c)")[:, 0:TT * D].rearrange("p (t n) -> p t n", t=TT)
        xo = sb("xo", [P, 2, D])
        hidf = hid[:, :, :, :].rearrange("p a b c -> p (a b c)").bitcast(F32)
        wst = hidf[:, 0:KT * NW1].rearrange("p (k n) -> p k n", k=KT)
        upst = hidf.rearrange("p (k n) -> p k n", k=KT)
        dnst = hidf.rearrange("p (k n) -> p k n", k=HT)

        OWN = {
            "pe": ["v_full", "a_full", "f_full", "down_full"],
            "act": ["a_took", "tanh_c", "tb_r", "ez_r", "lz_r", "gate_t", "osq", "th_r", "r32_r",
                    "yT_r"],
            "dve": ["v_took", "st_r", "mv_r", "rs0_r", "xs_r", "xh_r", "xl_r", "conv", "sil_r", "beta_r", "bhalf_r", "az_r",
                    "spl_r", "g_r", "nbg_r", "gcs_r", "T0_r", "T_r", "kS_r",
                    "V2_r", "ssS_r", "oss_r", "or_r", "y_r", "fd_r", "g2_r", "xo_r", "S0_r"],
            "pool": ["rs_r", "sq_r", "rn_r", "gL_r", "gU_r", "GTm_r", "Kt_r", "orn_r", "gw_r", "hid_r"],
            "pe2": ["sq_used"],
            "sp": ["xb_in", "xo_out0", "xo_out1"],
        }
        S = {n: sem("l1_" + n) for n in sum(OWN.values(), []) + [
            "const", "w_in", "up_in", "dn_in", "turns", "m_r", "m_a", "m_p", "un_r", "w1h_r", "w1l_r", "up_r", "down_r",
            "pads", "usn_r", "dsc_r", "negA_r", "onw_r"]}

        def settle(eng):
            eng.sem_inc(S["turns"], 1)

        def start(eng, who):
            for n in OWN[who]:
                eng.sem_inc(S[n], ONE + (3 if n in ("v_took", "a_took") else 0))

        def hb(col, n):
            return col.rearrange("p (h c) -> p h c", c=1).to_broadcast([P, col.shape[-1], n])

        def over(mat, n):
            return mat.rearrange("p (h c) -> p h c", h=1).to_broadcast([P, n, P])

        def heads(t):
            return t.rearrange("p (h c) -> p h c", h=LH)

        block = ctx.enter_context(nc.Block())

        @block.sync
        def _(sp):
            start(sp, "sp")
            sp.dma_start(wst, d["w1"]).then_inc(S["w_in"], 16)
            for t, n in ((ident16, "ident16"), (cmat, "cmat"), (negm, "negm"), (hsel, "hsel"), (wo1, "wo1"),
                         (cw, "cw"), (usn, "up_scale")):
                sp.dma_start(t[:], d[n]).then_inc(S["const"], 16)
            for t, n in ((dsc, "down_scale"), (onw, "onw"), (ab, "ab_bias"), (negA, "a_log"), (osc, "out_scale")):
                sp.dma_start(t[:, :], d[n].partition_broadcast(P)).then_inc(S["const"], 16)
            sp.wait_ge(S["w1h_r"], 1)
            sp.wait_ge(S["w1l_r"], 1)
            sp.dma_start(upst, d["upw"]).then_inc(S["up_in"], 16)
            sp.wait_ge(S["up_r"], 1)
            sp.dma_start(dnst, d["downw"]).then_inc(S["dn_in"], 16)
            with sp.Fori(0, B) as b:
                sp.wait_ge(S["xo_r"], b * TT + ONE)
                settle(sp)
                sp.dma_start(xb[:, :, :], x1_dram[b].rearrange("t p n -> p t n")).then_inc(S["xb_in"], 16)
                for tt in range(TT):
                    sp.wait_ge(S["xo_r"], b * TT + tt + 1 + ONE)
                    settle(sp)
                    sp.dma_start(out_dram[b, tt], xo[:, tt % 2, :]).then_inc(S[f"xo_out{tt % 2}"], 16)
            sp.wait_ge(S["xo_out0"], 16 * B * TT // 2 + ONE)
            sp.wait_ge(S["xo_out1"], 16 * B * TT // 2 + ONE)

        @block.gpsimd
        def _(pool):
            start(pool, "pool")
            pool.memset(pre[:, :, 0:CONV - 1], 0.0).then_inc(S["pads"], 1)
            pool.memset(expo[:, :], -0.5).then_inc(S["pads"], 1)
            pool.memset(onec[:, :], 1.0).then_inc(S["pads"], 1)
            for c in range(2):
                pool.wait_ge(S["m_r"], c + 1)
                pool.partition_all_reduce(ama[:, c:c + 1], am[:, c:c + 1], P, bass.bass_isa.ReduceOp.max).then_inc(S["m_a"], 1)
            pool.wait_ge(S["pads"], 3)
            pool.wait_ge(S["const"], 16 * 12)

            def hidden(b, ht):
                n = b * HT + ht
                pool.wait_ge(S["r32_r"], n + 1 + ONE)
                settle(pool)
                pool.tensor_scalar(hid[:, 0, ht, :], r32[:, :], 1.0, 1.0, ALU.mult, ALU.mult).then_inc(S["hid_r"], 1)
                pool.wait_ge(S["hid_r"], 2 * n + 1 + ONE)
                pool.tensor_tensor(hid[:, 1, ht, :], r32[:, :], hid[:, 0, ht, :], ALU.subtract).then_inc(S["hid_r"], 1)

            with pool.Fori(0, B) as b:
                pool.wait_ge(S["rs0_r"], b + 1 + ONE)
                pool.tensor_tensor(rs[:, :], rs0[:, :], expo[:, 0:TT], ALU.pow).then_inc(S["rs_r"], 1)
                for m in range(2 * MT):
                    n = b * 2 * MT + m
                    pool.wait_ge(S["sil_r"], b * NM + m + 1 + ONE)
                    pool.wait_ge(S["sq_used"], n + ONE)
                    pool.tensor_tensor(sqf[:, :], sil[:, m, :], sil[:, m, :], ALU.mult).then_inc(S["sq_r"], 1)
                pool.wait_ge(S["v_took"], b * NV + VI["ss",] + 1 + 3 + ONE)
                pool.tensor_tensor(rn[:, :, :].rearrange("p a b -> p (a b)"), ssq[:, :, :].rearrange("p a b -> p (a b)"),
                                   expo[:, :], ALU.pow).then_inc(S["rn_r"], 1)
                for tt in range(TT):
                    w = b * TT + tt
                    pool.wait_ge(S["g_r"], b + 1 + ONE)
                    pool.wait_ge(S["v_full"], b * NV + VI["Y", tt - 1, LV - 1, 1] + 1 + ONE if tt else b * NV + ONE)
                    pool.tensor_tensor(gL, over(after, LH), hb(gg[:, tt, :], P), ALU.mult).then_inc(S["gL_r"], 1)
                    pool.wait_ge(S["a_full"], b * NA + AI["DT", tt - 1, 1] + 1 + ONE if tt else b * NA + ONE)
                    pool.tensor_tensor(gU, over(upto, LH), hb(gg[:, tt, :], P), ALU.mult).then_inc(S["gU_r"], 1)
                    for hf in range(2):
                        pool.wait_ge(S["a_took"], b * NA + AI["DT", tt, hf] + 1 + 3 + ONE)
                        s = slice(hf, LH, 2)
                        pool.tensor_tensor(GT[:, s, :], GT[:, s, :], over(upto, HH), ALU.mult).then_inc(S["GTm_r"], 1)
                    pool.wait_ge(S["v_took"], b * NV + VI["k", tt] + 1 + 3 + ONE)
                    pool.wait_ge(S["v_full"], b * NV + VI["SU", tt - 1] + 1 + ONE if tt else b * NV + ONE)
                    pool.tensor_tensor(heads(Kt), heads(kt_), hb(vec[:, tt, LH:2 * LH], HD), ALU.mult).then_inc(S["Kt_r"], 1)
                    hidden(b, 4 * tt)
                    pool.wait_ge(S["v_took"], b * NV + VI["gate", tt] + 1 + 3 + ONE)
                    pool.tensor_tensor(gt, gt, onw[:, :], ALU.mult).then_inc(S["gw_r"], 1)
                    for i in range(1, 4):
                        hidden(b, 4 * tt + i)
                    pool.wait_ge(S["oss_r"], w * 2 + 2 + ONE)
                    pool.tensor_tensor(os_[:, 2, :], os_[:, 1, :], expo[:, 0:LH], ALU.pow).then_inc(S["orn_r"], 1)

        @block.vector
        def _(v):
            start(v, "dve")
            v.wait_ge(S["w_in"], 16)
            v.tensor_reduce(am[:, 0:1], wst, AX.XY, ALU.max, apply_absolute_value=True).then_inc(S["m_r"], 1)
            v.wait_ge(S["const"], 16 * 12)
            v.tensor_reduce(am[:, 1:2], usn[:, :], AX.X, ALU.max, apply_absolute_value=True).then_inc(S["m_r"], 1)
            v.wait_ge(S["m_a"], 2)
            v.tensor_scalar(ama[:, :], ama[:, :], 1e-30, None, ALU.max).then_inc(S["m_p"], 1)
            v.wait_ge(S["m_p"], 1)
            v.tensor_scalar(pw[:, :].bitcast(I32), ama[:, :].bitcast(I32), 0x7F800000, None, ALU.bitwise_and).then_inc(S["m_p"], 1)
            v.wait_ge(S["m_p"], 2)
            v.reciprocal(ipw[:, :], pw[:, :]).then_inc(S["m_p"], 1)
            v.wait_ge(S["m_p"], 3)
            v.tensor_scalar(ipw[:, 0:1], ipw[:, 0:1], WRAISE, None, ALU.mult).then_inc(S["m_p"], 1)
            v.tensor_scalar(un[:, :], pw[:, 0:1], 1.0 / (WRAISE * XRAISE), None, ALU.mult).then_inc(S["un_r"], 1)
            v.tensor_scalar(unh[:, :], pw[:, 0:1], 0.5 / (WRAISE * XRAISE), None, ALU.mult).then_inc(S["un_r"], 1)
            v.wait_ge(S["un_r"], 2)
            v.tensor_scalar(onw[:, :], onw[:, :], unh[:, 0:1], None, ALU.mult).then_inc(S["onw_r"], 1)
            v.tensor_scalar(usn[:, :], usn[:, :], ipw[:, 1:2], 0.5, ALU.mult, ALU.mult).then_inc(S["usn_r"], 1)
            v.tensor_scalar(dsc[:, :], dsc[:, :], osc[:, 0:1], 2.0 / XRAISE, ALU.mult, ALU.mult).then_inc(S["dsc_r"], 1)
            v.wait_ge(S["dsc_r"], 1)
            v.tensor_scalar(dsc[:, :], dsc[:, :], pw[:, 1:2], None, ALU.mult).then_inc(S["dsc_r"], 1)
            v.wait_ge(S["negA_r"], 1)
            v.tensor_scalar(negA[:, :], negA[:, :], -1.0, None, ALU.mult).then_inc(S["negA_r"], 1)
            v.wait_ge(S["w1h_r"], 1)
            v.scalar_tensor_tensor(w1l.rearrange("p a b -> p (a b)"), wst.rearrange("p a b -> p (a b)"), ipw[:, 0:1],
                                   w1h.rearrange("p a b -> p (a b)"), ALU.mult, ALU.subtract).then_inc(S["w1l_r"], 1)
            v.wait_ge(S["dsc_r"], 2)
            v.wait_ge(S["negA_r"], 2)
            v.wait_ge(S["onw_r"], 1)

            with v.Fori(0, B) as b:
                def take(*key):
                    v.wait_ge(S["v_full"], b * NV + VI[key] + 1 + ONE)
                    return vbank[VI[key] % 3]

                v.wait_ge(S["xb_in"], (b + 1) * 16 + ONE)
                for tt in range(TT):
                    v.bn_stats(st[:, tt, :], xb[:, tt, :]).then_inc(S["st_r"], 1)
                v.wait_ge(S["st_r"], (b + 1) * TT + ONE)
                settle(v)
                for tt in range(TT):
                    v.bn_aggr(mv[:, tt, :], st[:, tt, :]).then_inc(S["mv_r"], 1)
                v.wait_ge(S["mv_r"], (b + 1) * TT + ONE)
                v.tensor_scalar(rs0[:, :], mv[:, :, 1], 1e-5, XRAISE ** -2, ALU.add, ALU.mult).then_inc(S["rs0_r"], 1)
                v.wait_ge(S["rs_r"], b + 1 + ONE)
                for tt in range(TT):
                    v.tensor_scalar(xs[:, tt, :], xb[:, tt, :], mv[:, tt, 0:1], rs[:, tt:tt + 1], ALU.subtract,
                                    ALU.mult).then_inc(S["xs_r"], 1)
                for tt in range(TT):
                    w = b * TT + tt
                    v.wait_ge(S["xs_r"], w + 1 + ONE)
                    v.tensor_copy(xh[:, tt, :], xs[:, tt, :]).then_inc(S["xh_r"], 1)
                for tt in range(TT):
                    w = b * TT + tt
                    v.wait_ge(S["xh_r"], w + 1 + ONE)
                    v.tensor_tensor(xl[:, tt, :], xs[:, tt, :], xh[:, tt, :], ALU.subtract).then_inc(S["xl_r"], 1)

                def conv(m):
                    n = b * NM + m
                    v.wait_ge(S["a_took"], b * NA + AI["pre", m] + 1 + 3 + ONE)
                    v.wait_ge(S["sil_r"], n + ONE)
                    src = pre[:, m % 2, :]
                    v.tensor_scalar(ca[:, :], src[:, 0:T], cw[:, m, 0:1], None, ALU.mult).then_inc(S["conv"], 1)
                    for i in range(1, CONV):
                        v.wait_ge(S["conv"], n * CONV + i + ONE)
                        v.scalar_tensor_tensor(ca[:, :], src[:, i:i + T], cw[:, m, i:i + 1], ca[:, :], ALU.mult,
                                               ALU.add).then_inc(S["conv"], 1)

                def silu(m):
                    n = b * NM + m
                    v.wait_ge(S["tanh_c"], n + 1 + ONE)
                    v.scalar_tensor_tensor(sil[:, m, :], ct[:, :], 1.0, ca[:, :], ALU.add, ALU.mult).then_inc(S["sil_r"], 1)

                conv(0)
                bk = take("bat")
                v.tensor_tensor(z[:, :, :], bk[:, 0:TT * 2 * LH].rearrange("p (t c) -> p t c", t=TT),
                                ab[:, :].rearrange("p (t c) -> p t c", t=1).to_broadcast([P, TT, 2 * LH]),
                                ALU.add).then_inc(S["v_took"], 1)
                v.wait_ge(S["v_took"], b * NV + VI["bat",] + 1 + 3 + ONE)
                v.scalar_tensor_tensor(az, z[:, :, LH:], -1.0, z[:, :, LH:], ALU.mult, ALU.min).then_inc(S["az_r"], 1)
                silu(0)
                for m in range(1, 3):
                    conv(m)
                    silu(m)
                v.wait_ge(S["tb_r"], b + 1 + ONE)
                v.tensor_scalar(beta, tb, 0.5, 0.5, ALU.mult, ALU.add).then_inc(S["beta_r"], 1)
                v.tensor_scalar(bhalf, tb, 0.25, 0.25, ALU.mult, ALU.add).then_inc(S["bhalf_r"], 1)
                v.wait_ge(S["lz_r"], b + 1 + ONE)
                v.scalar_tensor_tensor(spl, z[:, :, LH:], 0.0, lz, ALU.max, ALU.add).then_inc(S["spl_r"], 1)
                v.wait_ge(S["spl_r"], b + 1 + ONE)
                v.tensor_tensor(gg, spl, negA[:, :].rearrange("p (t c) -> p t c", t=1).to_broadcast([P, TT, LH]),
                                ALU.mult).then_inc(S["g_r"], 1)
                for m in range(3, NM):
                    conv(m)
                    silu(m)
                bk = take("ss")[:, 0:TT * 2 * LH].rearrange("p (t c) -> p t c", t=TT)
                v.tensor_scalar(ssq[:, :, 0:LH], bk[:, :, 0:LH], 4e-6, float(HD), ALU.add, ALU.mult)
                v.tensor_scalar(ssq[:, :, LH:], bk[:, :, LH:], 4e-6, None, ALU.add).then_inc(S["v_took"], 1)
                v.wait_ge(S["a_took"], b * NA + AI["vec",] + 1 + 3 + ONE)
                v.wait_ge(S["beta_r"], b + 1 + ONE)
                v.scalar_tensor_tensor(nbg, beta, -1.0, vec[:, :, 0:LH], ALU.mult, ALU.mult).then_inc(S["nbg_r"], 1)
                for p in range(2):
                    v.tensor_copy(gcs[64 * p:64 * p + 64, :, :], vec[64 * p:64 * p + 64, :, 2 * LH + p:3 * LH:2]).then_inc(S["gcs_r"], 1)
                v.memset(S_[:, 0, :, :], 0.0).then_inc(S["S0_r"], 1)
                v.wait_ge(S["rn_r"], b + 1 + ONE)
                v.wait_ge(S["bhalf_r"], b + 1 + ONE)

                for tt in range(TT):
                    w = b * TT + tt
                    if tt:
                        v.wait_ge(S["a_full"], b * NA + AI["qT", tt - 1] + 1 + ONE)
                    v.tensor_tensor(heads(qt_), heads(take("q", tt)[:, 0:KW]), hb(rn[:, tt, 0:LH], HD), ALU.mult).then_inc(S["v_took"], 1)
                    if tt:
                        v.wait_ge(S["Kt_r"], w + ONE)
                    v.tensor_tensor(heads(kt_), heads(take("k", tt)[:, 0:KW]), hb(rn[:, tt, LH:], HD), ALU.mult).then_inc(S["v_took"], 1)
                    v.tensor_tensor(heads(Rv), heads(take("v", tt)[:, 0:KW]), hb(bhalf[:, tt, :], HD), ALU.mult).then_inc(S["v_took"], 1)
                    for hf in range(2):
                        s = slice(hf, LH, 2)
                        v.wait_ge(S["a_took"], b * NA + AI["D", tt, hf] + 1 + 3 + ONE)
                        bk = take("KK", tt, hf)
                        for j in range(HH):
                            hh = hf + 2 * j
                            i = v.scalar_tensor_tensor(A[:, hh, :], bk[:, j * P:(j + 1) * P], beta[:, tt, hh:hh + 1],
                                                       Gm[:, hh, :], ALU.mult, ALU.mult)
                        i.then_inc(S["v_took"], 1)
                        v.wait_ge(S["GTm_r"], w * 2 + hf + 1 + ONE)
                        v.tensor_tensor(BT[:, s, :], take("KQ", tt, hf)[:, 0:HH * P].rearrange("p (h c) -> p h c", h=HH),
                                        GT[:, s, :], ALU.mult).then_inc(S["v_took"], 1)
                        v.wait_ge(S["v_took"], b * NV + VI["KK", tt, hf] + 1 + 3 + ONE)
                        v.tensor_tensor(Tm[:, s, :], A[:, s, :], over(negm[:, 0, :], HH), ALU.mult).then_inc(S["T0_r"], 1)
                        v.wait_ge(S["T0_r"], w * 2 + hf + 1 + ONE)
                        v.tensor_tensor(Tm[:, s, :], Tm[:, s, :], over(ident, HH), ALU.add).then_inc(S["T_r"], 1)
                    v.wait_ge(S["gate_t"], w + 1 + ONE)
                    v.wait_ge(S["y_r"], w + ONE)
                    v.scalar_tensor_tensor(gt, t1, 1.0, take("gate", tt)[:, 0:KW], ALU.add, ALU.mult).then_inc(S["v_took"], 1)
                    for lv in range(1, LV):
                        for hf in range(2):
                            s = slice(hf, LH, 2)
                            v.tensor_tensor(E[:, s, :], take("X", tt, lv, hf)[:, 0:HH * P].rearrange("p (h c) -> p h c", h=HH),
                                            over(negm[:, lv, :], HH), ALU.mult).then_inc(S["v_took"], 1)
                        for hf in range(2):
                            s = slice(hf, LH, 2)
                            v.tensor_tensor(Tm[:, s, :], take("Y", tt, lv, hf)[:, 0:HH * P].rearrange("p (h c) -> p h c", h=HH),
                                            Tm[:, s, :], ALU.add).then_inc(S["v_took"], 1)
                    def every(t, hf):
                        return heads(t)[:, hf:LH:2, :]

                    for hf in range(2):
                        bk = take("S", tt, hf)[:, 0:KW].rearrange("p (i h c) -> p i h c", i=2, h=HH)
                        v.tensor_tensor(every(t1, hf), bk[:, 0], hb(nbg[:, tt, hf:LH:2], HD), ALU.mult).then_inc(S["kS_r"], 1)
                        v.tensor_tensor(every(o1, hf), bk[:, 1], hb(vec[:, tt, hf:LH:2], HD), ALU.mult).then_inc(S["v_took"], 1)
                    v.wait_ge(S["kS_r"], (w + 1) * 2 + ONE)
                    v.tensor_tensor(V2, t1, Rv, ALU.add).then_inc(S["V2_r"], 1)
                    cur, nxt = tt % 2, (tt + 1) % 2
                    v.wait_ge(S["gcs_r"], (b + 1) * 2 + ONE)
                    v.tensor_tensor(ssS[:, :, :], S_[:, cur, :, :], gcs[:, tt, :].rearrange("p (h c) -> p h c", c=1).to_broadcast([P, MT, HD]),
                                    ALU.mult).then_inc(S["ssS_r"], 1)
                    v.wait_ge(S["v_took"], b * NV + VI["S", tt, 1] + 1 + 3 + ONE)
                    v.tensor_tensor(o1, take("O", tt)[:, 0:KW], o1, ALU.add).then_inc(S["v_took"], 1)
                    v.wait_ge(S["ssS_r"], w + 1 + ONE)
                    v.tensor_tensor(S_[:, nxt, :, :], take("SU", tt)[:, 0:MT * HD].rearrange("p (h c) -> p h c", h=MT), ssS[:, :, :],
                                    ALU.add).then_inc(S["v_took"], 1)
                    v.wait_ge(S["osq"], w + 1 + ONE)
                    v.tensor_reduce(os_[:, 0, :], heads(t1), AX.X, ALU.add).then_inc(S["oss_r"], 1)
                    v.wait_ge(S["oss_r"], w * 2 + 1 + ONE)
                    v.tensor_scalar(os_[:, 1, :], os_[:, 0, :], 1.0 / HD, 1e-5, ALU.mult, ALU.add).then_inc(S["oss_r"], 1)
                    v.wait_ge(S["orn_r"], w + 1 + ONE)
                    v.tensor_tensor(heads(o1), heads(o1), hb(os_[:, 2, :], HD), ALU.mult).then_inc(S["or_r"], 1)
                    v.wait_ge(S["or_r"], w + 1 + ONE)
                    v.wait_ge(S["gw_r"], w + 1 + ONE)
                    v.tensor_tensor(o1, o1, gt, ALU.mult).then_inc(S["y_r"], 1)

                for tt in range(TT):
                    w = b * TT + tt
                    v.wait_ge(S["down_full"], w + 1 + ONE)
                    v.wait_ge(S["xo_r"], w + ONE)
                    v.tensor_tensor(fd[:, :], fbank[tt % 2][:, :], dsc[:, :], ALU.mult).then_inc(S["fd_r"], 1)
                    v.wait_ge(S["th_r"], w + 1 + ONE)
                    v.scalar_tensor_tensor(th[:, :], th[:, :], 1.0, fd[:, :], ALU.add, ALU.mult).then_inc(S["g2_r"], 1)
                    v.wait_ge(S["g2_r"], w + 1 + ONE)
                    v.scalar_tensor_tensor(fd[:, :], take("wo", tt)[:, :], 0.5, th[:, :], ALU.mult, ALU.mult).then_inc(S["v_took"], 1)
                    v.wait_ge(S["v_took"], b * NV + VI["wo", tt] + 1 + 3 + ONE)
                    v.wait_ge(S[f"xo_out{tt % 2}"], (b * 2 + tt // 2) * 16 + ONE)
                    v.tensor_tensor(xo[:, tt % 2, :], fd[:, :], xb[:, tt, :], ALU.add).then_inc(S["xo_r"], 1)

        @block.scalar
        def _(a):
            start(a, "act")
            a.wait_ge(S["const"], 16 * 12)
            a.activation(negA[:, :], negA[:, :], ACT.Exp).then_inc(S["negA_r"], 1)
            a.wait_ge(S["m_p"], 4)
            a.activation(w1h, wst, ACT.Copy, scale=ipw[:, 0:1]).then_inc(S["w1h_r"], 1)
            a.wait_ge(S["up_in"], 16)
            a.activation(up[:, :, :], upst, ACT.Sign).then_inc(S["up_r"], 1)
            a.wait_ge(S["dn_in"], 16)
            a.activation(down[:, :, :], dnst, ACT.Sign).then_inc(S["down_r"], 1)
            a.wait_ge(S["pads"], 3)
            a.wait_ge(S["un_r"], 2)
            a.wait_ge(S["usn_r"], 1)

            with a.Fori(0, B) as b:
                def take(*key):
                    a.wait_ge(S["a_full"], b * NA + AI[key] + 1 + ONE)
                    return abank[AI[key] % 3]

                def hidden(ht):
                    n = b * HT + ht
                    a.wait_ge(S["f_full"], n + 1 + ONE)
                    a.wait_ge(S["hid_r"], n * 2 + ONE)
                    a.activation(r32[:, :], fbank[ht % 2][:, :], ACT.Relu, scale=usn[:, ht:ht + 1]).then_inc(S["r32_r"], 1)

                for kt in range(KT):
                    a.activation(xT[:, kt, :, :].rearrange("p a b -> p (a b)"), take("xT", kt)[:, :].bitcast(F16), ACT.Copy).then_inc(S["a_took"], 1)
                a.activation(ba[:, :], take("ba")[0:2 * LH, :], ACT.Copy, scale=un[0:2 * LH, :]).then_inc(S["a_took"], 1)

                def evict_pre(m):
                    n = b * NM + m
                    a.wait_ge(S["conv"], (n - 1) * CONV + ONE if m >= 2 else b * NM * CONV + ONE)
                    a.activation(pre[:, m % 2, CONV - 1:], take("pre", m)[:, :], ACT.Copy, scale=un[:, :]).then_inc(S["a_took"], 1)

                def tanh_conv(m):
                    n = b * NM + m
                    a.wait_ge(S["conv"], (n + 1) * CONV + ONE)
                    a.activation(ct[:, :], ca[:, :], ACT.Tanh, scale=0.5).then_inc(S["tanh_c"], 1)

                evict_pre(0)
                evict_pre(1)
                for m in range(NM):
                    tanh_conv(m)
                    if m + 2 < NM:
                        evict_pre(m + 2)
                    if m == 1:
                        a.wait_ge(S["v_took"], b * NV + VI["bat",] + 1 + 3 + ONE)
                        a.activation(tb, z[:, :, 0:LH], ACT.Tanh, scale=0.5).then_inc(S["tb_r"], 1)
                        a.wait_ge(S["az_r"], b + 1 + ONE)
                        a.activation(ez, az, ACT.Exp).then_inc(S["ez_r"], 1)
                        a.wait_ge(S["ez_r"], b + 1 + ONE)
                        a.activation(lz, ez, ACT.Ln, bias=onec[:, :]).then_inc(S["lz_r"], 1)
                a.activation(vec[:, :, :].rearrange("p a b -> p (a b)"), take("vec")[:, 0:TT * 3 * LH], ACT.Exp).then_inc(S["a_took"], 1)
                for tt in range(TT):
                    w = b * TT + tt
                    for hf in range(2):
                        s = slice(hf, LH, 2)
                        for nm, dst in (("D", Gm), ("DT", GT)):
                            a.activation(dst[:, s, :], take(nm, tt, hf)[:, 0:HH * P].rearrange("p (h c) -> p h c", h=HH), ACT.Exp).then_inc(S["a_took"], 1)
                    a.activation(sil[:, MT:2 * MT, tt * P:(tt + 1) * P], take("kT", tt)[:, 0:KW].rearrange("p (m c) -> p m c", m=MT), ACT.Copy).then_inc(S["a_took"], 1)
                    a.activation(sil[:, 0:MT, tt * P:(tt + 1) * P], take("qT", tt)[:, 0:KW].rearrange("p (m c) -> p m c", m=MT), ACT.Copy).then_inc(S["a_took"], 1)

                    def copy3(dst, hf, *key):
                        s = slice(hf, LH, 2)
                        a.activation(dst[:, s, :], take(*key)[:, 0:HH * P].rearrange("p (h c) -> p h c", h=HH), ACT.Copy).then_inc(S["a_took"], 1)

                    copy3(AT, 0, "AT", tt, 0)
                    copy3(AT, 1, "AT", tt, 1)
                    hidden(4 * tt)
                    a.wait_ge(S["v_full"], b * NV + VI["gate", tt] + 1 + ONE)
                    a.activation(t1, vbank[VI["gate", tt] % 3][:, 0:KW], ACT.Tanh, scale=unh[:, :]).then_inc(S["gate_t"], 1)
                    copy3(TTm, 0, "TT", tt, 0, 0)
                    copy3(TTm, 1, "TT", tt, 0, 1)
                    for lv in range(1, LV):
                        if lv in (1, 3, 5):
                            hidden(4 * tt + 1 + lv // 2)
                        copy3(TTm, 0, "TT", tt, lv, 0)
                        copy3(TTm, 1, "TT", tt, lv, 1)
                    a.activation(U, take("U", tt)[:, 0:KW], ACT.Copy).then_inc(S["a_took"], 1)
                    a.wait_ge(S["v_took"], b * NV + VI["O", tt] + 1 + 3 + ONE)
                    a.activation(t1, o1, ACT.Square).then_inc(S["osq"], 1)
                    a.activation(yT[:, :, tt * P:(tt + 1) * P], take("yT", tt)[:, 0:KW].rearrange("p (m c) -> p m c", m=MT), ACT.Copy).then_inc(S["a_took"], 1)
                for tt in range(TT):
                    w = b * TT + tt
                    a.wait_ge(S["fd_r"], w + 1 + ONE)
                    a.wait_ge(S["v_took"], b * NV + VI["wo", tt - 1] + 1 + 3 + ONE if tt else b * NV + 3 + ONE)
                    a.activation(th[:, :], fd[:, :], ACT.Tanh, scale=0.5).then_inc(S["th_r"], 1)

        @block.tensor
        def _(pe):
            start(pe, "pe")
            start(pe, "pe2")
            pe.wait_ge(S["const"], 16 * 12)
            pe.wait_ge(S["w1l_r"], 1)
            pe.wait_ge(S["down_r"], 1)
            pe.wait_ge(S["up_r"], 1)

            with pe.Fori(0, B) as b:
                def vfill(*key):
                    pe.wait_ge(S["v_took"], b * NV + VI[key] + 1 + ONE)
                    return vbank[VI[key] % 3]

                def afill(*key):
                    pe.wait_ge(S["a_took"], b * NA + AI[key] + 1 + ONE)
                    return abank[AI[key] % 3]

                def three(bk, lhs, rhs):
                    n = 0
                    for kt in range(KT):
                        for i, j in ((0, 0), (0, 1), (1, 0)):
                            mm = pe.matmul(bk, lhs(i, kt), rhs(j, kt), start=n == 0, stop=n == 3 * KT - 1)
                            n += 1
                    return mm

                def x_half(i, kt):
                    return xT[:, kt, i, :]

                def up_tile(ht):
                    n = b * HT + ht
                    if ht >= 2:
                        pe.wait_ge(S["r32_r"], n - 1 + ONE)
                    else:
                        pe.wait_ge(S["fd_r"], b * TT + ONE)
                    for kt in range(KT):
                        for i in range(2):
                            mm = pe.matmul(fbank[ht % 2][:, :], up[:, kt, ht * P:(ht + 1) * P], x_half(i, kt),
                                           start=kt == 0 and i == 0, stop=kt == KT - 1 and i == 1)
                    mm.then_inc(S["f_full"], 1)

                for kt in range(KT):
                    bk = afill("xT", kt)[:, :].bitcast(F16)
                    pe.wait_ge(S["xl_r"], (b + 1) * TT + ONE)
                    for i, t in enumerate((xh, xl)):
                        for tt in range(TT):
                            mm = pe.transpose(bk[:, i * T + tt * P:i * T + (tt + 1) * P], t[:, tt, kt * P:(kt + 1) * P], ident16[:, :])
                    mm.then_inc(S["a_full"], 1)
                bk = afill("ba")
                pe.wait_ge(S["a_took"], b * NA + AI["xT", KT - 1] + 1 + 3 + ONE)
                three(bk[0:2 * LH, :], lambda i, kt: w1[:, i, kt, 4 * KW:NW1], x_half).then_inc(S["a_full"], 1)

                def pre_tile(m):
                    bk = afill("pre", m)
                    three(bk[:, :], lambda i, kt: w1[:, i, kt, m * P:(m + 1) * P], x_half).then_inc(S["a_full"], 1)

                pre_tile(0)
                bk = vfill("bat")
                pe.wait_ge(S["a_took"], b * NA + AI["ba",] + 1 + 3 + ONE)
                for tt in range(TT):
                    mm = pe.matmul(bk[:, tt * 2 * LH:(tt + 1) * 2 * LH], ba[:, tt * P:(tt + 1) * P], ident[0:2 * LH, 0:2 * LH],
                                   start=True, stop=True)
                mm.then_inc(S["v_full"], 1)

                def squares(m):
                    pe.wait_ge(S["sq_r"], b * 2 * MT + m + 1 + ONE)
                    bk = vbank[VI["ss",] % 3]
                    for tt in range(TT):
                        c = tt * 2 * LH + 2 * m
                        mm = pe.matmul(bk[:, c:c + 2], sqf[:, tt * P:(tt + 1) * P], hsel[:, :], start=True, stop=True)
                    mm.then_inc(S["sq_used"], 1)
                    return mm

                for m in range(1, NM):
                    pre_tile(m)
                    if m >= 3:
                        if m == 3:
                            vfill("ss")
                        squares(m - 3)
                pe.wait_ge(S["sq_used"], (b + 1) * 2 * MT + ONE)
                pe.sem_inc(S["v_full"], 1)
                bk = afill("vec")
                pe.wait_ge(S["g_r"], b + 1 + ONE)
                for tt in range(TT):
                    for i, mat in enumerate((upto, after, ones)):
                        c = tt * 3 * LH + i * LH
                        mm = pe.matmul(bk[:, c:c + LH], mat, gg[:, tt, :], start=True, stop=True)
                mm.then_inc(S["a_full"], 1)

                for tt in range(TT):
                    w = b * TT + tt
                    tk = slice(tt * P, (tt + 1) * P)
                    for i, nm in enumerate(("q", "k", "v")):
                        bk = vfill(nm, tt)
                        pe.wait_ge(S["sil_r"], (b + 1) * NM + ONE)
                        for m in range(MT):
                            mm = pe.transpose(bk[:, m * P:(m + 1) * P], sil[:, i * MT + m, tk], ident)
                        mm.then_inc(S["v_full"], 1)
                    for hf in range(2):
                        s = slice(hf, LH, 2)
                        bk = afill("D", tt, hf)
                        pe.wait_ge(S["gL_r"], w + 1 + ONE)
                        pe.matmul(bk[:, 0:HH * P], upto, gL[:, s, :], start=True, stop=True).then_inc(S["a_full"], 1)
                        bk = afill("DT", tt, hf)
                        pe.wait_ge(S["gU_r"], w + 1 + ONE)
                        pe.matmul(bk[:, 0:HH * P], after, gU[:, s, :], start=True, stop=True).then_inc(S["a_full"], 1)
                    for nm, src in (("kT", kt_), ("qT", qt_)):
                        bk = afill(nm, tt)
                        pe.wait_ge(S["v_took"], b * NV + VI["k", tt] + 1 + 3 + ONE)
                        for m in range(MT):
                            mm = pe.transpose(bk[:, m * P:(m + 1) * P], src[:, m * P:(m + 1) * P], ident)
                        mm.then_inc(S["a_full"], 1)

                    def head(base, hh):
                        return sil[64 * (hh % 2):64 * (hh % 2) + 64, base + hh // 2, tk]

                    for hf in range(2):
                        for nm, base in (("KK", MT), ("KQ", 0)):
                            bk = vfill(nm, tt, hf)
                            pe.wait_ge(S["a_took"], b * NA + AI["qT", tt] + 1 + 3 + ONE)
                            for j in range(HH):
                                hh = hf + 2 * j
                                mm = pe.matmul(bk[:, j * P:(j + 1) * P], head(MT, hh), head(base, hh), start=True, stop=True)
                            mm.then_inc(S["v_full"], 1)
                    up_tile(4 * tt)
                    bk = vfill("gate", tt)
                    three(bk[:, 0:KW], lambda i, kt: xT[:, kt, i, tk], lambda j, kt: w1[:, j, kt, 3 * KW:4 * KW]).then_inc(S["v_full"], 1)
                    for hf in range(2):
                        bk = afill("AT", tt, hf)
                        pe.wait_ge(S["v_took"], b * NV + VI["KK", tt, hf] + 1 + 3 + ONE)
                        for j in range(HH):
                            mm = pe.transpose(bk[:, j * P:(j + 1) * P], A[:, hf + 2 * j, :], ident)
                        mm.then_inc(S["a_full"], 1)

                    def turn_T(lv, hf):
                        bk = afill("TT", tt, lv, hf)
                        if lv:
                            pe.wait_ge(S["v_took"], b * NV + VI["Y", tt, lv, hf] + 1 + 3 + ONE)
                        else:
                            pe.wait_ge(S["T_r"], w * 2 + hf + 1 + ONE)
                        for j in range(HH):
                            mm = pe.transpose(bk[:, j * P:(j + 1) * P], Tm[:, hf + 2 * j, :], ident)
                        mm.then_inc(S["a_full"], 1)

                    turn_T(0, 0)
                    turn_T(0, 1)
                    for lv in range(1, LV):
                        for hf in range(2):
                            bk = vfill("X", tt, lv, hf)
                            if lv == 1:
                                pe.wait_ge(S["a_took"], b * NA + AI["AT", tt, hf] + 1 + 3 + ONE)
                            for j in range(HH):
                                hh = hf + 2 * j
                                mm = pe.matmul(bk[:, j * P:(j + 1) * P], AT[:, hh, :], Tm[:, hh, :], start=True, stop=True)
                            mm.then_inc(S["v_full"], 1)
                        if lv in (1, 3, 5):
                            up_tile(4 * tt + 1 + lv // 2)
                        for hf in range(2):
                            bk = vfill("Y", tt, lv, hf)
                            pe.wait_ge(S["a_took"], b * NA + AI["TT", tt, lv - 1, hf] + 1 + 3 + ONE)
                            pe.wait_ge(S["v_took"], b * NV + VI["X", tt, lv, hf] + 1 + 3 + ONE)
                            for j in range(HH):
                                hh = hf + 2 * j
                                mm = pe.matmul(bk[:, j * P:(j + 1) * P], TTm[:, hh, :], E[:, hh, :], start=True, stop=True)
                            mm.then_inc(S["v_full"], 1)
                        for hf in range(2):
                            turn_T(lv, hf)
                    for hf in range(2):
                        bk = vfill("S", tt, hf)
                        if tt:
                            pe.wait_ge(S["v_took"], b * NV + VI["SU", tt - 1] + 1 + 3 + ONE)
                        else:
                            pe.wait_ge(S["S0_r"], b + 1 + ONE)
                        for i, base in enumerate((MT, 0)):
                            for j in range(HH):
                                mm = pe.matmul(bk[:, (i * HH + j) * HD:(i * HH + j + 1) * HD], head(base, hf + 2 * j),
                                               S_[64 * hf:64 * hf + 64, tt % 2, j, :], start=True, stop=True)
                        mm.then_inc(S["v_full"], 1)
                    bk = afill("U", tt)
                    pe.wait_ge(S["a_took"], b * NA + AI["TT", tt, LV - 1, 1] + 1 + 3 + ONE)
                    pe.wait_ge(S["V2_r"], w + 1 + ONE)
                    for hh in range(LH):
                        mm = pe.matmul(bk[:, hh * HD:(hh + 1) * HD], TTm[:, hh, :], V2[:, hh * HD:(hh + 1) * HD], start=True, stop=True)
                    mm.then_inc(S["a_full"], 1)
                    bk = vfill("O", tt)
                    pe.wait_ge(S["a_took"], b * NA + AI["U", tt] + 1 + 3 + ONE)
                    for hh in range(LH):
                        mm = pe.matmul(bk[:, hh * HD:(hh + 1) * HD], BT[:, hh, :], U[:, hh * HD:(hh + 1) * HD], start=True, stop=True)
                    mm.then_inc(S["v_full"], 1)
                    bk = vfill("SU", tt)
                    pe.wait_ge(S["Kt_r"], w + 1 + ONE)
                    for hh in range(LH):
                        q = 64 * (hh % 2)
                        mm = pe.matmul(bk[q:q + 64, (hh // 2) * HD:(hh // 2 + 1) * HD], Kt[:, hh * HD:(hh + 1) * HD],
                                       U[:, hh * HD:(hh + 1) * HD], start=True, stop=True)
                    mm.then_inc(S["v_full"], 1)
                    bk = afill("yT", tt)
                    pe.wait_ge(S["y_r"], w + 1 + ONE)
                    for m in range(MT):
                        mm = pe.transpose(bk[:, m * P:(m + 1) * P], o1[:, m * P:(m + 1) * P], ident)
                    mm.then_inc(S["a_full"], 1)

                for tt in range(TT):
                    w = b * TT + tt
                    if tt < 2:
                        pe.wait_ge(S["r32_r"], (b + 1) * HT + ONE)
                    else:
                        pe.wait_ge(S["fd_r"], w - 1 + ONE)
                    pe.wait_ge(S["hid_r"], (b + 1) * HT * 2 + ONE)
                    for ht in range(HT):
                        for i in range(2):
                            mm = pe.matmul(fbank[tt % 2][:, :], hid[:, i, ht, tt * P:(tt + 1) * P], down[:, ht, :],
                                           start=ht == 0 and i == 0, stop=ht == HT - 1 and i == 1)
                    mm.then_inc(S["down_full"], 1)
                    bk = vfill("wo", tt)
                    pe.wait_ge(S["a_took"], b * NA + AI["yT", TT - 1] + 1 + 3 + ONE)
                    for m in range(MT):
                        mm = pe.matmul(bk[:, :], yT[:, m, tt * P:(tt + 1) * P], wo1[:, m, :], start=m == 0, stop=m == MT - 1)
                    mm.then_inc(S["v_full"], 1)


def host_layout(i):
    import numpy as np
    c = np.ascontiguousarray

    def rows(a):
        return a.reshape(-1, P, a.shape[-1]).transpose(1, 0, 2)

    def cols(a):
        return c(a.reshape(-1, P).T)

    a = {n: np.asarray(v) for n, v in i.items()}
    o = {}
    o["x"] = c(a["L0_attn_x"])
    wq = a["L0_attn_Wq"].reshape(D, NKV, G, DH)
    wk = a["L0_attn_Wk"].reshape(D, NKV, 1, DH)
    q = np.zeros((D, NKV, G, 32), wq.dtype)
    q[..., 0:DH] = wq
    k = np.zeros((D, NKV, G, 32), wk.dtype)
    k[..., 0:DH] = wk
    o["wq"] = c(rows(q.reshape(D, NKV * P)).reshape(P, KT, NKV, P))
    o["wk"] = c(rows(k.reshape(D, NKV * P)).reshape(P, KT, NKV, P))
    o["wv"] = c(rows(a["L0_attn_Wv"]))
    o["wo"] = c(rows(a["L0_attn_Wo"]))
    ug = np.concatenate([a["L0_ffn_W_up"], a["L0_ffn_W_gate"]], 0).T
    o["ug"] = c(rows(ug).reshape(P, KT, NCH, 512).transpose(2, 0, 1, 3))
    o["down"] = c(rows(a["L0_ffn_W_down"].T))
    o["su_ug"] = cols(a["L0_ffn_SU_ug"])
    o["su_dp"] = cols(a["L0_ffn_SU_dp"])
    o["wscale_ug"] = cols(a["L0_ffn_Wscale_ug"])
    o["wscale_dp"] = c(a["L0_ffn_Wscale_dp"])
    w1 = np.concatenate([a[n] for n in ("L1_attn_Wq", "L1_attn_Wk", "L1_attn_Wv", "L1_attn_Wg", "L1_attn_Wb", "L1_attn_Wa")], 0)
    o["w1"] = c(rows(w1.T))
    o["wo1"] = c(rows(a["L1_attn_Wo"].T))
    conv = np.concatenate([a[n] for n in ("L1_attn_conv_q", "L1_attn_conv_k", "L1_attn_conv_v")], 0)
    o["cw"] = c(rows(conv))
    o["upw"] = c(rows(a["L1_ffn_up_weight"].T))
    o["downw"] = c(rows(a["L1_ffn_down_weight"].T))
    o["up_scale"] = cols(a["L1_ffn_up_scale"])
    o["down_scale"] = c(a["L1_ffn_down_scale"])
    o["out_scale"] = c(a["L1_ffn_output_scale"])
    o["onw"] = c(np.tile(a["L1_attn_o_norm_w"], LH))
    o["ab_bias"] = c(np.concatenate([np.zeros(LH, np.float32), a["L1_attn_dt_bias"]]))
    o["a_log"] = c(a["L1_attn_A_log"])
    i, j = np.arange(P)[:, None], np.arange(P)[None, :]
    o["cmat"] = c(np.stack([i == j, i <= j, i > j, i >= 0 * j], 1).astype(np.float32))
    o["negm"] = c(np.stack([-1.0 * ((i >> (lv + 1) == j >> (lv + 1)) & (i >> lv & 1 == 1) & (j >> lv & 1 == 0))
                            for lv in range(LV)], 1).astype(np.float32))
    o["hsel"] = c((np.arange(P)[:, None] // HD == np.arange(2)[None, :]).astype(np.float32))
    o["ident16"] = np.eye(P, dtype=np.float16)
    had = np.array([[1.0]], np.float32)
    while had.shape[0] < P:
        had = np.block([[had, had], [had, -had]])
    o["had"] = c(had.astype(np.float32))
    one = np.zeros((P, 1), np.float32)
    one[DH::32] = 1.0
    o["onecol"] = one
    return o


def kernel(**inputs):
    import numpy as np
    import concourse.bacc as bacc
    from concourse.bass_utils import run_bass_kernel_spmd

    nc = bacc.Bacc("TRN2", target_bir_lowering=False, num_devices=1)
    arrays = host_layout(inputs)
    d = {n: nc.dram_tensor(f"in_{n}", a.shape, mybir.dt.from_np(a.dtype), kind="ExternalInput").ap()
         for n, a in arrays.items()}
    out = nc.dram_tensor("out_x", (B, TT, P, D), F32, kind="ExternalOutput").ap()
    x1 = nc.dram_tensor("x1_scratch", (B, TT, P, D), F32, kind="Internal").ap()
    layer0(nc, d, x1)
    layer1(nc, d, x1, out)
    r = run_bass_kernel_spmd(nc, [{f"in_{n}": a for n, a in arrays.items()}], core_ids=[0])
    return np.asarray(r.results[0]["out_x"]).reshape(B, T, D)
```

```python
import concourse.bass as bass
from concourse import mybir
from contextlib import ExitStack

F32 = mybir.dt.float32
F16 = mybir.dt.float16
I32 = mybir.dt.int32
ALU = mybir.AluOpType
ACT = mybir.ActivationFunctionType
AX = mybir.AxisListType

P = 128
B, T, D = 4, 512, 512
KT = D // P
TT = T // P
NT = B * TT
NH, NKV = 32, 8
G = NH // NKV
DH = D // NH
VW = DH + 1
SC = G * TT
INTER = 2048
FT = INTER // P
UG = 2 * FT
NCH = UG // 4
ONE = 1
RAISE = 16.0


def layer0(nc, d, x1_dram):
    ctx = ExitStack()
    with ctx:
        def sb(name, shape, dt):
            return ctx.enter_context(nc.sbuf_tensor(name, shape, dt))

        def sem(name):
            return ctx.enter_context(nc.semaphore(name))

        bank = [ctx.enter_context(nc.psum_tensor(f"bank{i}", [P, 512], F32)) for i in range(8)]
        SA, SB, OB, GB = bank[0:2], bank[2:4], bank[4], bank[5:8]

        ident = sb("ident", [P, P], F16)
        onecol = sb("onecol", [P, 1], F32)
        epscol = sb("epscol", [P, 1], F32)
        had = sb("had", [P, P], F32)
        wq = sb("wq", [P, KT, NKV, P], F16)
        wk = sb("wk", [P, KT, NKV, P], F16)
        wv = sb("wv", [P, KT, NKV * DH], F16)
        wo = sb("wo", [P, KT, D], F16)
        ug_hi = sb("ug_hi", [P, KT, 2 * INTER], F16)
        ug_lo = sb("ug_lo", [P, KT, 2 * INTER], F16)
        dn = sb("dn", [P, FT, D], F32)
        su_raw = sb("su_raw", [P, KT], F32)
        sud = sb("sud", [P, FT], F32)
        sudn = sb("sudn", [P, FT], F32)
        wsc = sb("wsc", [P, UG], F32)
        wsd = sb("wsd", [P, D], F32)
        amax = sb("amax", [P, 1 + NCH], F32)
        amaxa = sb("amaxa", [P, 1 + NCH], F32)
        powr = sb("powr", [P, 1 + NCH], F32)
        invp = sb("invp", [P, 1 + NCH], F32)
        sun = sb("sun", [P, KT], F32)
        suc = sb("suc", [P, 2, KT], F32)
        usc = sb("usc", [P, UG], F32)
        gsc = sb("gsc", [P, FT], F32)
        hsc = sb("hsc", [P, FT], F32)
        xnT = sb("xnT", [P, KT, B * T], F16)
        st = sb("st", [P, NT, 6], F32)
        mv = sb("mv", [P, NT, 2], F32)
        sd = sb("sd", [P, NT], F32)
        rs = sb("rs", [P, NT], F32)
        h = sb("h", [P, FT, T], F32)
        hflat = h[:, :, :].rearrange("p a b -> p (a b)")
        wbuf = [hflat[:, i * 2048:(i + 1) * 2048].rearrange("p (k n) -> p k n", k=KT) for i in range(2)]
        bfly = hflat[:, 4096:6144].rearrange("p (k n) -> p k n", k=KT)
        bout = hflat[:, 6144:8192].rearrange("p (k n) -> p k n", k=KT)
        q16 = sb("q16", [P, T], F16)
        kA = sb("kA", [P, T], F16)
        qB = sb("qB", [P, T], F16)
        kB = sb("kB", [P, T], F16)
        mS = sb("mS", [P, TT, P], F16)
        probs = sb("probs", [P, 4, T], F16)
        vaug = sb("vaug", [P, TT, NKV, VW], F16)
        rl = sb("rl", [P, SC], F32)
        otok = sb("otok", [P, TT, D], F16)
        oT = sb("oT", [P, KT, T], F16)
        tg = sb("tg", [P, T], F32)
        gs = sb("gs", [P, T], F32)
        fd = sb("fd", [P, 2, D], F32)
        th = sb("th", [P, 2, D], F32)
        xres = sb("xres", [P, 2, D], F16)
        x1 = sb("x1", [P, 2, D], F32)
        dflat = dn[:, :, :].rearrange("p a b -> p (a b)").bitcast(F16).rearrange("p (i t n) -> p i t n", i=2, t=NT)
        x16, xn = dflat[:, 0], dflat[:, 1]

        S = {n: sem(n) for n in (
            "turns", "x_in0", "x_in1", "x_in2", "x_in3", "const_in", "w_in0", "w_in1", "dn_in", "proj_in", "scal_in",
            "stats", "mvr", "sd_ready", "rs_ready", "xn_ready", "xnT_ps", "xnT_ready",
            "amax_ready", "amax_all", "pow_a", "pow_b", "suc_ready", "bf1", "bf2", "ug_ps", "ug_hi_ready", "ug_lo_ready",
            "sc_ready", "dbf", "dn_ps", "dn_ready", "init",
            "q_ps", "k_ps", "q_ready", "k_ready", "sa_ps", "max_done", "mT_ps", "qka_ready",
            "sb_ps", "p_ready", "pv_done", "rl_ready", "o_done", "v_ps", "v_ready",
            "gate_ps", "tanh_ready", "gs_done", "up_ps", "h_ready",
            "oT_ps", "oT_ready", "down_ps", "fd_done", "th_ready", "g2_done", "wo_ps", "y_done", "x1_ready", "x1_out0", "x1_out1", "xres_in0", "xres_in1", "spare_in")}

        def settle(eng):
            eng.sem_inc(S["turns"], 1)

        OWN0 = {
            "pe": ["sa_ps", "sb_ps", "mT_ps"],
            "act": ["oT_ready"],
            "dve": ["qka_ready", "h_ready", "gs_done", "fd_done", "x1_ready", "y_done", "o_done"],
            "sp": ["x1_out0", "x1_out1"],
        }

        def start(eng, who):
            for n in OWN0[who]:
                eng.sem_inc(S[n], ONE)

        block = ctx.enter_context(nc.Block())

        @block.sync
        def _(sp):
            start(sp, "sp")
            for b in range(B):
                sp.dma_start(x16[:, b * TT:(b + 1) * TT, :],
                             d["x"][b].rearrange("(t p) n -> p t n", p=P)).then_inc(S[f"x_in{b}"], 16)
            sp.dma_start(ident[:, :], d["ident16"]).then_inc(S["const_in"], 16)
            sp.dma_start(had[:, :], d["had"]).then_inc(S["const_in"], 16)
            sp.dma_start(onecol[:, :], d["onecol"]).then_inc(S["const_in"], 16)
            sp.dma_start(su_raw[:, :], d["su_ug"]).then_inc(S["scal_in"], 16)
            sp.dma_start(sud[:, :], d["su_dp"]).then_inc(S["scal_in"], 16)
            sp.dma_start(wsc[:, :], d["wscale_ug"]).then_inc(S["scal_in"], 16)
            sp.dma_start(wsd[:, :], d["wscale_dp"].partition_broadcast(P)).then_inc(S["scal_in"], 16)
            def load_down():
                sp.wait_ge(S["xnT_ps"], NT)
                sp.dma_start(dn[:, :, :], d["down"]).then_inc(S["dn_in"], 16)

            for c in range(NCH):
                if c == 4:
                    load_down()
                if c >= 2:
                    sp.wait_ge(S["bf1"], (c - 1) * 2)
                    sp.wait_ge(S["amax_ready"], c)
                sp.dma_start(wbuf[c % 2], d["ug"][c]).then_inc(S[f"w_in{c % 2}"], 16)
            sp.dma_start(wq[:, :, :, :], d["wq"]).then_inc(S["proj_in"], 16)
            sp.dma_start(wk[:, :, :, :], d["wk"]).then_inc(S["proj_in"], 16)
            sp.dma_start(wv[:, :, :], d["wv"]).then_inc(S["proj_in"], 16)
            sp.dma_start(wo[:, :, :], d["wo"]).then_inc(S["proj_in"], 16)
            sp.dma_start(x1_dram[B].rearrange("t p n -> (t p) n"), d["ug"][0].rearrange("p k n -> (p k) n")).then_inc(S["spare_in"], 16)
            with sp.Fori(0, B) as b:
                for tt in range(TT):
                    sp.wait_ge(S["x1_ready"], (b * TT + tt - 1 if tt >= 2 else b * TT) + ONE)
                    settle(sp)
                    sp.dma_start(xres[:, tt % 2, :], d["x"][b, tt * P:(tt + 1) * P, :]).then_inc(S[f"xres_in{tt % 2}"], 16)
                    if tt == 0:
                        continue
                    sp.wait_ge(S["x1_ready"], b * TT + tt + ONE)
                    settle(sp)
                    sp.dma_start(x1_dram[b, tt - 1], x1[:, (tt - 1) % 2, :]).then_inc(S[f"x1_out{(tt - 1) % 2}"], 16)
                sp.wait_ge(S["x1_ready"], b * TT + TT + ONE)
                settle(sp)
                sp.dma_start(x1_dram[b, TT - 1], x1[:, 1, :]).then_inc(S["x1_out1"], 16)
            sp.wait_ge(S["x1_out0"], 16 * NT // 2 + ONE)
            sp.wait_ge(S["x1_out1"], 16 * NT // 2 + ONE)
            sp.wait_ge(S["spare_in"], 16)

        @block.gpsimd
        def _(pool):
            pool.memset(mS[:, :, :], 0.0).then_inc(S["init"], 1)
            pool.memset(vaug[:, :, :, :], 1.0).then_inc(S["init"], 1)
            pool.memset(epscol[:, :], 1e-5).then_inc(S["init"], 1)
            for c in range(1 + NCH):
                pool.wait_ge(S["amax_ready"], c + 1)
                pool.partition_all_reduce(amaxa[:, c:c + 1], amax[:, c:c + 1], P,
                                          bass.bass_isa.ReduceOp.max).then_inc(S["amax_all"], 1)

        @block.vector
        def _(v):
            start(v, "dve")
            for tt in range(NT):
                if tt % TT == 0:
                    v.wait_ge(S[f"x_in{tt // TT}"], 16)
                v.bn_stats(st[:, tt, :], x16[:, tt, :]).then_inc(S["stats"], 1)
            for tt in range(NT):
                v.wait_ge(S["stats"], tt + 1)
                v.bn_aggr(mv[:, tt, :], st[:, tt, :]).then_inc(S["mvr"], 1)
            v.wait_ge(S["sd_ready"], 1)
            v.reciprocal(rs[:, :], sd[:, :]).then_inc(S["rs_ready"], 1)
            v.wait_ge(S["rs_ready"], 1)
            for tt in range(NT):
                v.tensor_scalar(xn[:, tt, :], x16[:, tt, :], mv[:, tt, 0:1], rs[:, tt:tt + 1],
                                ALU.subtract, ALU.mult).then_inc(S["xn_ready"], 1)
            v.wait_ge(S["scal_in"], 16 * 4)

            def power_of_two(c):
                v.wait_ge(S["amax_all"], c + 1)
                v.tensor_scalar(amaxa[:, c:c + 1], amaxa[:, c:c + 1], 1e-30, None, ALU.max).then_inc(S["pow_a"], 1)
                v.wait_ge(S["pow_a"], 3 * c + 1)
                v.tensor_scalar(powr[:, c:c + 1].bitcast(I32), amaxa[:, c:c + 1].bitcast(I32), 0x7F800000, None,
                                ALU.bitwise_and).then_inc(S["pow_a"], 1)
                v.wait_ge(S["pow_a"], 3 * c + 2)
                v.reciprocal(invp[:, c:c + 1], powr[:, c:c + 1]).then_inc(S["pow_a"], 1)
                v.wait_ge(S["pow_a"], 3 * c + 3)

            v.tensor_reduce(amax[:, 0:1], su_raw[:, :], AX.X, ALU.max,
                            apply_absolute_value=True).then_inc(S["amax_ready"], 1)
            power_of_two(0)
            v.tensor_scalar(sun[:, :], su_raw[:, :], invp[:, 0:1], RAISE, ALU.mult, ALU.mult).then_inc(S["pow_b"], 1)
            v.tensor_scalar(sudn[:, :], sud[:, :], float(INTER) ** -0.5, None, ALU.mult).then_inc(S["sc_ready"], 1)
            v.wait_ge(S["pow_b"], 1)
            def low_halves(c):
                for kt in range(KT):
                    n = KT * c + kt
                    v.wait_ge(S["ug_hi_ready"], n + 1)
                    v.scalar_tensor_tensor(ug_lo[:, kt, c * 512:(c + 1) * 512], bank[n % 4][:, :],
                                           suc[:, c % 2, kt:kt + 1], ug_hi[:, kt, c * 512:(c + 1) * 512],
                                           ALU.mult, ALU.subtract).then_inc(S["ug_lo_ready"], 1)

            for c in range(NCH):
                par = c % 2
                w = wbuf[par]
                v.wait_ge(S[f"w_in{par}"], 16 * (c // 2 + 1))
                v.tensor_reduce(amax[:, 1 + c:2 + c], w, AX.XY, ALU.max,
                                apply_absolute_value=True).then_inc(S["amax_ready"], 1)
                if c:
                    v.wait_ge(S["bf2"], 2 * c)
                wp = w.rearrange("p (a s) n -> p a s n", s=2)
                tp = bfly.rearrange("p (a s) n -> p a s n", s=2)
                v.tensor_tensor(tp[:, :, 0, :], wp[:, :, 0, :], wp[:, :, 1, :], ALU.add).then_inc(S["bf1"], 1)
                v.tensor_tensor(tp[:, :, 1, :], wp[:, :, 0, :], wp[:, :, 1, :], ALU.subtract).then_inc(S["bf1"], 1)
                if c:
                    low_halves(c - 1)
                    v.wait_ge(S["ug_ps"], KT * c)
                v.wait_ge(S["bf1"], 2 * (c + 1))
                v.tensor_tensor(bout[:, 0:2, :], bfly[:, 0:2, :], bfly[:, 2:4, :], ALU.add).then_inc(S["bf2"], 1)
                v.tensor_tensor(bout[:, 2:4, :], bfly[:, 0:2, :], bfly[:, 2:4, :], ALU.subtract).then_inc(S["bf2"], 1)
                power_of_two(c + 1)
                if c > 1:
                    v.wait_ge(S["ug_hi_ready"], KT * (c - 1))
                    v.wait_ge(S["ug_lo_ready"], KT * (c - 1))
                v.tensor_scalar(suc[:, par, :], sun[:, :], invp[:, c + 1:c + 2], None, ALU.mult).then_inc(S["suc_ready"], 1)
                v.tensor_scalar(usc[:, 4 * c:4 * c + 4], wsc[:, 4 * c:4 * c + 4], powr[:, c + 1:c + 2],
                                float(D) ** -0.5 / RAISE, ALU.mult, ALU.mult).then_inc(S["sc_ready"], 1)
                v.wait_ge(S["sc_ready"], 2 * c + 2)
                v.wait_ge(S["suc_ready"], c + 1)
                v.tensor_scalar(usc[:, 4 * c:4 * c + 4], usc[:, 4 * c:4 * c + 4], powr[:, 0:1],
                                None, ALU.mult).then_inc(S["sc_ready"], 1)
            low_halves(NCH - 1)
            v.wait_ge(S["sc_ready"], 2 * NCH + 1)
            v.tensor_scalar(gsc[:, :], usc[:, FT:UG], 0.5, None, ALU.mult).then_inc(S["sc_ready"], 1)
            v.scalar_tensor_tensor(hsc[:, :], usc[:, 0:FT], 0.5, usc[:, FT:UG], ALU.mult, ALU.mult).then_inc(S["sc_ready"], 1)
            v.wait_ge(S["dn_in"], 16)
            v.wait_ge(S["xnT_ps"], NT)
            v.wait_ge(S["ug_ps"], KT * NCH)
            src, dst = dn, h
            for lv in range(3):
                a = src[:, :, :].rearrange("p (a s c) n -> p a s (c n)", s=2, c=1 << lv)
                o = dst[:, :, :].rearrange("p (a s c) n -> p a s (c n)", s=2, c=1 << lv)
                if lv:
                    v.wait_ge(S["dbf"], 2 * lv)
                v.tensor_tensor(o[:, :, 0, :], a[:, :, 0, :], a[:, :, 1, :], ALU.add).then_inc(S["dbf"], 1)
                v.tensor_tensor(o[:, :, 1, :], a[:, :, 0, :], a[:, :, 1, :], ALU.subtract).then_inc(S["dbf"], 1)
                src, dst = dst, src
            v.wait_ge(S["dbf"], 6)
            for i in range(0, FT // 2, 2):
                lo, hi = slice(i, i + 2), slice(i + FT // 2, i + FT // 2 + 2)
                v.tensor_tensor(dn[:, lo, :], h[:, lo, :], h[:, hi, :], ALU.add).then_inc(S["dbf"], 1)
                v.tensor_tensor(dn[:, hi, :], h[:, lo, :], h[:, hi, :], ALU.subtract).then_inc(S["dbf"], 1)
            v.sem_inc(S["max_done"], 2)

            def row_max(un, i):
                v.wait_ge(S["sa_ps"], un * SC + i + 1 + ONE)
                qt, j = divmod(i, G)
                v.tensor_reduce(mS[:, qt, 32 * j + DH:32 * j + DH + 1], SA[i % 2][:, :], AX.X,
                                ALU.max).then_inc(S["max_done"], 1)

            def k_copy(un):
                v.wait_ge(S["k_ready"], un + 1)
                v.wait_ge(S["sb_ps"], un * SC + ONE)
                v.tensor_copy(kB[:, :], kA[:, :]).then_inc(S["qka_ready"], 1)

            def q_aug(un):
                v.wait_ge(S["mT_ps"], un + 1 + ONE)
                v.tensor_tensor(qB[:, :], q16[:, :], GB[0][:, :].bitcast(F16)[:, 0:T],
                                ALU.subtract).then_inc(S["qka_ready"], 1)

            def gate_mul(u, t):
                v.wait_ge(S["tanh_ready"], u * 2 + t + 1)
                v.wait_ge(S["h_ready"], u * 2 + t + ONE)
                v.scalar_tensor_tensor(gs[:, :], tg[:, :], 1.0, GB[2 - t][:, :],
                                       ALU.add, ALU.mult).then_inc(S["gs_done"], 1)

            def up_mul(u, g, t):
                v.wait_ge(S["gs_done"], u * 2 + t + 1 + ONE)
                v.wait_ge(S["up_ps"], u * 2 + t + 1)
                ft = g * 2 + t
                v.scalar_tensor_tensor(h[:, ft, :], GB[2 * t][:, :], hsc[:, ft:ft + 1] if isinstance(ft, int) else hsc[:, bass.ds(ft, 1)],
                                       gs[:, :], ALU.mult, ALU.mult).then_inc(S["h_ready"], 1)

            def normalise(u, g):
                v.wait_ge(S["pv_done"], u * SC + SC + 4)
                v.wait_ge(S["o_done"], u + ONE)
                ob = OB[:, 0:SC * VW].rearrange("p (t j c) -> p t j c", t=TT, j=G)
                v.reciprocal(rl[:, :].rearrange("p (t j c) -> p t j c", t=TT, c=1),
                             ob[:, :, :, DH:VW]).then_inc(S["rl_ready"], 1)
                v.wait_ge(S["rl_ready"], u + 1)
                v.tensor_tensor(otok[:, :, bass.ds(g * (G * DH), G * DH)].rearrange("p t (j c) -> p t j c", j=G),
                                ob[:, :, :, 0:DH],
                                rl[:, :].rearrange("p (t j c) -> p t j c", t=TT, c=1).to_broadcast([P, TT, G, DH]),
                                ALU.mult).then_inc(S["o_done"], 1)

            v.wait_ge(S["init"], 3)
            v.wait_ge(S["dn_ready"], FT)
            v.wait_ge(S["sc_ready"], 2 * NCH + 3)
            with v.Fori(0, B) as b:
                for i in range(SC):
                    if i == 0:
                        v.wait_ge(S["mT_ps"], b * NKV + ONE)
                    row_max(b * NKV, i)
                k_copy(b * NKV)
                q_aug(b * NKV)
                with v.Fori(0, NKV - 1) as g:
                    u = b * NKV + g
                    for i in range(SC):
                        if i == 0:
                            v.wait_ge(S["mT_ps"], u + 1 + ONE)
                        row_max(u + 1, i)
                        if i == 2:
                            gate_mul(u, 0)
                        if i == 9:
                            up_mul(u, g, 0)
                    k_copy(u + 1)
                    q_aug(u + 1)
                    gate_mul(u, 1)
                    normalise(u, g)
                    up_mul(u, g, 1)
                u = b * NKV + (NKV - 1)
                gate_mul(u, 0)
                up_mul(u, NKV - 1, 0)
                gate_mul(u, 1)
                up_mul(u, NKV - 1, 1)
                normalise(u, NKV - 1)
                for tt in range(TT):
                    n = b * TT + tt
                    v.wait_ge(S["down_ps"], n + 1)
                    v.wait_ge(S["x1_ready"], (n - 1 if tt >= 2 else b * TT) + ONE)
                    v.tensor_tensor(fd[:, tt % 2, :], GB[1 + tt % 2][:, :], wsd[:, :], ALU.mult).then_inc(S["fd_done"], 1)
                    v.wait_ge(S["th_ready"], n + 1)
                    v.scalar_tensor_tensor(th[:, tt % 2, :], th[:, tt % 2, :], 1.0, fd[:, tt % 2, :],
                                           ALU.add, ALU.mult).then_inc(S["g2_done"], 1)
                    v.wait_ge(S["g2_done"], n + 1)
                    v.wait_ge(S["wo_ps"], n + 1)
                    v.scalar_tensor_tensor(fd[:, tt % 2, :], SA[tt % 2][:, :], 0.5, th[:, tt % 2, :],
                                           ALU.mult, ALU.mult).then_inc(S["y_done"], 1)
                    v.wait_ge(S["y_done"], n + 1 + ONE)
                    v.wait_ge(S[f"x1_out{tt % 2}"], (b * 2 + tt // 2) * 16 + ONE)
                    v.wait_ge(S[f"xres_in{tt % 2}"], (b * 2 + tt // 2 + 1) * 16)
                    v.tensor_tensor(x1[:, tt % 2, :], fd[:, tt % 2, :], xres[:, tt % 2, :], ALU.add).then_inc(S["x1_ready"], 1)

        @block.scalar
        def _(a):
            start(a, "act")
            a.wait_ge(S["init"], 3)
            a.wait_ge(S["mvr"], NT)
            a.activation(sd[:, :], mv[:, :, 1], ACT.Sqrt, bias=epscol[:, :]).then_inc(S["sd_ready"], 1)
            for b in range(B):
                for kt in range(KT):
                    n = b * KT + kt
                    a.wait_ge(S["xnT_ps"], n + 1)
                    a.activation(xnT[:, kt, b * T:(b + 1) * T], bank[4 + n % 4][:, :].bitcast(F16)[:, 0:T],
                                 ACT.Copy).then_inc(S["xnT_ready"], 1)
            for c in range(NCH):
                a.wait_ge(S["suc_ready"], c + 1)
                for kt in range(KT):
                    n = KT * c + kt
                    a.wait_ge(S["ug_ps"], n + 1)
                    a.activation(ug_hi[:, kt, c * 512:(c + 1) * 512], bank[n % 4][:, :], ACT.Copy,
                                 scale=suc[:, c % 2, kt:kt + 1]).then_inc(S["ug_hi_ready"], 1)
            a.wait_ge(S["sc_ready"], 1)
            for n in range(FT):
                q, r = divmod(n, 4)
                ft = 2 * q + r % 2 + (FT // 2) * (r // 2)
                a.wait_ge(S["dn_ps"], n + 1)
                a.activation(dn[:, ft, :], bank[4 + n % 4][:, :], ACT.Copy,
                             scale=sudn[:, ft:ft + 1]).then_inc(S["dn_ready"], 1)
            a.sem_inc(S["p_ready"], 2)
            a.wait_ge(S["const_in"], 48)
            a.wait_ge(S["sc_ready"], 2 * NCH + 3)

            def projections(un):
                a.wait_ge(S["q_ps"], un + 1)
                a.wait_ge(S["sa_ps"], un * SC + ONE)
                a.wait_ge(S["qka_ready"], un * 2 + ONE)
                a.activation(q16[:, :], GB[0][:, :], ACT.Copy).then_inc(S["q_ready"], 1)
                a.wait_ge(S["k_ps"], un + 1)
                a.activation(kA[:, :], GB[1][:, :], ACT.Identity, bias=onecol[:, :]).then_inc(S["k_ready"], 1)

            def exps(u, i):
                a.wait_ge(S["sb_ps"], u * SC + i + 1 + ONE)
                a.wait_ge(S["pv_done"], u * SC + i + 1)
                a.activation(probs[:, i % 4, :], SB[i % 2][:, :], ACT.Exp,
                             scale=float(DH) ** -0.5).then_inc(S["p_ready"], 1)

            def tanh_gate(u, g, t):
                a.wait_ge(S["gate_ps"], u * 2 + t + 1)
                a.wait_ge(S["gs_done"], u * 2 + t + ONE)
                ft = g * 2 + t
                a.activation(tg[:, :], GB[2 - t][:, :], ACT.Tanh,
                             scale=gsc[:, ft:ft + 1] if isinstance(ft, int) else gsc[:, bass.ds(ft, 1)]).then_inc(S["tanh_ready"], 1)

            with a.Fori(0, B) as b:
                a.wait_ge(S["v_ps"], b + 1)
                a.activation(vaug[:, :, :, 0:DH],
                             OB[:, :].rearrange("p (t g c) -> p t g c", t=TT, g=NKV), ACT.Copy).then_inc(S["v_ready"], 1)
                projections(b * NKV)
                with a.Fori(0, NKV - 1) as g:
                    u = b * NKV + g
                    projections(u + 1)
                    for i in range(SC):
                        exps(u, i)
                        if i == 1:
                            tanh_gate(u, g, 0)
                    tanh_gate(u, g, 1)
                u = b * NKV + (NKV - 1)
                for i in range(SC):
                    exps(u, i)
                    if i == 1:
                        tanh_gate(u, NKV - 1, 0)
                tanh_gate(u, NKV - 1, 1)
                for kt in range(KT):
                    a.wait_ge(S["oT_ps"], b * KT + kt + 1)
                    a.activation(oT[:, kt, :], SB[kt % 2][:, :].bitcast(F16)[:, 0:T], ACT.Copy).then_inc(S["oT_ready"], 1)
                for tt in range(TT):
                    n = b * TT + tt
                    a.wait_ge(S["fd_done"], n + 1 + ONE)
                    a.wait_ge(S["y_done"], ((n - 1) if tt >= 2 else b * TT) + ONE)
                    a.activation(th[:, tt % 2, :], fd[:, tt % 2, :], ACT.Tanh, scale=0.5).then_inc(S["th_ready"], 1)

        @block.tensor
        def _(pe):
            start(pe, "pe")
            pe.wait_ge(S["const_in"], 48)
            for b in range(B):
                pe.wait_ge(S["xn_ready"], (b + 1) * TT)
                for kt in range(KT):
                    n = b * KT + kt
                    if n >= 4:
                        pe.wait_ge(S["xnT_ready"], n - 3)
                    bk = bank[4 + n % 4][:, :].bitcast(F16)
                    for tt in range(TT):
                        mm = pe.transpose(bk[:, tt * P:(tt + 1) * P], xn[:, b * TT + tt, kt * P:(kt + 1) * P], ident[:, :])
                    mm.then_inc(S["xnT_ps"], 1)
            for c in range(NCH):
                pe.wait_ge(S["bf2"], 2 * (c + 1))
                for kt in range(KT):
                    n = KT * c + kt
                    if n >= 4:
                        pe.wait_ge(S["ug_lo_ready"], n - 3)
                    pe.matmul(bank[n % 4][:, :], had[:, :], bout[:, kt, :], start=True, stop=True).then_inc(S["ug_ps"], 1)
            pe.wait_ge(S["xnT_ready"], NT)
            for n in range(FT):
                q, r = divmod(n, 4)
                ft = 2 * q + r % 2 + (FT // 2) * (r // 2)
                pe.wait_ge(S["dbf"], 6 + 2 * q + 1 + r // 2)
                if n >= 4:
                    pe.wait_ge(S["dn_ready"], n - 3)
                pe.matmul(bank[4 + n % 4][:, :], had[:, :], dn[:, ft, :], start=True, stop=True).then_inc(S["dn_ps"], 1)
            pe.wait_ge(S["proj_in"], 64)
            pe.wait_ge(S["dn_ready"], FT)
            pe.wait_ge(S["ug_lo_ready"], KT * NCH)
            pe.sem_inc(S["pv_done"], 4)

            def xnb(b, kt):
                return xnT[:, kt, bass.ds(b * T, T)]

            def projections(un, b, g):
                first = isinstance(g, int)
                pe.wait_ge(S["qka_ready"], un * 2 + ONE)
                if first:
                    pe.wait_ge(S["h_ready"], un * 2 + ONE)
                for kt in range(KT):
                    mm = pe.matmul(GB[0][:, :], wq[:, kt, g, :] if first else wq[:, kt, bass.ds(g, 1), :], xnb(b, kt),
                                   start=kt == 0, stop=kt == KT - 1)
                mm.then_inc(S["q_ps"], 1)
                if first:
                    pe.wait_ge(S["fd_done"], b * TT + ONE)
                else:
                    pe.wait_ge(S["gs_done"], (un - 1) * 2 + ONE)
                    pe.wait_ge(S["k_ready"], un)
                for kt in range(KT):
                    mm = pe.matmul(GB[1][:, :], wk[:, kt, g, :] if first else wk[:, kt, bass.ds(g, 1), :], xnb(b, kt),
                                   start=kt == 0, stop=kt == KT - 1)
                mm.then_inc(S["k_ps"], 1)

            def score_a(un, i):
                qt, j = divmod(i, G)
                pe.wait_ge(S["max_done"], un * SC + i + 1)
                pe.matmul(SA[i % 2][:, :], q16[32 * j:32 * j + 32, qt * P:(qt + 1) * P],
                          kA[32 * j:32 * j + 32, :], start=True, stop=True).then_inc(S["sa_ps"], 1)

            def maxima(un, first):
                pe.wait_ge(S["max_done"], un * SC + SC + 2)
                if first:
                    pe.wait_ge(S["q_ready"], un + 1)
                else:
                    pe.wait_ge(S["h_ready"], un * 2 - 1 + ONE)
                bk = GB[0][:, :].bitcast(F16)
                for qt in range(TT):
                    mm = pe.transpose(bk[:, qt * P:(qt + 1) * P], mS[:, qt, :], ident[:, :])
                mm.then_inc(S["mT_ps"], 1)

            def score_b(u, i):
                kt, j = divmod(i, G)
                pe.wait_ge(S["p_ready"], u * SC + i + 1)
                pe.matmul(SB[i % 2][:, :], kB[32 * j:32 * j + 32, kt * P:(kt + 1) * P],
                          qB[32 * j:32 * j + 32, :], start=True, stop=True).then_inc(S["sb_ps"], 1)

            def weigh(u, g, i):
                kt, j = divmod(i, G)
                pe.wait_ge(S["p_ready"], u * SC + i + 3)
                for qt in range(TT):
                    c = (qt * G + j) * VW
                    mm = pe.matmul(OB[:, c:c + VW], probs[:, i % 4, qt * P:(qt + 1) * P],
                                   vaug[:, kt, g, :] if isinstance(g, int) else vaug[:, kt, bass.ds(g, 1), :],
                                   start=i == 0 and qt == 0, stop=i == SC - 1 and qt == TT - 1, skip_group_check=True)
                mm.then_inc(S["pv_done"], 1)

            def ffn_mm(u, b, g, n, last):
                grp, r = divmod(n, 8)
                t, up = divmod(grp, 2)
                bk = GB[2 * t] if up else GB[2 - t]
                if r == 0:
                    if grp == 0:
                        pe.wait_ge(S["h_ready"], u * 2 + ONE)
                        pe.wait_ge(S["fd_done"], b * TT + ONE)
                    if grp == 1:
                        pe.wait_ge(S["qka_ready"], u * 2 + 2 + ONE)
                        if not last:
                            pe.wait_ge(S["q_ready"], u + 2)
                    if grp == 2:
                        pe.wait_ge(S["gs_done"], u * 2 + ONE)
                        if not last:
                            pe.wait_ge(S["k_ready"], u + 2)
                    if grp == 3:
                        pe.wait_ge(S["gs_done"], u * 2 + 1 + ONE)
                kt, part = divmod(r, 2)
                w = (ug_hi, ug_lo)[part]
                col = (g * 2 + t) * P + (0 if up else INTER)
                mm = pe.matmul(bk[:, :], w[:, kt, bass.ds(col, P)], xnb(b, kt), start=r == 0, stop=r == 7)
                if r == 7:
                    mm.then_inc(S["up_ps" if up else "gate_ps"], 1)

            with pe.Fori(0, B) as b:
                pe.wait_ge(S["o_done"], b * NKV + ONE)
                for tt in range(TT):
                    for kt in range(KT):
                        mm = pe.matmul(OB[:, tt * P:(tt + 1) * P], xnT[:, kt, bass.ds(b * T + tt * P, P)],
                                       wv[:, kt, :], start=kt == 0, stop=kt == KT - 1)
                mm.then_inc(S["v_ps"], 1)
                u0 = b * NKV
                projections(u0, b, 0)
                pe.wait_ge(S["q_ready"], u0 + 1)
                pe.wait_ge(S["k_ready"], u0 + 1)
                pe.wait_ge(S["y_done"], b * TT + ONE)
                for i in range(SC):
                    score_a(u0, i)
                maxima(u0, True)
                pe.wait_ge(S["v_ready"], b + 1)
                pe.wait_ge(S["oT_ready"], b * KT + ONE)
                settle(pe)
                with pe.Fori(0, NKV - 1) as g:
                    u = b * NKV + g
                    projections(u + 1, b, g + 1)
                    for n in range(8):
                        ffn_mm(u, b, g, n, False)
                    pe.wait_ge(S["qka_ready"], u * 2 + 2 + ONE)
                    for i in range(SC):
                        if i == 0:
                            pe.wait_ge(S["q_ready"], u + 2)
                            pe.wait_ge(S["k_ready"], u + 2)
                        score_a(u + 1, i)
                        score_b(u, i)
                        if i == 2:
                            pe.wait_ge(S["o_done"], u + ONE)
                        if i >= 2:
                            weigh(u, g, i - 2)
                        ffn_mm(u, b, g, 8 + i, False)
                    weigh(u, g, SC - 2)
                    weigh(u, g, SC - 1)
                    maxima(u + 1, False)
                    for n in range(24, 32):
                        ffn_mm(u, b, g, n, False)
                u, g = b * NKV + (NKV - 1), NKV - 1
                for n in range(8):
                    ffn_mm(u, b, g, n, True)
                pe.wait_ge(S["qka_ready"], u * 2 + 2 + ONE)
                for i in range(SC):
                    score_b(u, i)
                    if i == 2:
                        pe.wait_ge(S["o_done"], u + ONE)
                    if i >= 2:
                        weigh(u, g, i - 2)
                    ffn_mm(u, b, g, 8 + i, True)
                weigh(u, g, SC - 2)
                weigh(u, g, SC - 1)
                for n in range(24, 32):
                    ffn_mm(u, b, g, n, True)

                def down(tt):
                    bk = GB[1 + tt % 2]
                    if tt == 0:
                        pe.wait_ge(S["gs_done"], u * 2 + 2 + ONE)
                        pe.wait_ge(S["h_ready"], u * 2 + 2 + ONE)
                    if tt >= 2:
                        pe.wait_ge(S["fd_done"], b * TT + tt - 1 + ONE)
                    for ft in range(FT):
                        mm = pe.matmul(bk[:, :], h[:, ft, tt * P:(tt + 1) * P], dn[:, ft, :],
                                       start=ft == 0, stop=ft == FT - 1)
                    mm.then_inc(S["down_ps"], 1)

                def turn(kt):
                    if kt == 0:
                        pe.wait_ge(S["o_done"], u + 1 + ONE)
                        pe.wait_ge(S["p_ready"], u * SC + SC + 2)
                    if kt >= 2:
                        pe.wait_ge(S["oT_ready"], b * KT + kt - 1 + ONE)
                    bk = SB[kt % 2][:, :].bitcast(F16)
                    for qt in range(TT):
                        mm = pe.transpose(bk[:, qt * P:(qt + 1) * P], otok[:, qt, kt * P:(kt + 1) * P], ident[:, :])
                    mm.then_inc(S["oT_ps"], 1)

                def project(tt):
                    if tt == 0:
                        pe.wait_ge(S["oT_ready"], b * KT + KT + ONE)
                        pe.wait_ge(S["max_done"], u * SC + SC + 2)
                    if tt >= 2:
                        pe.wait_ge(S["y_done"], b * TT + tt - 1 + ONE)
                    for kt in range(KT):
                        mm = pe.matmul(SA[tt % 2][:, :], oT[:, kt, tt * P:(tt + 1) * P], wo[:, kt, :],
                                       start=kt == 0, stop=kt == KT - 1)
                    mm.then_inc(S["wo_ps"], 1)

                down(0)
                turn(0)
                turn(1)
                down(1)
                turn(2)
                turn(3)
                project(0)
                down(2)
                project(1)
                down(3)
                project(2)
                project(3)


HD = 64
LH = 6
KW = LH * HD
MT = KW // P
NM = 3 * MT
HH = 3
NW1 = 4 * KW + 2 * LH
CONV = 4
BS = 16
NB = P // BS
LEVELS = (4, 5, 6)
SYS = LH * NB
ORDER = (3, 4, 5, 0, 1, 2, 6, 7, 8)
UP_HEAD = 2
UP_EARLY = 3
UP_MID = 11
TURNS = ((), (0,), (1,), (2, 3))
UP_STEP = (0, 1, 1, 1, 0)
HT = 2048 // P
XRAISE, WRAISE = 64.0, 128.0


def bank_order():
    v = [("bat",), ("ss",)]
    a = [("ba",)] + [("pre", m) for m in range(NM - 2)] + [("vec",)]
    for tt in range(TT):
        a += [("DT", tt, 0), ("DT", tt, 1)]
        a += [("pre", NM - 2 + tt)] if tt < 2 else []
        a += [("sT",)] if tt == 1 else []
        v += [("KK", tt, 0), ("KK", tt, 1), ("KQ", tt, 0), ("KQ", tt, 1)]
    for tt in range(TT + 1):
        inv, rec = tt < TT, tt > 0
        v += inv * [("X", tt, 4, 0), ("X", tt, 4, 1)]
        v += rec * [("k", tt - 1), ("v", tt - 1), ("S", tt - 1, 0), ("S", tt - 1, 1)]
        v += inv * [("Y", tt, 4, 0), ("Y", tt, 4, 1)]
        v += rec * [("gate", tt - 1)]
        a += (tt > 1) * [("yT", tt - 2)]
        a += inv * [("TT", tt, 4, 0), ("TT", tt, 4, 1)]
        a += rec * [("U", tt - 1)]
        v += inv * [("X", tt, 5, 0), ("X", tt, 5, 1), ("Y", tt, 5, 0), ("Y", tt, 5, 1)]
        v += rec * [("O", tt - 1)]
        a += inv * [("TT", tt, 5, 0), ("TT", tt, 5, 1)]
        v += inv * [("X", tt, 6, 0), ("X", tt, 6, 1)]
        v += rec * [("SU", tt - 1)]
        v += inv * [("Z", tt, 0), ("Z", tt, 1)]
    v += [("wo", tt) for tt in range(TT)]
    v += [("spare", i) for i in range(-len(v) % 3)]
    a += [("yT", TT - 1)] + [("xT", k) for k in range(KT)]
    assert len(a) % 3 == 0
    return {k: n for n, k in enumerate(v)}, {k: n + KT for n, k in enumerate(a)}


def layer1(nc, d, x1_dram, lt_dram, s_dram, t_dram, out_dram):
    VI, AI = bank_order()
    NV, NA = len(VI), len(AI)
    ctx = ExitStack()
    with ctx:
        def sb(name, shape, dt=F32):
            return ctx.enter_context(nc.sbuf_tensor(name, shape, dt))

        def sem(name):
            return ctx.enter_context(nc.semaphore(name))

        vbank = [ctx.enter_context(nc.psum_tensor(f"vbank{i}", [P, 512], F32)) for i in range(3)]
        abank = [ctx.enter_context(nc.psum_tensor(f"abank{i}", [P, 512], F32)) for i in range(3)]
        fbank = [ctx.enter_context(nc.psum_tensor(f"fbank{i}", [P, 512], F32)) for i in range(2)]

        ident16 = sb("l1_ident16", [P, P], F16)
        cmat = sb("cmat", [P, 4, P])
        ident, upto, after, ones = (cmat[:, i, :] for i in range(4))
        corner = sb("corner", [P, len(LEVELS), P])
        blocks = sb("blocks", [P, P])
        hsel = sb("hsel", [P, 2])
        onec = sb("onec", [P, 1])
        expo = sb("expo", [P, 48])
        w1 = sb("w1", [P, 2, KT, NW1], F16)
        w1h, w1l = w1[:, 0], w1[:, 1]
        up = sb("up", [P, KT, 2048], F16)
        down = sb("down", [P, HT, D], F16)
        wo1 = sb("wo1", [P, MT, D])
        cw = sb("cw", [P, NM, CONV])
        usn = sb("usn", [P, HT])
        dsc = sb("dsc", [P, D])
        onw = sb("onw", [P, KW])
        ab = sb("ab", [P, 2 * LH])
        negA = sb("negA", [P, LH])
        osc = sb("osc", [P, 1])
        spare = sb("spare", [2, 1])
        am = sb("am", [P, 3])
        ama = sb("ama", [P, 2])
        pw = sb("pw", [P, 2])
        ipw = sb("ipw", [P, 2])
        un = sb("un", [P, 1])
        unh = sb("unh", [P, 1])
        hid = sb("hid", [P, 2, HT, T], F16)
        xT = sb("xT", [P, KT, 2, T], F16)
        st = sb("l1_st", [P, TT, 6])
        mv = sb("l1_mv", [P, TT, 2])
        rs0 = sb("rs0", [P, TT])
        rs = sb("l1_rs", [P, TT])
        pre = sb("pre", [P, 2, CONV - 1 + T])
        ca = sb("ca", [P, T])
        ct = sb("ct", [P, T])
        r32 = sb("r32", [P, T])
        sil = sb("sil", [P, NM, T])
        yT = sb("yT", [P, MT, T])
        z = sb("z", [P, TT, 2 * LH])
        ssq = sb("ssq", [P, TT, 2 * LH])
        sm = sb("sm", [P, 13, TT, LH])
        tb, beta, az, ez, lz, spl, gg, nbg, rn, rsk, sn, rvs, e5 = (sm[:, i] for i in range(13))
        vec = sb("vec", [P, TT, 3 * LH])
        gcs = sb("gcs", [P, TT, MT])
        sT = sb("sT", [TT * LH, P])
        ssol = sb("ssol", [2 * SYS, 2, BS])
        big = sb("big", [P, 14, LH, P])
        LT = [big[:, i] for i in range(4)]
        BT = [big[:, 4 + i] for i in range(4)]
        E, RT, GT, gU = (big[:, i] for i in range(8, 12))
        Tm, TTm = [big[:, 12], GT], [big[:, 13], gU]
        tok = sb("tok", [P, 7, KW])
        Rv, Kt, V2, U, o1, t1, gt = (tok[:, i, :] for i in range(7))
        S_ = sb("S_", [P, 2, MT, HD])
        ssS = sb("ssS", [P, MT, HD])
        os_ = sb("os_", [P, 3, LH])
        res = sb("res", [P, 2, D])
        fd, th, sqf, ba = ca, ct, yT[:, 0, :], yT[0:2 * LH, 1, :]
        cas, r32s = (ca, r32), (r32, ct)
        Tc = [t[:, :].rearrange("p (t h c) -> p t h c", t=TT, h=LH) for t in
              (ca[:, 0:TT * LH * BS], pre[:, 0, CONV - 1:CONV - 1 + TT * LH * BS])]
        silf = sil[:, :, :].rearrange("p a b -> p (a b)").bitcast(F16)
        xh = silf[:, 0:TT * D].rearrange("p (t n) -> p t n", t=TT)
        xl = silf[:, TT * D:2 * TT * D].rearrange("p (t n) -> p t n", t=TT)
        bigf = big[:, :, :, :].rearrange("p a b c -> p (a b c)")
        xb = bigf[:, 0:TT * D].rearrange("p (t n) -> p t n", t=TT)
        xs = bigf[:, TT * D:2 * TT * D].rearrange("p (t n) -> p t n", t=TT)
        wst = bigf[:, 2 * TT * D:2 * TT * D + KT * NW1].rearrange("p (k n) -> p k n", k=KT)
        tokf = tok[:, :, :].rearrange("p a b -> p (a b)")
        l_in, l_s, t_t, prod, t_n = (tokf[0:2 * SYS, i * 2 * BS * BS:(i + 1) * 2 * BS * BS].rearrange(
            "p (s a c) -> p s a c", s=2, a=BS) for i in range(5))
        hidf = hid[:, :, :, :].rearrange("p a b c -> p (a b c)").bitcast(F32)
        upst = hidf.rearrange("p (k n) -> p k n", k=KT)
        dnst = hidf.rearrange("p (k n) -> p k n", k=HT)

        OWN = {
            "pe": ["v_full", "a_full", "f_full", "down_full", "sq_used"],
            "act": ["a_took", "tanh_c", "tb_r", "ez_r", "lz_r", "gate_t", "osq", "th_r", "r32_r"],
            "dve": ["v_took", "st_r", "mv_r", "rs0_r", "xs_r", "xh_r", "xl_r", "conv", "sil_r", "beta_r", "az_r",
                    "spl_r", "g_r", "small_r", "gcs_r", "kS_r", "V2_r", "ssS_r", "oss_r", "or_r", "y_r", "fd_r", "g2_r",
                    "out_r", "S0_r", "ls_r", "sub", "inv_r"],
            "pool": ["rs_r", "sq_r", "rn_r", "gU_r", "GTm_r", "eye_r", "T0_r", "orn_r", "gw_r", "hid_r"],
            "sp": ["xb_in", "res_in0", "res_in1", "out0", "out1", "s_out", "s_in", "lt_out", "lt_in0", "lt_in1", "t_out", "t_in0", "t_in1"],
        }
        S = {n: sem("l1_" + n) for n in sum(OWN.values(), []) + [
            "const", "w_in0", "w_in1", "wo_in", "up_in", "dn_in", "turns", "m_h", "m_r", "m_a", "m_p", "un_r", "w1h_r", "w1l_r", "up_r", "down_r",
            "pads", "usn_r", "dsc_r", "negA_r", "onw_r"]}

        def settle(eng):
            eng.sem_inc(S["turns"], 1)

        def start(eng, who):
            for n in OWN[who]:
                eng.sem_inc(S[n], ONE + (3 if n in ("v_took", "a_took") else 0))

        def hb(col, n):
            return col.rearrange("p (h c) -> p h c", c=1).to_broadcast([P, col.shape[-1], n])

        def over(mat, n):
            return mat.rearrange("p (h c) -> p h c", h=1).to_broadcast([P, n, P])

        def heads(t):
            return t.rearrange("p (h c) -> p h c", h=LH)

        block = ctx.enter_context(nc.Block())

        @block.sync
        def _(sp):
            start(sp, "sp")
            def load_x(n):
                sp.dma_start(xb, x1_dram[n].rearrange("t p n -> p t n")).then_inc(S["xb_in"], 16)

            load_x(0)
            for i in range(2):
                sp.dma_start(wst[:, 2 * i:2 * i + 2], d["w1"][:, 2 * i:2 * i + 2]).then_inc(S[f"w_in{i}"], 16)
            for t, n in ((ident16, "ident16"), (cmat, "cmat"), (corner, "corner"), (blocks, "blocks"), (hsel, "hsel"),
                         (cw, "cw"), (usn, "up_scale")):
                sp.dma_start(t[:], d[n]).then_inc(S["const"], 16)
            for t, n in ((dsc, "down_scale"), (onw, "onw"), (ab, "ab_bias"), (negA, "a_log"), (osc, "out_scale")):
                sp.dma_start(t[:, :], d[n].partition_broadcast(P)).then_inc(S["const"], 16)
            sp.dma_start(upst, d["upw"]).then_inc(S["up_in"], 16)
            sp.dma_start(wo1[:, :, :], d["wo1"]).then_inc(S["wo_in"], 16)
            sp.wait_ge(S["up_r"], 1)
            sp.dma_start(dnst, d["downw"]).then_inc(S["dn_in"], 16)
            with sp.Fori(0, B) as b:
                def load_residual(tt):
                    sp.wait_ge(S[f"out{tt % 2}"], (b * 2 + tt // 2) * 16 + ONE)
                    settle(sp)
                    sp.dma_start(res[:, tt % 2, :], x1_dram[b, tt]).then_inc(S[f"res_in{tt % 2}"], 16)

                load_residual(0)
                load_residual(1)
                def store_matrices(tt):
                    sp.wait_ge(S["v_took"], b * NV + VI["KK", tt, 1] + 1 + 3 + ONE)
                    sp.dma_start(lt_dram[tt, :, 0:P, :].rearrange("h p i -> p h i"), LT[tt]).then_inc(S["lt_out"], 16)

                def load_blocks(pair):
                    sp.wait_ge(S["lt_out"], (b * TT + 2 * pair + 2) * 16 + ONE)
                    for par in range(2):
                        tt = 2 * pair + par
                        sp.dma_start(l_in[par * SYS:(par + 1) * SYS, pair],
                                     bass.AP(lt_dram.tensor, tt * LH * (P + 1) * P,
                                             [[BS * P + BS, SYS], [P, BS], [1, BS]])).then_inc(S[f"lt_in{pair}"], 16)

                store_matrices(0)
                store_matrices(1)
                load_blocks(0)
                sp.wait_ge(S["a_took"], b * NA + AI["sT",] + 1 + 3 + ONE)
                sp.dma_start(s_dram, sT[:, :]).then_inc(S["s_out"], 16)
                sp.wait_ge(S["s_out"], (b + 1) * 16 + ONE)
                for par in range(2):
                    sp.dma_start(ssol[par * SYS:(par + 1) * SYS],
                                 s_dram.rearrange("(s q h) (b i) -> q (h b) s i", s=2, q=2, i=BS)[par]).then_inc(S["s_in"], 16)
                store_matrices(2)
                store_matrices(3)
                load_blocks(1)
                for pair in range(2):
                    sp.wait_ge(S["inv_r"], b * 2 + pair + 1 + ONE)
                    for i, t in enumerate((t_n, t_t)):
                        sp.dma_start(t_dram[i, 2 * pair:2 * pair + 2].rearrange("q s a c -> (q s) a c"), t[:, pair]).then_inc(S["t_out"], 16)
                    sp.wait_ge(S["t_out"], (b * 2 + pair + 1) * 32 + ONE)
                    for i in range(2):
                        sp.dma_start(Tc[i][:, 2 * pair:2 * pair + 2],
                                     bass.AP(t_dram.tensor, (i * TT + 2 * pair) * SYS * BS * BS,
                                             [[BS, P], [NB * BS * BS, 2 * LH], [1, BS]])).then_inc(S[f"t_in{pair}"], 16)
                sp.wait_ge(S["v_took"], b * NV + VI["SU", TT - 1] + 1 + 3 + ONE)
                settle(sp)
                load_x(b + 1)
                for tt in range(TT):
                    sp.wait_ge(S["out_r"], b * TT + tt + 1 + ONE)
                    settle(sp)
                    sp.dma_start(out_dram[b, tt], res[:, tt % 2, :]).then_inc(S[f"out{tt % 2}"], 16)
                    if tt < 2:
                        load_residual(tt + 2)
            sp.wait_ge(S["out0"], 16 * B * TT // 2 + ONE)
            sp.wait_ge(S["out1"], 16 * B * TT // 2 + ONE)

        @block.gpsimd
        def _(pool):
            start(pool, "pool")
            pool.memset(pre[:, :, 0:CONV - 1], 0.0).then_inc(S["pads"], 1)
            pool.memset(expo[:, :], -0.5).then_inc(S["pads"], 1)
            pool.memset(onec[:, :], 1.0).then_inc(S["pads"], 1)
            def rsqrt_var(n):
                pool.wait_ge(S["rs0_r"], n + 1 + ONE)
                pool.tensor_tensor(rs[:, :], rs0[:, :], expo[:, 0:TT], ALU.pow).then_inc(S["rs_r"], 1)

            pool.wait_ge(S["pads"], 3)
            rsqrt_var(0)
            for c in range(2):
                pool.wait_ge(S["m_r"], c + 1)
                pool.partition_all_reduce(ama[:, c:c + 1], am[:, c:c + 1], P, bass.bass_isa.ReduceOp.max).then_inc(S["m_a"], 1)
            pool.wait_ge(S["const"], 16 * 12)

            def hidden(b, ht):
                n = b * HT + ht
                pool.wait_ge(S["r32_r"], n + 1 + ONE)
                settle(pool)
                pool.tensor_scalar(hid[:, 0, ht, :], r32s[ht % 2][:, :], 1.0, 1.0, ALU.mult, ALU.mult).then_inc(S["hid_r"], 1)
                pool.wait_ge(S["hid_r"], 2 * n + 1 + ONE)
                pool.tensor_tensor(hid[:, 1, ht, :], r32s[ht % 2][:, :], hid[:, 0, ht, :], ALU.subtract).then_inc(S["hid_r"], 1)

            with pool.Fori(0, B) as b:
                def spread(tt):
                    if tt:
                        pool.wait_ge(S["a_full"], b * NA + AI["DT", tt - 1, 1] + 1 + ONE)
                    pool.wait_ge(S["g_r"], b + 1 + ONE)
                    pool.tensor_tensor(gU, over(upto, LH), hb(gg[:, tt, :], P), ALU.mult).then_inc(S["gU_r"], 1)

                for m in range(2 * MT):
                    n = b * 2 * MT + m
                    pool.wait_ge(S["sil_r"], b * NM + m + 1 + ONE)
                    pool.wait_ge(S["sq_used"], n + ONE)
                    pool.tensor_tensor(sqf[:, :], sil[:, ORDER[m], :], sil[:, ORDER[m], :], ALU.mult).then_inc(S["sq_r"], 1)

                    if m == 2:
                        spread(0)

                def k_norms():
                    pool.wait_ge(S["v_took"], b * NV + VI["ss",] + 1 + 3 + ONE)
                    pool.tensor_tensor(rn, ssq[:, :, LH:], expo[:, 0:TT * LH].rearrange("p (t h) -> p t h", t=TT),
                                       ALU.pow).then_inc(S["rn_r"], 1)

                for tt in range(TT):
                    for hf in range(2):
                        pool.wait_ge(S["a_took"], b * NA + AI["DT", tt, hf] + 1 + 3 + ONE)
                        s = slice(hf, LH, 2)
                        pool.tensor_tensor(GT[:, s, :], GT[:, s, :], over(upto, HH), ALU.mult).then_inc(S["GTm_r"], 1)
                    if tt + 1 < TT:
                        spread(tt + 1)
                    if tt == TT - 3:
                        settle(pool)
                        pool.memset(t_t.rearrange("p s a c -> p (s a c)"), 0.0).then_inc(S["eye_r"], 1)
                        pool.wait_ge(S["eye_r"], b * 3 + 1 + ONE)
                        settle(pool)
                        for slot in range(2):
                            pool.memset(t_t[:, slot].rearrange("p a c -> p (a c)")[:, ::BS + 1], 1.0).then_inc(S["eye_r"], 1)
                    if tt == TT - 2:
                        for ht in range(UP_HEAD + UP_EARLY):
                            hidden(b, ht)
                k_norms()
                for ht in range(UP_HEAD + UP_EARLY, UP_HEAD + UP_MID):
                    hidden(b, ht)
                ht = UP_HEAD + UP_MID
                def onto_diagonal(tt):
                    if tt % 2 == 0:
                        pool.wait_ge(S[f"t_in{tt // 2}"], (b + 1) * 32 + ONE)
                    if tt == 1:
                        pool.wait_ge(S["v_took"], b * NV + VI["KQ", TT - 1, 1] + 1 + 3 + ONE)
                    if tt >= 2:
                        pool.wait_ge(S["v_took"], b * NV + VI["Z", tt - 2, 1] + 1 + 3 + ONE)
                    for i, dst in enumerate((Tm, TTm)):
                        for hf in range(2):
                            s = slice(hf, LH, 2)
                            pool.tensor_tensor(dst[tt % 2][:, s, :].rearrange("p h (c j) -> p h c j", c=NB),
                                               Tc[i][:, tt, s, :].rearrange("p h (c j) -> p h c j", c=1).to_broadcast([P, HH, NB, BS]),
                                               blocks[:, :].rearrange("p (h c j) -> p h c j", h=1, c=NB).to_broadcast([P, HH, NB, BS]),
                                               ALU.mult).then_inc(S["T0_r"], 1)

                onto_diagonal(0)
                for tt in range(TT + 1):
                    w = b * TT + tt
                    if tt + 1 < TT:
                        onto_diagonal(tt + 1)
                    for _ in range(UP_STEP[tt]):
                        hidden(b, ht)
                        ht += 1
                    if tt:
                        pool.wait_ge(S["v_took"], b * NV + VI["gate", tt - 1] + 1 + 3 + ONE)
                        pool.tensor_tensor(gt, gt, onw[:, :], ALU.mult).then_inc(S["gw_r"], 1)
                        pool.wait_ge(S["oss_r"], (w - 1) * 2 + 2 + ONE)
                        pool.tensor_tensor(os_[:, 2, :], os_[:, 1, :], expo[:, 0:LH], ALU.pow).then_inc(S["orn_r"], 1)
                rsqrt_var(b + 1)

        @block.vector
        def _(v):
            start(v, "dve")
            def layernorm(n):
                v.wait_ge(S["xb_in"], (n + 1) * 16 + ONE)
                for tt in range(TT):
                    v.bn_stats(st[:, tt, :], xb[:, tt, :]).then_inc(S["st_r"], 1)
                v.wait_ge(S["st_r"], (n + 1) * TT + ONE)
                settle(v)
                for tt in range(TT):
                    v.bn_aggr(mv[:, tt, :], st[:, tt, :]).then_inc(S["mv_r"], 1)
                v.wait_ge(S["mv_r"], (n + 1) * TT + ONE)
                v.tensor_scalar(rs0[:, :], mv[:, :, 1], 1e-5, XRAISE ** -2, ALU.add, ALU.mult).then_inc(S["rs0_r"], 1)
                v.wait_ge(S["rs_r"], n + 1 + ONE)
                for tt in range(TT):
                    v.tensor_scalar(xs[:, tt, :], xb[:, tt, :], mv[:, tt, 0:1], rs[:, tt:tt + 1], ALU.subtract,
                                    ALU.mult).then_inc(S["xs_r"], 1)
                for tt in range(TT):
                    v.wait_ge(S["xs_r"], n * TT + tt + 1 + ONE)
                    v.tensor_copy(xh[:, tt, :], xs[:, tt, :]).then_inc(S["xh_r"], 1)
                for tt in range(TT):
                    v.wait_ge(S["xh_r"], n * TT + tt + 1 + ONE)
                    v.tensor_tensor(xl[:, tt, :], xs[:, tt, :], xh[:, tt, :], ALU.subtract).then_inc(S["xl_r"], 1)

            layernorm(0)
            for i in range(2):
                v.wait_ge(S[f"w_in{i}"], 16)
                v.tensor_reduce(am[:, 2 * i:2 * i + 1], wst[:, 2 * i:2 * i + 2], AX.XY, ALU.max,
                                apply_absolute_value=True).then_inc(S["m_h"], 1)
            v.wait_ge(S["m_h"], 2)
            v.tensor_tensor(am[:, 0:1], am[:, 0:1], am[:, 2:3], ALU.max).then_inc(S["m_r"], 1)
            v.wait_ge(S["const"], 16 * 12)
            v.tensor_reduce(am[:, 1:2], usn[:, :], AX.X, ALU.max, apply_absolute_value=True).then_inc(S["m_r"], 1)
            v.wait_ge(S["m_a"], 2)
            v.tensor_scalar(ama[:, :], ama[:, :], 1e-30, None, ALU.max).then_inc(S["m_p"], 1)
            v.wait_ge(S["m_p"], 1)
            v.tensor_scalar(pw[:, :].bitcast(I32), ama[:, :].bitcast(I32), 0x7F800000, None, ALU.bitwise_and).then_inc(S["m_p"], 1)
            v.wait_ge(S["m_p"], 2)
            v.reciprocal(ipw[:, :], pw[:, :]).then_inc(S["m_p"], 1)
            v.wait_ge(S["m_p"], 3)
            v.tensor_scalar(ipw[:, 0:1], ipw[:, 0:1], WRAISE, None, ALU.mult).then_inc(S["m_p"], 1)
            v.tensor_scalar(un[:, :], pw[:, 0:1], 1.0 / (WRAISE * XRAISE), None, ALU.mult).then_inc(S["un_r"], 1)
            v.tensor_scalar(unh[:, :], pw[:, 0:1], 0.5 / (WRAISE * XRAISE), None, ALU.mult).then_inc(S["un_r"], 1)
            v.wait_ge(S["un_r"], 2)
            v.tensor_scalar(onw[:, :], onw[:, :], unh[:, 0:1], float(HD) ** 0.5, ALU.mult, ALU.mult).then_inc(S["onw_r"], 1)
            v.tensor_scalar(usn[:, :], usn[:, :], ipw[:, 1:2], 0.5, ALU.mult, ALU.mult).then_inc(S["usn_r"], 1)
            v.tensor_scalar(dsc[:, :], dsc[:, :], osc[:, 0:1], 2.0 / XRAISE, ALU.mult, ALU.mult).then_inc(S["dsc_r"], 1)
            v.wait_ge(S["dsc_r"], 1)
            v.tensor_scalar(dsc[:, :], dsc[:, :], pw[:, 1:2], None, ALU.mult).then_inc(S["dsc_r"], 1)
            v.wait_ge(S["negA_r"], 1)
            v.tensor_scalar(negA[:, :], negA[:, :], -1.0, None, ALU.mult).then_inc(S["negA_r"], 1)
            for kt in range(KT):
                v.wait_ge(S["w1h_r"], kt + 1)
                v.scalar_tensor_tensor(w1l[:, kt], wst[:, kt], ipw[:, 0:1], w1h[:, kt], ALU.mult, ALU.subtract).then_inc(S["w1l_r"], 1)
            v.wait_ge(S["dsc_r"], 2)
            v.wait_ge(S["negA_r"], 2)
            v.wait_ge(S["onw_r"], 1)

            with v.Fori(0, B) as b:
                def take(*key):
                    v.wait_ge(S["v_full"], b * NV + VI[key] + 1 + ONE)
                    return vbank[VI[key] % 3]

                def mats(bk):
                    return bk[:, 0:HH * P].rearrange("p (h c) -> p h c", h=HH)

                def tile_heads(col, tt):
                    return col[:, tt, :]

                def conv(m):
                    n = b * NM + m
                    v.wait_ge(S["a_took"], b * NA + AI["pre", m] + 1 + 3 + ONE)
                    v.wait_ge(S["sil_r"], n - 1 + ONE if m else n + ONE)
                    src, c, cm = pre[:, m % 2, :], cas[m % 2], ORDER[m]
                    v.tensor_scalar(c[:, :], src[:, 0:T], cw[:, cm, 0:1], None, ALU.mult).then_inc(S["conv"], 1)
                    for i in range(1, CONV):
                        v.wait_ge(S["conv"], n * CONV + i + ONE)
                        v.scalar_tensor_tensor(c[:, :], src[:, i:i + T], cw[:, cm, i:i + 1], c[:, :], ALU.mult,
                                               ALU.add).then_inc(S["conv"], 1)

                def silu(m):
                    n = b * NM + m
                    v.wait_ge(S["tanh_c"], n + 1 + ONE)
                    v.scalar_tensor_tensor(sil[:, ORDER[m], :], ct[:, :], 1.0, cas[m % 2][:, :], ALU.add, ALU.mult).then_inc(S["sil_r"], 1)

                def small(n):
                    v.wait_ge(S["small_r"], b * 5 + n + ONE)

                v.wait_ge(S["out_r"], b * TT + ONE)
                conv(0)
                bk = take("bat")
                v.tensor_tensor(z[:, :, :], bk[:, 0:TT * 2 * LH].rearrange("p (t c) -> p t c", t=TT),
                                ab[:, :].rearrange("p (t c) -> p t c", t=1).to_broadcast([P, TT, 2 * LH]),
                                ALU.add).then_inc(S["v_took"], 1)
                v.wait_ge(S["v_took"], b * NV + VI["bat",] + 1 + 3 + ONE)
                v.scalar_tensor_tensor(az, z[:, :, LH:], -1.0, z[:, :, LH:], ALU.mult, ALU.min).then_inc(S["az_r"], 1)
                conv(1)
                silu(0)
                conv(2)
                silu(1)
                v.wait_ge(S["tb_r"], b + 1 + ONE)
                v.tensor_scalar(beta, tb, 0.5, 0.5, ALU.mult, ALU.add).then_inc(S["beta_r"], 1)
                v.wait_ge(S["lz_r"], b + 1 + ONE)
                v.scalar_tensor_tensor(spl, z[:, :, LH:], 0.0, lz, ALU.max, ALU.add).then_inc(S["spl_r"], 1)
                v.wait_ge(S["spl_r"], b + 1 + ONE)
                v.tensor_tensor(gg, spl, negA[:, :].rearrange("p (t c) -> p t c", t=1).to_broadcast([P, TT, LH]),
                                ALU.mult).then_inc(S["g_r"], 1)
                for m in range(3, 7):
                    conv(m)
                    silu(m - 1)
                bk = take("ss")[:, 0:TT * 2 * LH].rearrange("p (t c) -> p t c", t=TT)
                v.tensor_scalar(ssq[:, :, LH:], bk[:, :, LH:], 4e-6, None, ALU.add)
                v.tensor_scalar(ssq[:, :, 0:LH], bk[:, :, 0:LH], 4e-6, float(HD), ALU.add, ALU.mult).then_inc(S["v_took"], 1)
                v.wait_ge(S["v_took"], b * NV + VI["ss",] + 1 + 3 + ONE)
                v.reciprocal(rsk, ssq[:, :, LH:]).then_inc(S["small_r"], 1)
                v.tensor_scalar(e5, ssq[:, :, 0:LH], 1e-5 * HD, None, ALU.mult).then_inc(S["small_r"], 1)
                v.wait_ge(S["beta_r"], b + 1 + ONE)
                small(2)
                v.scalar_tensor_tensor(sn, beta, -1.0, rsk, ALU.mult, ALU.mult).then_inc(S["small_r"], 1)

                def matrices(tt):
                    for nm, dst in (("KK", LT[tt]), ("KQ", BT[tt])):
                        for hf in range(2):
                            v.wait_ge(S["GTm_r"], (b * TT + tt) * 2 + hf + 1 + ONE)
                            v.tensor_tensor(dst[:, hf:LH:2, :], mats(take(nm, tt, hf)), GT[:, hf:LH:2, :],
                                            ALU.mult).then_inc(S["v_took"], 1)

                def invert_blocks(pair):
                    v.wait_ge(S["s_in"], (b + 1) * 32 + ONE)
                    v.wait_ge(S["eye_r"], (b + 1) * 3 + ONE)
                    v.wait_ge(S[f"lt_in{pair}"], (b + 1) * 32 + ONE)
                    v.tensor_tensor(l_s[:, pair], l_in[:, pair],
                                    ssol[:, pair, :].rearrange("p (j i) -> p j i", j=1).to_broadcast([2 * SYS, BS, BS]),
                                    ALU.mult).then_inc(S["ls_r"], 1)
                    v.wait_ge(S["ls_r"], b * 2 + pair + 1 + ONE)
                    for i in range(1, BS):
                        n = ((b * 2 + pair) * (BS - 1) + i - 1) * 2
                        v.wait_ge(S["sub"], n + ONE)
                        v.tensor_tensor(prod[:, pair, 0:i, 0:i], t_t[:, pair, 0:i, 0:i],
                                        l_s[:, pair, 0:i, i:i + 1].rearrange("p j c -> p c j").to_broadcast([2 * SYS, i, i]),
                                        ALU.mult).then_inc(S["sub"], 1)
                        v.wait_ge(S["sub"], n + 1 + ONE)
                        v.tensor_reduce(t_t[:, pair, 0:i, i], prod[:, pair, 0:i, 0:i], AX.X, ALU.add).then_inc(S["sub"], 1)
                    v.wait_ge(S["sub"], (b * 2 + pair + 1) * (BS - 1) * 2 + ONE)
                    v.tensor_copy(t_n[:, pair], t_t[:, pair].rearrange("p c a -> p a c")).then_inc(S["inv_r"], 1)

                matrices(0)
                conv(7)
                silu(6)
                matrices(1)
                conv(8)
                silu(7)
                matrices(2)
                silu(8)
                invert_blocks(0)
                matrices(3)
                v.wait_ge(S["a_took"], b * NA + AI["vec",] + 1 + 3 + ONE)
                small(3)
                v.tensor_tensor(nbg, sn, vec[:, :, 0:LH], ALU.mult).then_inc(S["small_r"], 1)
                for p in range(2):
                    v.tensor_copy(gcs[64 * p:64 * p + 64, :, :], vec[64 * p:64 * p + 64, :, 2 * LH + p:3 * LH:2]).then_inc(S["gcs_r"], 1)
                v.memset(S_[:, 0, :, :], 0.0).then_inc(S["S0_r"], 1)
                invert_blocks(1)
                v.wait_ge(S["rn_r"], b + 1 + ONE)
                v.scalar_tensor_tensor(rvs, beta, 0.5, rn, ALU.mult, ALU.mult).then_inc(S["small_r"], 1)
                small(5)

                for tt in range(TT + 1):
                    inv, rec = tt < TT, tt > 0
                    T_, TT_ = Tm[tt % 2], TTm[tt % 2]
                    rt = tt - 1
                    w = b * TT + rt

                    def corner_of(lv):
                        for hf in range(2):
                            bk = take("X", tt, lv, hf)
                            for j in range(HH):
                                hh = hf + 2 * j
                                i = v.scalar_tensor_tensor(E[:, hh, :], bk[:, j * P:(j + 1) * P], sn[:, tt, hh:hh + 1],
                                                           corner[:, lv - LEVELS[0], :], ALU.mult, ALU.mult)
                            i.then_inc(S["v_took"], 1)

                    def add_to(dst, src, *key):
                        for hf in range(2):
                            v.tensor_tensor(dst[:, hf:LH:2, :], mats(take(*key, hf)), src[:, hf:LH:2, :],
                                            ALU.add).then_inc(S["v_took"], 1)

                    if inv:
                        corner_of(4)
                    if tt == 1:
                        v.wait_ge(S["t_out"], (b + 1) * 64 + ONE)
                    if rec:
                        v.tensor_tensor(heads(Kt), heads(take("k", rt)[:, 0:KW]), hb(vec[:, rt, LH:2 * LH], HD), ALU.mult).then_inc(S["v_took"], 1)
                        v.tensor_tensor(heads(Rv), heads(take("v", rt)[:, 0:KW]), hb(rvs[:, rt, :], HD), ALU.mult).then_inc(S["v_took"], 1)

                        def every(t, hf):
                            return heads(t)[:, hf:LH:2, :]

                        for hf in range(2):
                            bk = take("S", rt, hf)[:, 0:KW].rearrange("p (i h c) -> p i h c", i=2, h=HH)
                            v.tensor_tensor(every(t1, hf), bk[:, 0], hb(nbg[:, rt, hf:LH:2], HD), ALU.mult).then_inc(S["kS_r"], 1)
                            v.tensor_tensor(every(o1, hf), bk[:, 1], hb(vec[:, rt, hf:LH:2], HD), ALU.mult).then_inc(S["v_took"], 1)
                        v.wait_ge(S["kS_r"], (w + 1) * 2 + ONE)
                        v.tensor_tensor(V2, t1, Rv, ALU.add).then_inc(S["V2_r"], 1)
                    if inv:
                        add_to(T_, T_, "Y", tt, 4)
                    if rec:
                        cur, nxt = rt % 2, (rt + 1) % 2
                        v.wait_ge(S["gcs_r"], (b + 1) * 2 + ONE)
                        v.tensor_tensor(ssS[:, :, :], S_[:, cur, :, :], gcs[:, rt, :].rearrange("p (h c) -> p h c", c=1).to_broadcast([P, MT, HD]),
                                        ALU.mult).then_inc(S["ssS_r"], 1)
                        v.wait_ge(S["gate_t"], w + 1 + ONE)
                        v.scalar_tensor_tensor(gt, gt, 1.0, take("gate", rt)[:, 0:KW], ALU.add, ALU.mult).then_inc(S["v_took"], 1)
                    if inv:
                        corner_of(5)
                        add_to(T_, T_, "Y", tt, 5)
                    if rec:
                        v.tensor_tensor(o1, take("O", rt)[:, 0:KW], o1, ALU.add).then_inc(S["v_took"], 1)
                    if inv:
                        corner_of(6)
                    if rec:
                        v.wait_ge(S["ssS_r"], w + 1 + ONE)
                        v.tensor_tensor(S_[:, nxt, :, :], take("SU", rt)[:, 0:MT * HD].rearrange("p (h c) -> p h c", h=MT), ssS[:, :, :],
                                        ALU.add).then_inc(S["v_took"], 1)
                        v.wait_ge(S["osq"], w + 1 + ONE)
                        v.tensor_reduce(os_[:, 0, :], heads(t1), AX.X, ALU.add).then_inc(S["oss_r"], 1)
                        v.wait_ge(S["oss_r"], w * 2 + 1 + ONE)
                        v.tensor_tensor(os_[:, 1, :], os_[:, 0, :], e5[:, rt, :], ALU.add).then_inc(S["oss_r"], 1)
                    if inv:
                        add_to(RT, TT_, "Z", tt)
                    if rec:
                        v.wait_ge(S["orn_r"], w + 1 + ONE)
                        v.tensor_tensor(heads(o1), heads(o1), hb(os_[:, 2, :], HD), ALU.mult).then_inc(S["or_r"], 1)
                        v.wait_ge(S["or_r"], w + 1 + ONE)
                        v.wait_ge(S["gw_r"], w + 1 + ONE)
                        v.tensor_tensor(o1, o1, gt, ALU.mult).then_inc(S["y_r"], 1)
                layernorm(b + 1)

                for tt in range(TT):
                    w = b * TT + tt
                    v.wait_ge(S["down_full"], w + 1 + ONE)
                    v.wait_ge(S["out_r"], w + ONE)
                    v.tensor_tensor(fd[:, :], fbank[tt % 2][:, :], dsc[:, :], ALU.mult).then_inc(S["fd_r"], 1)
                    v.wait_ge(S["th_r"], w + 1 + ONE)
                    v.scalar_tensor_tensor(th[:, :], th[:, :], 1.0, fd[:, :], ALU.add, ALU.mult).then_inc(S["g2_r"], 1)
                    v.wait_ge(S["g2_r"], w + 1 + ONE)
                    v.scalar_tensor_tensor(fd[:, :], take("wo", tt)[:, :], 0.5, th[:, :], ALU.mult, ALU.mult).then_inc(S["v_took"], 1)
                    v.wait_ge(S["v_took"], b * NV + VI["wo", tt] + 1 + 3 + ONE)
                    v.wait_ge(S[f"res_in{tt % 2}"], (b * 2 + tt // 2 + 1) * 16 + ONE)
                    v.tensor_tensor(res[:, tt % 2, :], fd[:, :], res[:, tt % 2, :], ALU.add).then_inc(S["out_r"], 1)
                for i in range(NV - VI["wo", TT - 1] - 1):
                    v.tensor_copy(spare[:, :], take("spare", i)[0:2, 0:1]).then_inc(S["v_took"], 1)

        @block.scalar
        def _(a):
            start(a, "act")
            def turn_x(n, kts):
                for kt in kts:
                    a.wait_ge(S["a_full"], n * NA + kt + 1 + ONE)
                    a.activation(xT[:, kt, :, :].rearrange("p a b -> p (a b)"), abank[kt % 3][:, :].bitcast(F16), ACT.Copy).then_inc(S["a_took"], 1)

            turn_x(0, range(KT))
            a.wait_ge(S["const"], 16 * 12)
            a.activation(negA[:, :], negA[:, :], ACT.Exp).then_inc(S["negA_r"], 1)
            a.wait_ge(S["m_p"], 4)
            for kt in range(KT):
                a.activation(w1h[:, kt], wst[:, kt], ACT.Copy, scale=ipw[:, 0:1]).then_inc(S["w1h_r"], 1)
            a.wait_ge(S["up_in"], 16)
            a.activation(up[:, :, :], upst, ACT.Sign).then_inc(S["up_r"], 1)
            a.wait_ge(S["dn_in"], 16)
            a.activation(down[:, :, :], dnst, ACT.Sign).then_inc(S["down_r"], 1)
            a.wait_ge(S["pads"], 3)
            a.wait_ge(S["un_r"], 2)
            a.wait_ge(S["usn_r"], 1)

            with a.Fori(0, B) as b:
                def take(*key):
                    a.wait_ge(S["a_full"], b * NA + AI[key] + 1 + ONE)
                    return abank[AI[key] % 3]

                def hidden(ht):
                    n = b * HT + ht
                    a.wait_ge(S["f_full"], n + 1 + ONE)
                    a.wait_ge(S["hid_r"], (n - 1) * 2 + ONE if ht >= 2 else b * HT * 2 + ONE)
                    if ht < 2:
                        a.wait_ge(S["sil_r"], (b + 1) * NM + ONE)
                    a.activation(r32s[ht % 2][:, :], fbank[ht % 2][:, :], ACT.Relu, scale=usn[:, ht:ht + 1]).then_inc(S["r32_r"], 1)

                a.activation(ba, take("ba")[0:2 * LH, :], ACT.Copy, scale=un[0:2 * LH, :]).then_inc(S["a_took"], 1)

                def evict_pre(m):
                    n = b * NM + m
                    a.wait_ge(S["conv"], (n - 1) * CONV + ONE if m >= 2 else b * NM * CONV + ONE)
                    a.activation(pre[:, m % 2, CONV - 1:], take("pre", m)[:, :], ACT.Copy, scale=un[:, :]).then_inc(S["a_took"], 1)

                def tanh_conv(m):
                    n = b * NM + m
                    a.wait_ge(S["conv"], (n + 1) * CONV + ONE)
                    a.wait_ge(S["sil_r"], n + ONE)
                    a.activation(ct[:, :], cas[m % 2][:, :], ACT.Tanh, scale=0.5).then_inc(S["tanh_c"], 1)

                evict_pre(0)
                evict_pre(1)
                def three_mats(dst, fn, *key):
                    a.activation(dst[:, key[-1]:LH:2, :], take(*key)[:, 0:HH * P].rearrange("p (h c) -> p h c", h=HH), fn).then_inc(S["a_took"], 1)

                def decays(tt):
                    for hf in range(2):
                        if tt:
                            a.wait_ge(S["v_took"], b * NV + VI["KQ", tt - 1, hf] + 1 + 3 + ONE)
                        three_mats(GT, ACT.Exp, "DT", tt, hf)

                for m in range(5):
                    tanh_conv(m)
                    evict_pre(m + 2)
                    if m == 1:
                        a.wait_ge(S["v_took"], b * NV + VI["bat",] + 1 + 3 + ONE)
                        a.activation(tb, z[:, :, 0:LH], ACT.Tanh, scale=0.5).then_inc(S["tb_r"], 1)
                        a.wait_ge(S["az_r"], b + 1 + ONE)
                        a.activation(ez, az, ACT.Exp).then_inc(S["ez_r"], 1)
                        a.wait_ge(S["ez_r"], b + 1 + ONE)
                        a.activation(lz, ez, ACT.Ln, bias=onec[:, :]).then_inc(S["lz_r"], 1)
                tanh_conv(5)
                a.activation(vec[:, :, :].rearrange("p a b -> p (a b)"), take("vec")[:, 0:TT * 3 * LH], ACT.Exp).then_inc(S["a_took"], 1)
                decays(0)
                tanh_conv(6)
                evict_pre(7)
                decays(1)
                tanh_conv(7)
                evict_pre(8)
                a.activation(sT[:, :], take("sT")[0:TT * LH, 0:P], ACT.Copy).then_inc(S["a_took"], 1)
                decays(2)
                tanh_conv(8)
                for ht in range(UP_HEAD + UP_EARLY):
                    hidden(ht)
                decays(3)
                for ht in range(UP_HEAD + UP_EARLY, UP_HEAD + UP_MID):
                    hidden(ht)
                ht = UP_HEAD + UP_MID

                def evict_y(rt):
                    a.activation(yT[:, :, rt * P:(rt + 1) * P], take("yT", rt)[:, 0:KW].rearrange("p (m c) -> p m c", m=MT), ACT.Copy).then_inc(S["a_took"], 1)

                for tt in range(TT + 1):
                    inv, rec = tt < TT, tt > 0
                    rt = tt - 1
                    w = b * TT + rt
                    ups = UP_STEP[tt]
                    if tt > 1:
                        evict_y(tt - 2)
                    if rec:
                        if rt == 0:
                            a.wait_ge(S["t_out"], (b + 1) * 64 + ONE)
                        a.wait_ge(S["y_r"], w + ONE)
                        a.wait_ge(S["v_full"], b * NV + VI["gate", rt] + 1 + ONE)
                        a.activation(gt, vbank[VI["gate", rt] % 3][:, 0:KW], ACT.Tanh, scale=unh[:, :]).then_inc(S["gate_t"], 1)
                    if ups:
                        hidden(ht)
                        ht += 1
                    if inv:
                        three_mats(TTm[tt % 2], ACT.Copy, "TT", tt, 4, 0)
                        three_mats(TTm[tt % 2], ACT.Copy, "TT", tt, 4, 1)
                    if rec:
                        a.activation(U, take("U", rt)[:, 0:KW], ACT.Copy).then_inc(S["a_took"], 1)
                    if ups > 1:
                        hidden(ht)
                        ht += 1
                    if inv:
                        three_mats(TTm[tt % 2], ACT.Copy, "TT", tt, 5, 0)
                        three_mats(TTm[tt % 2], ACT.Copy, "TT", tt, 5, 1)
                    if rec:
                        a.wait_ge(S["v_took"], b * NV + VI["O", rt] + 1 + 3 + ONE)
                        a.activation(t1, o1, ACT.Square).then_inc(S["osq"], 1)
                evict_y(TT - 1)
                for tt in range(TT):
                    w = b * TT + tt
                    a.wait_ge(S["fd_r"], w + 1 + ONE)
                    a.wait_ge(S["v_took"], b * NV + VI["wo", tt - 1] + 1 + 3 + ONE if tt else b * NV + 3 + ONE)
                    a.activation(th[:, :], fd[:, :], ACT.Tanh, scale=0.5).then_inc(S["th_r"], 1)
                    turn_x(b + 1, TURNS[tt])

        @block.tensor
        def _(pe):
            start(pe, "pe")
            pe.wait_ge(S["const"], 16 * 12)

            def turn_x(n, kts):
                for kt in kts:
                    pe.wait_ge(S["a_took"], n * NA + kt + 1 + ONE)
                    pe.wait_ge(S["xl_r"], (n + 1) * TT + ONE)
                    bk = abank[kt % 3][:, :].bitcast(F16)
                    for i, t in enumerate((xh, xl)):
                        for tt in range(TT):
                            mm = pe.transpose(bk[:, i * T + tt * P:i * T + (tt + 1) * P], t[:, tt, kt * P:(kt + 1) * P], ident16[:, :])
                    mm.then_inc(S["a_full"], 1)

            turn_x(0, range(KT))
            pe.wait_ge(S["wo_in"], 16)
            pe.wait_ge(S["w1l_r"], KT)
            with pe.Fori(0, B) as b:
                def vfill(*key):
                    pe.wait_ge(S["v_took"], b * NV + VI[key] + 1 + ONE)
                    return vbank[VI[key] % 3]

                def afill(*key):
                    pe.wait_ge(S["a_took"], b * NA + AI[key] + 1 + ONE)
                    return abank[AI[key] % 3]

                def three(bk, lhs, rhs):
                    n = 0
                    for kt in range(KT):
                        for i, j in ((0, 0), (0, 1), (1, 0)):
                            mm = pe.matmul(bk, lhs(i, kt), rhs(j, kt), start=n == 0, stop=n == 3 * KT - 1)
                            n += 1
                    return mm

                def x_half(i, kt):
                    return xT[:, kt, i, :]

                def up_tile(ht):
                    n = b * HT + ht
                    if ht >= 2:
                        pe.wait_ge(S["r32_r"], n - 1 + ONE)
                    else:
                        pe.wait_ge(S["fd_r"], b * TT + ONE)
                    for kt in range(KT):
                        for i in range(2):
                            mm = pe.matmul(fbank[ht % 2][:, :], up[:, kt, ht * P:(ht + 1) * P], x_half(i, kt),
                                           start=kt == 0 and i == 0, stop=kt == KT - 1 and i == 1)
                    mm.then_inc(S["f_full"], 1)

                bk = afill("ba")
                pe.wait_ge(S["a_took"], b * NA + KT + 3 + ONE)
                three(bk[0:2 * LH, :], lambda i, kt: w1[:, i, kt, 4 * KW:NW1], x_half).then_inc(S["a_full"], 1)

                def pre_tile(m):
                    bk = afill("pre", m)
                    three(bk[:, :], lambda i, kt: w1[:, i, kt, ORDER[m] * P:(ORDER[m] + 1) * P], x_half).then_inc(S["a_full"], 1)

                pre_tile(0)
                bk = vfill("bat")
                pe.wait_ge(S["a_took"], b * NA + AI["ba",] + 1 + 3 + ONE)
                for tt in range(TT):
                    mm = pe.matmul(bk[:, tt * 2 * LH:(tt + 1) * 2 * LH], ba[:, tt * P:(tt + 1) * P], ident[0:2 * LH, 0:2 * LH],
                                   start=True, stop=True)
                mm.then_inc(S["v_full"], 1)

                def squares(m):
                    pe.wait_ge(S["sq_r"], b * 2 * MT + m + 1 + ONE)
                    bk = vbank[VI["ss",] % 3]
                    for tt in range(TT):
                        c = tt * 2 * LH + 2 * ORDER[m]
                        mm = pe.matmul(bk[:, c:c + 2], sqf[:, tt * P:(tt + 1) * P], hsel[:, :], start=True, stop=True)
                    mm.then_inc(S["sq_used"], 1)
                    return mm

                for m in range(1, 6):
                    pre_tile(m)
                    if m >= 3:
                        if m == 3:
                            vfill("ss")
                        squares(m - 3)
                squares(3)
                pre_tile(6)
                pe.wait_ge(S["up_r"], 1)
                up_tile(0)
                squares(4)
                bk = afill("vec")
                pe.wait_ge(S["g_r"], b + 1 + ONE)
                for tt in range(TT):
                    for i, mat in enumerate((upto, after, ones)):
                        c = tt * 3 * LH + i * LH
                        mm = pe.matmul(bk[:, c:c + LH], mat, gg[:, tt, :], start=True, stop=True)
                mm.then_inc(S["a_full"], 1)

                def head(base, hh, tt):
                    return sil[64 * (hh % 2):64 * (hh % 2) + 64, base + hh // 2, tt * P:(tt + 1) * P]

                def mats(fill, key, lhs, rhs):
                    bk = fill(*key)
                    for j in range(HH):
                        hh = key[-1] + 2 * j
                        if rhs is None:
                            mm = pe.transpose(bk[:, j * P:(j + 1) * P], lhs(hh), ident)
                        else:
                            mm = pe.matmul(bk[:, j * P:(j + 1) * P], lhs(hh), rhs(hh), start=True, stop=True)
                    mm.then_inc(S["v_full" if fill is vfill else "a_full"], 1)

                for tt in range(TT):
                    w = b * TT + tt
                    for hf in range(2):
                        bk = afill("DT", tt, hf)
                        pe.wait_ge(S["gU_r"], w + 1 + ONE)
                        pe.matmul(bk[:, 0:HH * P], after, gU[:, hf:LH:2, :], start=True, stop=True).then_inc(S["a_full"], 1)
                    if tt == 0:
                        up_tile(1)
                        squares(5)
                        pe.wait_ge(S["sq_used"], (b + 1) * 2 * MT + ONE)
                        pe.sem_inc(S["v_full"], 1)
                    for nm, base in (("KK", MT), ("KQ", 0)):
                        for hf in range(2):
                            mats(vfill, (nm, tt, hf), lambda hh: head(MT, hh, tt), lambda hh: head(base, hh, tt))
                    if tt < 2:
                        pre_tile(NM - 2 + tt)
                    if tt == 1:
                        bk = afill("sT")
                        pe.wait_ge(S["small_r"], b * 5 + 3 + ONE)
                        pe.transpose(bk[0:TT * LH, 0:P], sn.rearrange("p t h -> p (t h)"), ident).then_inc(S["a_full"], 1)
                    if tt == 2:
                        pe.wait_ge(S["down_r"], 1)
                        for ht in range(UP_HEAD, UP_HEAD + UP_EARLY):
                            up_tile(ht)
                for ht in range(UP_HEAD + UP_EARLY, UP_HEAD + UP_MID):
                    up_tile(ht)
                ht = UP_HEAD + UP_MID

                def turn_y(rt):
                    bk = afill("yT", rt)
                    pe.wait_ge(S["y_r"], b * TT + rt + 1 + ONE)
                    for m in range(MT):
                        mm = pe.transpose(bk[:, m * P:(m + 1) * P], o1[:, m * P:(m + 1) * P], ident)
                    mm.then_inc(S["a_full"], 1)

                for tt in range(TT + 1):
                    inv, rec = tt < TT, tt > 0
                    T_, TT_ = Tm[tt % 2], TTm[tt % 2]
                    rt = tt - 1
                    w = b * TT + rt
                    ups = UP_STEP[tt]

                    def product_X(lv):
                        for hf in range(2):
                            if lv == LEVELS[0]:
                                pe.wait_ge(S["T0_r"], (b * TT + tt) * 4 + hf + 1 + ONE)
                            else:
                                pe.wait_ge(S["v_took"], b * NV + VI["Y", tt, lv - 1, hf] + 1 + 3 + ONE)
                            mats(vfill, ("X", tt, lv, hf), lambda hh: LT[tt][:, hh, :], lambda hh: T_[:, hh, :])

                    def product_Y(lv):
                        for hf in range(2):
                            if lv == LEVELS[0]:
                                pe.wait_ge(S["T0_r"], (b * TT + tt) * 4 + 2 + hf + 1 + ONE)
                            else:
                                pe.wait_ge(S["a_took"], b * NA + AI["TT", tt, lv - 1, hf] + 1 + 3 + ONE)
                            pe.wait_ge(S["v_took"], b * NV + VI["X", tt, lv, hf] + 1 + 3 + ONE)
                            mats(vfill, ("Y", tt, lv, hf), lambda hh: TT_[:, hh, :], lambda hh: E[:, hh, :])

                    def turn_T(lv):
                        for hf in range(2):
                            pe.wait_ge(S["v_took"], b * NV + VI["Y", tt, lv, hf] + 1 + 3 + ONE)
                            mats(afill, ("TT", tt, lv, hf), lambda hh: T_[:, hh, :], None)

                    if inv:
                        product_X(4)
                    if rec:
                        for nm, base in (("k", MT), ("v", 2 * MT)):
                            bk = vfill(nm, rt)
                            for m in range(MT):
                                mm = pe.transpose(bk[:, m * P:(m + 1) * P], sil[:, base + m, rt * P:(rt + 1) * P], ident)
                            mm.then_inc(S["v_full"], 1)
                        if rt:
                            turn_y(rt - 1)
                        if rt:
                            pe.wait_ge(S["v_took"], b * NV + VI["SU", rt - 1] + 1 + 3 + ONE)
                        else:
                            pe.wait_ge(S["S0_r"], b + 1 + ONE)
                        for hf in range(2):
                            bk = vfill("S", rt, hf)
                            for i, base in enumerate((MT, 0)):
                                for j in range(HH):
                                    mm = pe.matmul(bk[:, (i * HH + j) * HD:(i * HH + j + 1) * HD], head(base, hf + 2 * j, rt),
                                                   S_[64 * hf:64 * hf + 64, rt % 2, j, :], start=True, stop=True)
                            mm.then_inc(S["v_full"], 1)
                    if inv:
                        product_Y(4)
                    if rec:
                        rk = slice(rt * P, (rt + 1) * P)
                        bk = vfill("gate", rt)
                        three(bk[:, 0:KW], lambda i, kt: xT[:, kt, i, rk], lambda j, kt: w1[:, j, kt, 3 * KW:4 * KW]).then_inc(S["v_full"], 1)
                    if ups:
                        up_tile(ht)
                        ht += 1
                    if inv:
                        turn_T(4)
                    if inv:
                        product_X(5)
                    if rec:
                        bk = afill("U", rt)
                        pe.wait_ge(S["V2_r"], w + 1 + ONE)
                        for hh in range(LH):
                            mm = pe.matmul(bk[:, hh * HD:(hh + 1) * HD], RT[:, hh, :], V2[:, hh * HD:(hh + 1) * HD], start=True, stop=True)
                        mm.then_inc(S["a_full"], 1)
                    if ups > 1:
                        up_tile(ht)
                        ht += 1
                    if inv:
                        product_Y(5)
                    if rec:
                        bk = vfill("O", rt)
                        pe.wait_ge(S["a_took"], b * NA + AI["U", rt] + 1 + 3 + ONE)
                        for hh in range(LH):
                            mm = pe.matmul(bk[:, hh * HD:(hh + 1) * HD], BT[rt][:, hh, :], U[:, hh * HD:(hh + 1) * HD], start=True, stop=True)
                        mm.then_inc(S["v_full"], 1)
                    if inv:
                        turn_T(5)
                        product_X(6)
                    if rec:
                        bk = vfill("SU", rt)
                        for hh in range(LH):
                            q = 64 * (hh % 2)
                            mm = pe.matmul(bk[q:q + 64, (hh // 2) * HD:(hh // 2 + 1) * HD], Kt[:, hh * HD:(hh + 1) * HD],
                                           U[:, hh * HD:(hh + 1) * HD], start=True, stop=True)
                        mm.then_inc(S["v_full"], 1)
                    if inv:
                        for hf in range(2):
                            pe.wait_ge(S["a_took"], b * NA + AI["TT", tt, 5, hf] + 1 + 3 + ONE)
                            pe.wait_ge(S["v_took"], b * NV + VI["X", tt, 6, hf] + 1 + 3 + ONE)
                            mats(vfill, ("Z", tt, hf), lambda hh: E[:, hh, :], lambda hh: TT_[:, hh, :])
                for tt in range(TT):
                    w = b * TT + tt
                    if tt < 2:
                        pe.wait_ge(S["r32_r"], (b + 1) * HT + ONE)
                    else:
                        pe.wait_ge(S["fd_r"], w - 1 + ONE)
                    pe.wait_ge(S["hid_r"], (b + 1) * HT * 2 + ONE)
                    for ht in range(HT):
                        for i in range(2):
                            mm = pe.matmul(fbank[tt % 2][:, :], hid[:, i, ht, tt * P:(tt + 1) * P], down[:, ht, :],
                                           start=ht == 0 and i == 0, stop=ht == HT - 1 and i == 1)
                    mm.then_inc(S["down_full"], 1)
                    if tt == 0:
                        turn_y(TT - 1)
                    bk = vfill("wo", tt)
                    pe.wait_ge(S["a_took"], b * NA + AI["yT", TT - 1] + 1 + 3 + ONE)
                    for m in range(MT):
                        mm = pe.matmul(bk[:, :], yT[:, m, tt * P:(tt + 1) * P], wo1[:, m, :], start=m == 0, stop=m == MT - 1)
                    mm.then_inc(S["v_full"], 1)
                    turn_x(b + 1, TURNS[tt])
                for i in range(NV - VI["wo", TT - 1] - 1):
                    pe.transpose(vfill("spare", i)[0:2, 0:P], hsel[:, :], ident).then_inc(S["v_full"], 1)


def host_layout(i):
    import numpy as np
    c = np.ascontiguousarray

    def rows(a):
        return a.reshape(-1, P, a.shape[-1]).transpose(1, 0, 2)

    def cols(a):
        return c(a.reshape(-1, P).T)

    a = {n: np.asarray(v) for n, v in i.items()}
    o = {}
    o["x"] = c(a["L0_attn_x"])
    wq = a["L0_attn_Wq"].reshape(D, NKV, G, DH)
    wk = a["L0_attn_Wk"].reshape(D, NKV, 1, DH)
    q = np.zeros((D, NKV, G, 32), wq.dtype)
    q[..., 0:DH] = wq
    k = np.zeros((D, NKV, G, 32), wk.dtype)
    k[..., 0:DH] = wk
    o["wq"] = c(rows(q.reshape(D, NKV * P)).reshape(P, KT, NKV, P))
    o["wk"] = c(rows(k.reshape(D, NKV * P)).reshape(P, KT, NKV, P))
    o["wv"] = c(rows(a["L0_attn_Wv"]))
    o["wo"] = c(rows(a["L0_attn_Wo"]))
    ug = np.concatenate([a["L0_ffn_W_up"], a["L0_ffn_W_gate"]], 0).T
    o["ug"] = c(rows(ug).reshape(P, KT, NCH, 512).transpose(2, 0, 1, 3))
    o["down"] = c(rows(a["L0_ffn_W_down"].T))
    o["su_ug"] = cols(a["L0_ffn_SU_ug"])
    o["su_dp"] = cols(a["L0_ffn_SU_dp"])
    o["wscale_ug"] = cols(a["L0_ffn_Wscale_ug"])
    o["wscale_dp"] = c(a["L0_ffn_Wscale_dp"])
    w1 = np.concatenate([a[n] for n in ("L1_attn_Wq", "L1_attn_Wk", "L1_attn_Wv", "L1_attn_Wg", "L1_attn_Wb", "L1_attn_Wa")], 0)
    o["w1"] = c(rows(w1.T))
    o["wo1"] = c(rows(a["L1_attn_Wo"].T))
    conv = np.concatenate([a[n] for n in ("L1_attn_conv_q", "L1_attn_conv_k", "L1_attn_conv_v")], 0)
    o["cw"] = c(rows(conv))
    o["upw"] = c(rows(a["L1_ffn_up_weight"].T))
    o["downw"] = c(rows(a["L1_ffn_down_weight"].T))
    o["up_scale"] = cols(a["L1_ffn_up_scale"])
    o["down_scale"] = c(a["L1_ffn_down_scale"])
    o["out_scale"] = c(a["L1_ffn_output_scale"])
    o["onw"] = c(np.tile(a["L1_attn_o_norm_w"], LH))
    o["ab_bias"] = c(np.concatenate([np.zeros(LH, np.float32), a["L1_attn_dt_bias"]]))
    o["a_log"] = c(a["L1_attn_A_log"])
    i, j = np.arange(P)[:, None], np.arange(P)[None, :]
    o["cmat"] = c(np.stack([i == j, i <= j, i > j, i >= 0 * j], 1).astype(np.float32))
    o["corner"] = c(np.stack([(i >> (lv + 1) == j >> (lv + 1)) & (i >> lv & 1 == 1) & (j >> lv & 1 == 0)
                              for lv in LEVELS], 1).astype(np.float32))
    o["blocks"] = c((i // BS == j // BS).astype(np.float32))
    o["hsel"] = c((np.arange(P)[:, None] // HD == np.arange(2)[None, :]).astype(np.float32))
    o["ident16"] = np.eye(P, dtype=np.float16)
    had = np.array([[1.0]], np.float32)
    while had.shape[0] < P:
        had = np.block([[had, had], [had, -had]])
    o["had"] = c(had.astype(np.float32))
    one = np.zeros((P, 1), np.float32)
    one[DH::32] = 1.0
    o["onecol"] = one
    return o


def kernel(**inputs):
    import numpy as np
    import concourse.bacc as bacc
    from concourse.bass_utils import run_bass_kernel_spmd

    nc = bacc.Bacc("TRN2", target_bir_lowering=False, num_devices=1)
    arrays = host_layout(inputs)
    d = {n: nc.dram_tensor(f"in_{n}", a.shape, mybir.dt.from_np(a.dtype), kind="ExternalInput").ap()
         for n, a in arrays.items()}
    out = nc.dram_tensor("out_x", (B, TT, P, D), F32, kind="ExternalOutput").ap()
    x1 = nc.dram_tensor("x1_scratch", (B + 1, TT, P, D), F32, kind="Internal").ap()
    lt = nc.dram_tensor("lt_scratch", (TT, LH, P + 1, P), F32, kind="Internal").ap()
    sc = nc.dram_tensor("s_scratch", (TT * LH, P), F32, kind="Internal").ap()
    ti = nc.dram_tensor("t_scratch", (2, TT, SYS, BS, BS), F32, kind="Internal").ap()
    layer0(nc, d, x1)
    layer1(nc, d, x1, lt, sc, ti, out)
    r = run_bass_kernel_spmd(nc, [{f"in_{n}": a for n, a in arrays.items()}], core_ids=[0])
    return np.asarray(r.results[0]["out_x"]).reshape(B, T, D)
```
